# Optimizing a Trainium2 kernel written in Bass

```python
import numpy as np
import jax
import jax.numpy as jnp

def _softmax(x, axis=-1):
    return jax.nn.softmax(x, axis=axis)

def _gelu(x):
    return jax.nn.gelu(x, approximate=True)

def _silu(x):
    return jax.nn.silu(x)

def _sigmoid(x):
    return jax.nn.sigmoid(x)

def _layernorm(x, axis=-1, eps=1e-05):
    m = jnp.mean(x, axis=axis, keepdims=True)
    v = jnp.var(x, axis=axis, keepdims=True)
    return (x - m) / jnp.sqrt(v + eps)

def _scatter_add(tgt, idx, src, axis=0):
    return tgt.at[idx].add(src)

def _segment_sum(src, seg, n):
    return jax.ops.segment_sum(src, seg, n)
kernel_name = 'mk_perceiver_d2_seqx_r4_bee59b'

def setup_inputs(seed: int=0):
    np.random.seed(seed)
    _w = jnp.asarray

    def _rec_inputs():
        import jax
        import jax.numpy as jnp
        _rk = jax.random.key(seed)
        x = -0.0002928 + 1 * jax.random.normal(jax.random.fold_in(_rk, 1), (32, 64, 256), jnp.float32)
        _lenS = 64 - jax.random.randint(jax.random.fold_in(_rk, 7), (32,), 0, max(1, 64 // 4) + 1, jnp.int32)
        _lenS2 = 256 - jax.random.randint(jax.random.fold_in(_rk, 8), (32,), 0, max(1, 256 // 4) + 1, jnp.int32)
        _ctx_1024P = jax.random.normal(jax.random.fold_in(_rk, 11), (32, 16, 256), jnp.float32)
        _ctx_1024c = jax.random.dirichlet(jax.random.fold_in(_rk, 511), 0.3 * jnp.ones((16,), jnp.float32), (32, 256))
        _ctx_1024t = jnp.einsum('bsk,bkd->bsd', _ctx_1024c, _ctx_1024P)
        _ctx_1024t = _ctx_1024t * jax.lax.rsqrt(jnp.mean(jnp.square(_ctx_1024t)) + 1e-12) * 0.953939
        ctx_1024 = -1.39393e-06 + 0.999914 * (_ctx_1024t + 0.3 * jax.random.normal(jax.random.fold_in(_rk, 611), (32, 256, 256), jnp.float32))
        _validS = jnp.arange(64)[None, :] < _lenS[:, None]
        _validS2 = jnp.arange(256)[None, :] < _lenS2[:, None]
        _causal = jnp.tril(jnp.ones((64, 64), dtype=bool))
        mask_1x1xSxS2_ik0 = jnp.where(jnp.broadcast_to(_validS2[0:1, None, None, :], (1, 1, 64, 256)), 0, 1).astype(jnp.int32)
        return (x, ctx_1024, mask_1x1xSxS2_ik0)
    x, ctx_1024, mask_1x1xSxS2_ik0 = _rec_inputs()

    def _L0_xattn_setup():
        import jax, jax.numpy as jnp
        import numpy as np
        B, N, DIM, H = (2, 512, 256, 16)
        HD = DIM // H
        SCALE = HD ** (-0.5)

        def _split_heads(x):
            b, n, _ = x.shape
            return x.reshape(b, n, H, HD).transpose(0, 2, 1, 3)
        key = jax.random.key(seed)
        ks = jax.random.split(key, 11)
        std = DIM ** (-0.5)
        inp = {'q': jax.random.normal(ks[0], (B, N, DIM), jnp.float32), 'k': jax.random.normal(ks[1], (B, N, DIM), jnp.float32), 'v': jax.random.normal(ks[2], (B, N, DIM), jnp.float32), 'mask': jnp.tril(jnp.ones((N, N), jnp.int32))[None, None], 'Wq': jax.random.normal(ks[3], (DIM, DIM), jnp.float32) * std, 'bq': jnp.zeros((DIM,), jnp.float32), 'Wk': jax.random.normal(ks[4], (DIM, DIM), jnp.float32) * std, 'bk': jnp.zeros((DIM,), jnp.float32), 'Wv': jax.random.normal(ks[5], (DIM, DIM), jnp.float32) * std, 'bv': jnp.zeros((DIM,), jnp.float32), 'Wo': jax.random.normal(ks[6], (DIM, DIM), jnp.float32) * std, 'bo': jnp.zeros((DIM,), jnp.float32)}
        return inp
    _L0_xattn_all = _L0_xattn_setup()
    _L0_xattn_in = {k: v for k, v in _L0_xattn_all.items() if k in ('Wq', 'bq', 'Wk', 'bk', 'Wv', 'bv', 'Wo', 'bo')}
    del _L0_xattn_all

    def _L0_attn_setup():
        import jax, jax.numpy as jnp
        import numpy as np
        from jax.scipy.linalg import solve_triangular
        HID = 256
        H = 4
        D = HID // H
        P = H * D
        KW = 4
        C = 64
        EPS = 1e-05

        def _dwconv_silu(x, w):
            y = jax.lax.conv_general_dilated(x.transpose(0, 2, 1), w, window_strides=(1,), padding=[(KW - 1, 0)], feature_group_count=P, dimension_numbers=('NCH', 'OIH', 'NCH'))
            return jax.nn.silu(y).transpose(0, 2, 1)

        def _forward(x, Wq, Wk, Wv, Wb, conv_q_w, conv_k_w, conv_v_w, rms_w, Wo):
            B, L, _ = x.shape
            nc = L // C
            dt = x.dtype
            q = _dwconv_silu(x @ Wq, conv_q_w).reshape(B, L, H, D)
            k = _dwconv_silu(x @ Wk, conv_k_w).reshape(B, L, H, D)
            v = _dwconv_silu(x @ Wv, conv_v_w).reshape(B, L, H, D)
            q = q / jnp.linalg.norm(q, axis=-1, keepdims=True)
            k = k / jnp.linalg.norm(k, axis=-1, keepdims=True)
            beta = jax.nn.sigmoid(x @ Wb)

            def to_chunks(t):
                return t.transpose(0, 2, 1, 3).reshape(B, H, nc, C, D).transpose(2, 0, 1, 3, 4)
            Qc = to_chunks(q) * D ** (-0.5)
            Kc = to_chunks(k)
            Vc = to_chunks(v)
            Bc = beta.transpose(0, 2, 1).reshape(B, H, nc, C, 1).transpose(2, 0, 1, 3, 4)
            I32 = jnp.eye(C, dtype=jnp.float32)
            M = jnp.tril(jnp.ones((C, C), dt))

            def step(S, ch):
                Q, K, V, bt = ch
                Kb = K * bt
                Vb = V * bt
                A = jnp.eye(C, dtype=dt) + jnp.tril(jnp.einsum('bhcd,bhed->bhce', Kb, K), -1)
                T = solve_triangular(A.astype(jnp.float32), jnp.broadcast_to(I32, A.shape), lower=True).astype(dt)
                W = T @ Kb
                U = T @ Vb
                St = S.swapaxes(-1, -2)
                mid = U - W @ St
                O = Q @ St + jnp.einsum('bhcd,bhed->bhce', Q, K) * M @ mid
                S_new = S + mid.swapaxes(-1, -2) @ K
                return (S_new, O)
            S0 = jnp.zeros((B, H, D, D), dt)
            S, Os = jax.lax.scan(step, S0, (Qc, Kc, Vc, Bc))
            o = Os.transpose(1, 0, 3, 2, 4).reshape(B, L, H, D)
            o = o * jax.lax.rsqrt(jnp.mean(o * o, axis=-1, keepdims=True) + EPS) * rms_w
            o = o.reshape(B, L, P) @ Wo
            return (o, S)

        def _reference_tuple_inner(x, Wq, Wk, Wv, Wb, conv_q_w, conv_k_w, conv_v_w, rms_w, Wo):
            return _forward(x, Wq, Wk, Wv, Wb, conv_q_w, conv_k_w, conv_v_w, rms_w, Wo)
        key = jax.random.key(seed)
        ks = jax.random.split(key, 10)
        B, L = (4, 1024)
        f32 = jnp.float32
        return {'x': jax.random.normal(ks[0], (B, L, HID), f32), 'Wq': jax.random.normal(ks[1], (HID, P), f32) * 0.02, 'Wk': jax.random.normal(ks[2], (HID, P), f32) * 0.02, 'Wv': jax.random.normal(ks[3], (HID, P), f32) * 0.02, 'Wb': jax.random.normal(ks[4], (HID, H), f32) * 0.02, 'conv_q_w': jax.random.normal(ks[5], (P, 1, KW), f32) * 0.2, 'conv_k_w': jax.random.normal(ks[6], (P, 1, KW), f32) * 0.2, 'conv_v_w': jax.random.normal(ks[7], (P, 1, KW), f32) * 0.2, 'rms_w': jnp.ones((D,), f32), 'Wo': jax.random.normal(ks[8], (P, HID), f32) * 0.02}
    _L0_attn_all = _L0_attn_setup()
    _L0_attn_in = {k: v for k, v in _L0_attn_all.items() if k in ('Wq', 'Wk', 'Wv', 'Wb', 'conv_q_w', 'conv_k_w', 'conv_v_w', 'rms_w', 'Wo')}
    del _L0_attn_all

    def _L0_ffn_setup():
        import jax, jax.numpy as jnp
        import numpy as np
        import math
        HID, HD, E, MIN_E = (256, 128, 16, 2)
        B, T = (4, 512)
        IS_CAUSAL = True

        def _l2norm(x, axis):
            return x / jnp.sqrt(jnp.sum(x * x, axis=axis, keepdims=True) + 1e-12)

        def _gating(hidden_states, sim_matrix, gates):
            b, t, c = hidden_states.shape
            flat = hidden_states.reshape(b * t, c)
            logits = _l2norm(flat, -1) @ _l2norm(sim_matrix, 0) - jax.nn.sigmoid(gates)
            gated = jax.nn.relu(logits)
            mask = (gated > 0).astype(gated.dtype)
            inactive = jnp.sum(mask, axis=1) == 0
            _, top_idx = jax.lax.top_k(logits, MIN_E)
            fb = jnp.sum(jax.nn.one_hot(top_idx, E, dtype=mask.dtype), axis=1)
            mask = mask + inactive[:, None].astype(mask.dtype) * fb
            masked = jnp.where(mask > 0, gated, -jnp.inf)
            probs = jax.nn.softmax(masked, axis=-1)
            return probs
        key = jax.random.key(seed)
        ks = jax.random.split(key, 6)
        a_qkv = math.sqrt(6.0 / (HID + HD))
        a_o = math.sqrt(6.0 / (HD + HID))
        return {'hidden_states': jax.random.normal(ks[0], (B, T, HID), jnp.float32), 'sim_matrix': jax.random.normal(ks[1], (HID, E), jnp.float32), 'gates': jnp.zeros((E,), jnp.float32), 'q_proj': jax.random.uniform(ks[2], (E, HID, HD), jnp.float32, -a_qkv, a_qkv), 'k_proj': jax.random.uniform(ks[3], (E, HID, HD), jnp.float32, -a_qkv, a_qkv), 'v_proj': jax.random.uniform(ks[4], (E, HID, HD), jnp.float32, -a_qkv, a_qkv), 'o_proj': jax.random.uniform(ks[5], (E, HD, HID), jnp.float32, -a_o, a_o)}
    _L0_ffn_all = _L0_ffn_setup()
    _L0_ffn_in = {k: v for k, v in _L0_ffn_all.items() if k in ('sim_matrix', 'gates', 'q_proj', 'k_proj', 'v_proj', 'o_proj')}
    del _L0_ffn_all

    def _L1_xattn_setup():
        import jax, jax.numpy as jnp
        import numpy as np
        EMBED_DIM = 256
        HEADS = 16
        HEAD_DIM = EMBED_DIM // HEADS
        key = jax.random.key(seed)
        ks = jax.random.split(key, 12)
        B, Sq, Sk, E = (4, 512, 512, EMBED_DIM)
        s = 1.0 / np.sqrt(E)
        return {'query': jax.random.normal(ks[0], (B, Sq, E), jnp.float32), 'key': jax.random.normal(ks[1], (B, Sk, E), jnp.float32), 'value': jax.random.normal(ks[2], (B, Sk, E), jnp.float32), 'Wq': jax.random.normal(ks[3], (E, E), jnp.float32) * s, 'bq': jnp.zeros((E,), jnp.float32), 'Wk': jax.random.normal(ks[4], (E, E), jnp.float32) * s, 'bk': jnp.zeros((E,), jnp.float32), 'Wv': jax.random.normal(ks[5], (E, E), jnp.float32) * s, 'bv': jnp.zeros((E,), jnp.float32), 'Wo': jax.random.normal(ks[6], (E, E), jnp.float32) * s, 'bo': jnp.zeros((E,), jnp.float32)}
    _L1_xattn_all = _L1_xattn_setup()
    _L1_xattn_in = {k: v for k, v in _L1_xattn_all.items() if k in ('Wq', 'bq', 'Wk', 'bk', 'Wv', 'bv', 'Wo', 'bo')}
    del _L1_xattn_all

    def _L1_attn_setup():
        import jax, jax.numpy as jnp
        import numpy as np
        key = jax.random.key(seed)
        x = jax.random.normal(key, (8, 512, 256), dtype=jnp.float32)
        return {'x': x}
    _L1_attn_all = _L1_attn_setup()
    _L1_attn_in = {k: v for k, v in _L1_attn_all.items() if k in ()}
    del _L1_attn_all

    def _L1_ffn_setup():
        import jax, jax.numpy as jnp
        import numpy as np
        TOP_K = 2
        key = jax.random.key(seed)
        k1, k2, k3, k4 = jax.random.split(key, 4)
        B, N, D, E, F = (4, 512, 256, 8, 1024)
        x = jax.random.normal(k1, (B, N, D), dtype=jnp.float32)
        gate_w = jax.random.normal(k2, (D, E), dtype=jnp.float32) * D ** (-0.5)
        w1 = jax.random.normal(k3, (E, D, F), dtype=jnp.float32) * D ** (-0.5)
        w2 = jax.random.normal(k4, (E, F, D), dtype=jnp.float32) * F ** (-0.5)
        return {'x': x, 'gate_w': gate_w, 'w1': w1, 'w2': w2}
    _L1_ffn_all = _L1_ffn_setup()
    _L1_ffn_in = {k: v for k, v in _L1_ffn_all.items() if k in ('gate_w', 'w1', 'w2')}
    del _L1_ffn_all
    return {'x': x, 'ctx_1024': ctx_1024, 'mask_1x1xSxS2_ik0': mask_1x1xSxS2_ik0, 'L0_xattn_Wq': _L0_xattn_in['Wq'], 'L0_xattn_bq': _L0_xattn_in['bq'], 'L0_xattn_Wk': _L0_xattn_in['Wk'], 'L0_xattn_bk': _L0_xattn_in['bk'], 'L0_xattn_Wv': _L0_xattn_in['Wv'], 'L0_xattn_bv': _L0_xattn_in['bv'], 'L0_xattn_Wo': _L0_xattn_in['Wo'], 'L0_xattn_bo': _L0_xattn_in['bo'], 'L0_attn_Wq': _L0_attn_in['Wq'], 'L0_attn_Wk': _L0_attn_in['Wk'], 'L0_attn_Wv': _L0_attn_in['Wv'], 'L0_attn_Wb': _L0_attn_in['Wb'], 'L0_attn_conv_q_w': _L0_attn_in['conv_q_w'], 'L0_attn_conv_k_w': _L0_attn_in['conv_k_w'], 'L0_attn_conv_v_w': _L0_attn_in['conv_v_w'], 'L0_attn_rms_w': _L0_attn_in['rms_w'], 'L0_attn_Wo': _L0_attn_in['Wo'], 'L0_ffn_sim_matrix': _L0_ffn_in['sim_matrix'], 'L0_ffn_gates': _L0_ffn_in['gates'], 'L0_ffn_q_proj': _L0_ffn_in['q_proj'], 'L0_ffn_k_proj': _L0_ffn_in['k_proj'], 'L0_ffn_v_proj': _L0_ffn_in['v_proj'], 'L0_ffn_o_proj': _L0_ffn_in['o_proj'], 'L1_xattn_Wq': _L1_xattn_in['Wq'], 'L1_xattn_bq': _L1_xattn_in['bq'], 'L1_xattn_Wk': _L1_xattn_in['Wk'], 'L1_xattn_bk': _L1_xattn_in['bk'], 'L1_xattn_Wv': _L1_xattn_in['Wv'], 'L1_xattn_bv': _L1_xattn_in['bv'], 'L1_xattn_Wo': _L1_xattn_in['Wo'], 'L1_xattn_bo': _L1_xattn_in['bo'], 'L1_ffn_gate_w': _L1_ffn_in['gate_w'], 'L1_ffn_w1': _L1_ffn_in['w1'], 'L1_ffn_w2': _L1_ffn_in['w2']}

def reference(x, ctx_1024, mask_1x1xSxS2_ik0, L0_xattn_Wq, L0_xattn_bq, L0_xattn_Wk, L0_xattn_bk, L0_xattn_Wv, L0_xattn_bv, L0_xattn_Wo, L0_xattn_bo, L0_attn_Wq, L0_attn_Wk, L0_attn_Wv, L0_attn_Wb, L0_attn_conv_q_w, L0_attn_conv_k_w, L0_attn_conv_v_w, L0_attn_rms_w, L0_attn_Wo, L0_ffn_sim_matrix, L0_ffn_gates, L0_ffn_q_proj, L0_ffn_k_proj, L0_ffn_v_proj, L0_ffn_o_proj, L1_xattn_Wq, L1_xattn_bq, L1_xattn_Wk, L1_xattn_bk, L1_xattn_Wv, L1_xattn_bv, L1_xattn_Wo, L1_xattn_bo, L1_ffn_gate_w, L1_ffn_w1, L1_ffn_w2):
    import jax
    import jax.numpy as jnp

    def _L0_xattn_ref(q, k, v, mask, Wq, bq, Wk, bk, Wv, bv, Wo, bo):
        import jax, jax.numpy as jnp
        import numpy as np
        B, N, DIM, H = (2, 512, 256, 16)
        HD = DIM // H
        SCALE = HD ** (-0.5)

        def _split_heads(x):
            b, n, _ = x.shape
            return x.reshape(b, n, H, HD).transpose(0, 2, 1, 3)
        qh = _split_heads(q @ Wq.T + bq)
        kh = _split_heads(k @ Wk.T + bk)
        vh = _split_heads(v @ Wv.T + bv)
        attn = jnp.einsum('bhqc,bhkc->bhqk', qh, kh) * SCALE
        attn = jnp.where(mask == 0, -jnp.inf, attn)
        attn = jax.nn.softmax(attn, axis=-1)
        out = jnp.einsum('bhqk,bhkc->bhqc', attn, vh)
        b, h, n, c = out.shape
        out = out.transpose(0, 2, 1, 3).reshape(b, n, h * c)
        return out @ Wo.T + bo

    def _L0_attn_ref(x, Wq, Wk, Wv, Wb, conv_q_w, conv_k_w, conv_v_w, rms_w, Wo):
        import jax, jax.numpy as jnp
        import numpy as np
        from jax.scipy.linalg import solve_triangular
        HID = 256
        H = 4
        D = HID // H
        P = H * D
        KW = 4
        C = 64
        EPS = 1e-05

        def _dwconv_silu(x, w):
            y = jax.lax.conv_general_dilated(x.transpose(0, 2, 1), w, window_strides=(1,), padding=[(KW - 1, 0)], feature_group_count=P, dimension_numbers=('NCH', 'OIH', 'NCH'))
            return jax.nn.silu(y).transpose(0, 2, 1)

        def _forward(x, Wq, Wk, Wv, Wb, conv_q_w, conv_k_w, conv_v_w, rms_w, Wo):
            B, L, _ = x.shape
            nc = L // C
            dt = x.dtype
            q = _dwconv_silu(x @ Wq, conv_q_w).reshape(B, L, H, D)
            k = _dwconv_silu(x @ Wk, conv_k_w).reshape(B, L, H, D)
            v = _dwconv_silu(x @ Wv, conv_v_w).reshape(B, L, H, D)
            q = q / jnp.linalg.norm(q, axis=-1, keepdims=True)
            k = k / jnp.linalg.norm(k, axis=-1, keepdims=True)
            beta = jax.nn.sigmoid(x @ Wb)

            def to_chunks(t):
                return t.transpose(0, 2, 1, 3).reshape(B, H, nc, C, D).transpose(2, 0, 1, 3, 4)
            Qc = to_chunks(q) * D ** (-0.5)
            Kc = to_chunks(k)
            Vc = to_chunks(v)
            Bc = beta.transpose(0, 2, 1).reshape(B, H, nc, C, 1).transpose(2, 0, 1, 3, 4)
            I32 = jnp.eye(C, dtype=jnp.float32)
            M = jnp.tril(jnp.ones((C, C), dt))

            def step(S, ch):
                Q, K, V, bt = ch
                Kb = K * bt
                Vb = V * bt
                A = jnp.eye(C, dtype=dt) + jnp.tril(jnp.einsum('bhcd,bhed->bhce', Kb, K), -1)
                T = solve_triangular(A.astype(jnp.float32), jnp.broadcast_to(I32, A.shape), lower=True).astype(dt)
                W = T @ Kb
                U = T @ Vb
                St = S.swapaxes(-1, -2)
                mid = U - W @ St
                O = Q @ St + jnp.einsum('bhcd,bhed->bhce', Q, K) * M @ mid
                S_new = S + mid.swapaxes(-1, -2) @ K
                return (S_new, O)
            S0 = jnp.zeros((B, H, D, D), dt)
            S, Os = jax.lax.scan(step, S0, (Qc, Kc, Vc, Bc))
            o = Os.transpose(1, 0, 3, 2, 4).reshape(B, L, H, D)
            o = o * jax.lax.rsqrt(jnp.mean(o * o, axis=-1, keepdims=True) + EPS) * rms_w
            o = o.reshape(B, L, P) @ Wo
            return (o, S)

        def _reference_tuple_inner(x, Wq, Wk, Wv, Wb, conv_q_w, conv_k_w, conv_v_w, rms_w, Wo):
            return _forward(x, Wq, Wk, Wv, Wb, conv_q_w, conv_k_w, conv_v_w, rms_w, Wo)
        return _reference_tuple_inner(x, Wq, Wk, Wv, Wb, conv_q_w, conv_k_w, conv_v_w, rms_w, Wo)[0]

    def _L0_ffn_ref(hidden_states, sim_matrix, gates, q_proj, k_proj, v_proj, o_proj):
        import jax, jax.numpy as jnp
        import numpy as np
        import math
        HID, HD, E, MIN_E = (256, 128, 16, 2)
        B, T = (4, 512)
        IS_CAUSAL = True

        def _l2norm(x, axis):
            return x / jnp.sqrt(jnp.sum(x * x, axis=axis, keepdims=True) + 1e-12)

        def _gating(hidden_states, sim_matrix, gates):
            b, t, c = hidden_states.shape
            flat = hidden_states.reshape(b * t, c)
            logits = _l2norm(flat, -1) @ _l2norm(sim_matrix, 0) - jax.nn.sigmoid(gates)
            gated = jax.nn.relu(logits)
            mask = (gated > 0).astype(gated.dtype)
            inactive = jnp.sum(mask, axis=1) == 0
            _, top_idx = jax.lax.top_k(logits, MIN_E)
            fb = jnp.sum(jax.nn.one_hot(top_idx, E, dtype=mask.dtype), axis=1)
            mask = mask + inactive[:, None].astype(mask.dtype) * fb
            masked = jnp.where(mask > 0, gated, -jnp.inf)
            probs = jax.nn.softmax(masked, axis=-1)
            return probs
        b, t, c = hidden_states.shape
        rw = _gating(hidden_states, sim_matrix, gates).reshape(b, t, E)
        q = jnp.einsum('btc,ech,bte->bth', hidden_states, q_proj, rw)
        k = jnp.einsum('btc,ech,bte->bth', hidden_states, k_proj, rw)
        v = jnp.einsum('btc,ech,bte->bth', hidden_states, v_proj, rw)
        scale = 1.0 / math.sqrt(HD)
        scores = jnp.einsum('bqh,bkh->bqk', q, k) * scale
        if IS_CAUSAL:
            causal = jnp.tril(jnp.ones((t, t), dtype=bool))
            scores = jnp.where(causal[None], scores, -jnp.inf)
        attn = jax.nn.softmax(scores, axis=-1)
        ao = jnp.einsum('bqk,bkh->bqh', attn, v)
        out = jnp.einsum('bth,ehc,bte->btc', ao, o_proj, rw)
        return out

    def _L1_xattn_ref(query, key, value, Wq, bq, Wk, bk, Wv, bv, Wo, bo):
        import jax, jax.numpy as jnp
        import numpy as np
        EMBED_DIM = 256
        HEADS = 16
        HEAD_DIM = EMBED_DIM // HEADS
        B, Sq, E = query.shape
        Sk = key.shape[1]
        H, D = (HEADS, HEAD_DIM)
        Q = (query @ Wq + bq).reshape(B, Sq, H, D).transpose(0, 2, 1, 3)
        K = (key @ Wk + bk).reshape(B, Sk, H, D).transpose(0, 2, 1, 3)
        V = (value @ Wv + bv).reshape(B, Sk, H, D).transpose(0, 2, 1, 3)
        scores = jnp.einsum('bhqd,bhkd->bhqk', Q, K) / jnp.sqrt(jnp.float32(D))
        attn = jax.nn.softmax(scores, axis=-1)
        out = jnp.einsum('bhqk,bhkd->bhqd', attn, V)
        out = out.transpose(0, 2, 1, 3).reshape(B, Sq, E)
        return out @ Wo + bo

    def _L1_attn_ref(x):
        import jax, jax.numpy as jnp
        import numpy as np
        scores = jnp.einsum('bld,bmd->blm', x, x)
        scores = jax.nn.softmax(scores, axis=1)
        return jnp.einsum('blm,bmd->bld', scores, x)

    def _L1_ffn_ref(x, gate_w, w1, w2):
        import jax, jax.numpy as jnp
        import numpy as np
        TOP_K = 2
        E = gate_w.shape[-1]
        gate_logits = jnp.einsum('bnd,de->bne', x, gate_w)
        gate_probs = jax.nn.softmax(gate_logits, axis=-1)
        top_k_probs, top_k_idx = jax.lax.top_k(gate_probs, TOP_K)
        top_k_weights = top_k_probs / jnp.sum(top_k_probs, axis=-1, keepdims=True)
        comb = jnp.sum(jax.nn.one_hot(top_k_idx, E, dtype=x.dtype) * top_k_weights[..., None], axis=2)
        h = jax.nn.gelu(jnp.einsum('bnd,edf->benf', x, w1))
        expert_out = jnp.einsum('benf,efd->bend', h, w2)
        output = jnp.einsum('bne,bend->bnd', comb, expert_out)
        return output
    x = x + _L0_xattn_ref(_layernorm(x, axis=-1), ctx_1024, ctx_1024, mask_1x1xSxS2_ik0, L0_xattn_Wq, L0_xattn_bq, L0_xattn_Wk, L0_xattn_bk, L0_xattn_Wv, L0_xattn_bv, L0_xattn_Wo, L0_xattn_bo)
    x = x + _L0_attn_ref(_layernorm(x, axis=-1), L0_attn_Wq, L0_attn_Wk, L0_attn_Wv, L0_attn_Wb, L0_attn_conv_q_w, L0_attn_conv_k_w, L0_attn_conv_v_w, L0_attn_rms_w, L0_attn_Wo)
    x = x + _L0_ffn_ref(_layernorm(x, axis=-1), L0_ffn_sim_matrix, L0_ffn_gates, L0_ffn_q_proj, L0_ffn_k_proj, L0_ffn_v_proj, L0_ffn_o_proj)
    x = x + _L1_xattn_ref(_layernorm(x, axis=-1), ctx_1024, ctx_1024, L1_xattn_Wq, L1_xattn_bq, L1_xattn_Wk, L1_xattn_bk, L1_xattn_Wv, L1_xattn_bv, L1_xattn_Wo, L1_xattn_bo)
    x = x + _L1_attn_ref(_layernorm(x, axis=-1))
    x = x + _L1_ffn_ref(_layernorm(x, axis=-1), L1_ffn_gate_w, L1_ffn_w1, L1_ffn_w2)
    return x

_drawn_inputs = setup_inputs


def setup_inputs(seed=0):
    import zlib

    import numpy as np

    out = dict(_drawn_inputs(seed))
    spreads = {'L0_xattn_bq': (0.0, 0.1),
     'L0_xattn_bk': (0.0, 0.8),
     'L0_xattn_bv': (0.0, 0.1),
     'L0_xattn_bo': (0.0, 0.1),
     'L0_attn_rms_w': (1.0, 0.2),
     'L0_ffn_gates': (0.0, 0.1),
     'L1_xattn_bq': (0.0, 0.296),
     'L1_xattn_bk': (0.0, 0.8),
     'L1_xattn_bv': (0.0, 0.1),
     'L1_xattn_bo': (0.0, 0.1)}
    factors = {}
    for name, (base, spread) in spreads.items():
        noise = np.random.default_rng([zlib.crc32(name.encode()), seed]).standard_normal(out[name].shape)
        drawn = base * np.exp(spread * noise) if base else spread * noise
        out[name] = jnp.asarray(drawn.astype(out[name].dtype))
    for name, factor in factors.items():
        out[name] = (out[name] * factor).astype(out[name].dtype)
    return out
```

```python
from contextlib import ExitStack

import concourse.bass as bass
from concourse import mybir

F32 = mybir.dt.float32
I32 = mybir.dt.int32
U32 = mybir.dt.uint32
ACT = mybir.ActivationFunctionType
ALU = mybir.AluOpType
AX = mybir.AxisListType

P = 128
BATCH, SEQ, DIM = 32, 64, 256
KEYS = 256
TOKENS = BATCH * SEQ
TILES = TOKENS // P
BPT = P // SEQ
KC = DIM // P
LN_EPS = 1e-5


class Resident:
    pass


class Stage:

    def __init__(self, nc, ctx, tag):
        self.nc, self.ctx, self.tag, self.sems = nc, ctx, tag, []
        ctx.callback(self.clear)

    def clear(self):
        if self.sems:
            self.nc.clear_and_free_semaphores(self.sems)
            self.nc.all_engine_barrier()

    def sb(self, name, shape, dt=F32):
        return self.ctx.enter_context(self.nc.sbuf_tensor(f"{self.tag}_{name}", shape, dt))

    def ps(self, name, shape=(P, 512)):
        return self.ctx.enter_context(self.nc.psum_tensor(f"{self.tag}_{name}_ps", list(shape), F32))

    def sem(self, name):
        self.sems.append(self.nc.alloc_semaphore(f"{self.tag}_{name}"))
        return self.sems[-1]


class Chain:

    def __init__(self, eng, sem, base=0):
        self.eng, self.sem, self.base, self.n = eng, sem, base, 0

    def step(self, ins):
        self.n += 1
        ins.then_inc(self.sem, 1)

    def settle(self):
        self.eng.wait_ge(self.sem, self.base + self.n)


def row(tensor, t):
    if isinstance(t, int):
        return tensor[:, t, :]
    return tensor[:, bass.ds(t, 1), :].rearrange("p a c -> p (a c)")


def norm_scales_vector(nc, res, chain, s_var, s_std, s_rstd):
    for t in range(TILES):
        chain.step(nc.vector.bn_aggr(res.mean_var[:, t, :], res.stats[:, t, :]))
    chain.settle()
    nc.vector.tensor_scalar(res.rstd[:, :, 0], res.mean_var[:, :, 1], LN_EPS, None, ALU.add).then_inc(s_var, 1)
    chain.eng.wait_ge(s_std, 1)
    nc.vector.reciprocal(res.rstd[:, :, 0], res.std[:, :]).then_inc(s_rstd, 1)
    chain.eng.wait_ge(s_rstd, 1)


def norm_scales_scalar(nc, res, act, s_var, s_std):
    act.wait_ge(s_var, 1)
    nc.scalar.activation(res.std[:, :], res.rstd[:, :, 0], ACT.Sqrt).then_inc(s_std, 1)


def normalise(nc, res, out, t):
    return nc.vector.tensor_scalar(out, row(res.x, t), row(res.mean_var, t)[:, 0:1], row(res.rstd, t),
                                   ALU.subtract, ALU.mult)


PAIR = 2
PAIRS_OF_TILES = TILES // PAIR


def two_at_a_time(eng, head, tail):
    head(0, 0)
    with eng.Fori(0, PAIRS_OF_TILES // 2 - 1) as i:
        for p in range(2):
            head(2 * i + p + 1, 1 - p)
            tail(2 * i + p, p)
    head(PAIRS_OF_TILES - 1, 1)
    tail(PAIRS_OF_TILES - 2, 0)
    tail(PAIRS_OF_TILES - 1, 1)


def pair_rows(tensor, u, j):
    return row(tensor, PAIR * u + j)


def pair_of(tensor, u):
    if isinstance(u, int):
        return tensor[:, PAIR * u:PAIR * (u + 1), :]
    return tensor[:, bass.ds(PAIR * u, PAIR), :]


def load_residual(nc, res, x, consts):
    with ExitStack() as ctx:
        st = Stage(nc, ctx, "load")
        s_x, s_const, s_stats = st.sem("x_loaded"), st.sem("const_loaded"), st.sem("stats")
        with nc.Block() as block:
            @block.sync
            def _(sp):
                sp.dma_start(res.x[:], x.rearrange("(t p) d -> p t d", p=P)).then_inc(s_x, 16)
                sp.dma_start(res.ident[:], consts["ident"]).then_inc(s_const, 16)
                sp.wait_ge(s_const, 16)

            @block.vector
            def _(dve):
                nc.vector.memset(res.ones[:], 1.0).then_inc(s_stats, 1)
                dve.wait_ge(s_x, 16)
                for t in range(TILES):
                    nc.vector.bn_stats(res.stats[:, t, :], res.x[:, t, :]).then_inc(s_stats, 1)
                dve.wait_ge(s_stats, TILES + 1)


HEADS, HEAD = 16, 16
HALF_HEADS = P // HEAD
PAIRS = HALF_HEADS // 2
GROUPS = BPT * KC
CTX_ROWS = BPT * KEYS
CTX_CHUNKS = CTX_ROWS // P
ORDER = ["S0", "S1", "G0", "G1", "T0", "G2", "S2", "V0", "T1", "G3", "S3", "V1", "G4", "T2", "G5", "V2",
         "T3", "G6", "G7", "V3", "O"]
PREP = 8
STEPS = PREP + 1
TURNED = 4
LOWEST = -3.0e38


def cross_attention(nc, res, tag, ctx_rows, w, mask):
    with ExitStack() as ctx:
        st = Stage(nc, ctx, tag)
        wq, wk, wv, wo = (st.sb(n, [P, KC, DIM]) for n in ("wq", "wk", "wv", "wo"))
        bq, bk, bv = (st.sb(n, [P, KC]) for n in ("bq", "bk", "bv"))
        bo = st.sb("bo", [P, DIM])
        headmask, parmask = st.sb("headmask", [P, HALF_HEADS]), st.sb("parmask", [P, 2])
        ctx_in = st.sb("ctx_in", [P, CTX_CHUNKS, DIM])
        ctxT = st.sb("ctxT", [P, KC, CTX_ROWS])
        keysT = [st.sb(f"keysT{i}", [P, KC, CTX_ROWS]) for i in range(2)]
        values = [st.sb(f"values{i}", [P, CTX_CHUNKS, DIM]) for i in range(2)]
        xn, xnT, queries = st.sb("xn", [P, DIM]), st.sb("xnT", [P, KC, P]), st.sb("queries", [P, KC, P])
        qspread = [st.sb(f"qspread{i}", [P, GROUPS, HALF_HEADS, SEQ]) for i in range(2)]
        peak, total, inverse = (st.sb(n, [P, 2, PAIRS]) for n in ("peak", "total", "inverse"))
        negpeak = st.sb("negpeak", [P, 2, PAIRS])
        probs = st.sb("probs", [P, 2, PAIRS, KEYS])
        probsT = st.sb("probsT", [P, PAIRS, 2, P])
        outT, outT0 = st.sb("outT", [P, KC, BPT, SEQ]), st.sb("outT0", [P, KC, BPT, SEQ])
        if mask is not None:
            maskadd, keep, zeros = st.sb("maskadd", [P, KEYS]), st.sb("keep", [P, KEYS], I32), st.sb("zeros", [P, KEYS])
            masked = st.sb("masked", [P, 2, PAIRS, KEYS])
        score_ps = [[st.ps(f"score{i}{j}") for j in range(2)] for i in range(2)]
        turn_ps = [st.ps(f"turn{j}") for j in range(2)]
        out_ps, stage_ps = st.ps("out"), st.ps("stage")

        s_w, s_ctx = st.sem("weights"), st.sem("ctx_loaded")
        s_var, s_std, s_rstd = st.sem("var"), st.sem("std"), st.sem("rstd")
        s_chain, s_tile, s_mask, s_maskadd = (st.sem(n) for n in ("vector_step", "tile_step", "mask", "maskadd"))
        s_bo, s_stats, s_seen = st.sem("bo_added"), st.sem("stats"), st.sem("scores_seen")
        s_xn = st.sem("xn_ready")
        s_full, s_free = st.sem("stage_full"), st.sem("stage_free")
        s_spread = st.sem("queries_spread")
        s_score, s_score_used = st.sem("scores_ready"), st.sem("scores_used")
        s_peak, s_exp = st.sem("peaks_ready"), st.sem("exp_done")
        s_probs = st.sem("probs_ready")
        if mask is None:
            s_score_used = s_exp
        s_turn, s_turned0, s_turned1 = st.sem("turn_full"), st.sem("turned_by_vector"), st.sem("turned_by_scalar")
        s_out, s_outT = st.sem("out_full"), st.sem("outT_ready")

        def step_number(t, s):
            return PREP + STEPS * t + s

        def out_step(t, last):
            return step_number(t, PREP) - (PREP if last else 0)

        N_LOADS = 10
        with nc.Block() as block:
            @block.sync
            def _(sp):
                for dst, src in ((wq, w["Wq"]), (wk, w["Wk"]), (wv, w["Wv"]), (wo, w["Wo"])):
                    sp.dma_start(dst[:], src.rearrange("(k p) n -> p k n", p=P)).then_inc(s_w, 16)
                for dst, src in ((bq, w["bq"]), (bk, w["bk"]), (bv, w["bv"]),
                                 (headmask, w["headmask"]), (parmask, w["parmask"])):
                    sp.dma_start(dst[:], src).then_inc(s_w, 16)
                sp.dma_start(bo[:], w["bo"].to_broadcast([P, DIM])).then_inc(s_w, 16)
                if mask is not None:
                    for half in range(2):
                        sp.dma_start(keep[half * SEQ:(half + 1) * SEQ, :], mask).then_inc(s_mask, 16)
                source = ctx_rows.rearrange("(j p) d -> p j d", p=P)
                sp.dma_start(ctx_in[:], source[:, 0:CTX_CHUNKS, :]).then_inc(s_ctx, 16)
                sp.wait_ge(s_full, 4)
                sp.dma_start(ctx_in[:], source[:, CTX_CHUNKS:2 * CTX_CHUNKS, :]).then_inc(s_ctx, 16)
                with sp.Fori(2, TILES) as t:
                    first = sp.snap(t * CTX_CHUNKS)
                    turned = sp.snap(t * STEPS + (step_number(0, 3) + 1 - 2 * STEPS))
                    sp.wait_ge(s_full, turned)
                    sp.dma_start(ctx_in[:], source[:, bass.ds(first, CTX_CHUNKS), :]).then_inc(s_ctx, 16)

            @block.tensor
            def _(pe):
                def prep(u, p, n, s):
                    if s == 0:
                        pe.wait_ge(s_xn, u + 1)
                    if s == 2:
                        pe.wait_ge(s_ctx, 16 * (u + 1))
                    pe.wait_ge(s_free, n)
                    if s == 0:
                        for k in range(KC):
                            mm = nc.tensor.transpose(stage_ps[:, k * P:(k + 1) * P], xn[:, k * P:(k + 1) * P], res.ident[:])
                    elif s == 1:
                        for m in range(KC):
                            for k in range(KC):
                                mm = nc.tensor.matmul(stage_ps[:, m * P:(m + 1) * P], wq[:, k, m * P:(m + 1) * P],
                                                      xnT[:, k, :], start=k == 0, stop=k == KC - 1)
                    elif s in (2, 3):
                        for j in range(CTX_CHUNKS):
                            mm = nc.tensor.transpose(stage_ps[:, j * P:(j + 1) * P],
                                                     ctx_in[:, j, (s - 2) * P:(s - 1) * P], res.ident[:])
                    elif s in (4, 5):
                        m = s - 4
                        for k in range(KC):
                            mm = nc.tensor.matmul(stage_ps[:, :], wk[:, k, m * P:(m + 1) * P], ctxT[:, k, :],
                                                  start=k == 0, stop=k == KC - 1)
                    else:
                        for j in range(2):
                            chunk = (s - 6) * 2 + j
                            for k in range(KC):
                                mm = nc.tensor.matmul(stage_ps[:, j * DIM:(j + 1) * DIM], ctxT[:, k, chunk * P:(chunk + 1) * P],
                                                      wv[:, k, :], start=k == 0, stop=k == KC - 1)
                    return mm

                def tile(t, p, last):
                    for what in ORDER:
                        g = int(what[1:] or 0)
                        b, half = g // KC, g % KC
                        if what[0] == "S":
                            if g == 0:
                                pe.wait_ge(s_spread, GROUPS * (t + 1))
                            pe.wait_ge(s_score_used, GROUPS * t + g + 1)
                            for r in range(PAIRS):
                                mm = nc.tensor.matmul(
                                    score_ps[g % 2][r // 2][:, (r % 2) * KEYS:(r % 2 + 1) * KEYS],
                                    qspread[p][:, g, 2 * r:2 * r + 2, :].rearrange("p h q -> p (h q)"),
                                    keysT[p][:, half, b * KEYS:(b + 1) * KEYS], start=True, stop=True)
                                if r % 2:
                                    mm.then_inc(s_score, 1)
                        elif what[0] == "T":
                            pe.wait_ge(s_probs, GROUPS * t + g + 1)
                            for j in range(2):
                                pe.wait_ge((s_turned0, s_turned1)[j], GROUPS * t + g)
                                for r in range(2 * j, 2 * j + 2):
                                    for k in range(2):
                                        at = ((r % 2) * 2 + k) * P
                                        mm = nc.tensor.transpose(turn_ps[j][:, at:at + P],
                                                                 probs[:, g % 2, r, k * P:(k + 1) * P], res.ident[:])
                                mm.then_inc(s_turn, 1)
                        elif what[0] == "V":
                            pe.wait_ge(s_turned0, GROUPS * t + g + 1)
                            pe.wait_ge(s_turned1, GROUPS * t + g + 1)
                            if g == 0:
                                pe.wait_ge(s_outT, t)
                            for r in range(PAIRS):
                                for k in range(2):
                                    chan = half * P + 2 * HEAD * r
                                    mm = nc.tensor.matmul(out_ps[2 * HEAD * r:2 * HEAD * (r + 1), g * P:(g + 1) * P],
                                                          values[p][:, b * 2 + k, chan:chan + 2 * HEAD],
                                                          probsT[:, r, k, :], start=k == 0, stop=k == 1)
                            if g == GROUPS - 1:
                                mm.then_inc(s_out, 1)
                        elif what[0] == "G":
                            if not last:
                                prep(t + 1, 1 - p, step_number(t, g), g).then_inc(s_full, 1)
                        else:
                            pe.wait_ge(s_free, out_step(t, last))
                            pe.wait_ge(s_outT, t + 1)
                            for k in range(KC):
                                mm = nc.tensor.matmul(stage_ps[:, 0:DIM], outT[:, k, :, :].rearrange("p b q -> p (b q)"),
                                                      wo[:, k, :], start=k == 0, stop=k == KC - 1)
                            mm.then_inc(s_full, 1)

                pe.wait_ge(s_w, 16 * N_LOADS)
                for s in range(PREP):
                    prep(0, 0, s, s).then_inc(s_full, 1)
                pe.wait_ge(s_free, PREP)
                with pe.Fori(0, TILES // 2 - 1) as i:
                    tile(2 * i, 0, False)
                    tile(2 * i + 1, 1, False)
                tile(TILES - 2, 0, False)
                tile(TILES - 1, 1, True)

            @block.scalar
            def _(act):
                def prep(u, p, n, s):
                    if s not in (1, 2, 4, 5):
                        return
                    act.wait_ge(s_full, n + 1)
                    if s == 1:
                        act.wait_ge(s_spread, GROUPS * u)
                        for m in range(KC):
                            ins = nc.scalar.activation(queries[:, m, :], stage_ps[:, m * P:(m + 1) * P], ACT.Identity,
                                                       bias=bq[:, m:m + 1])
                    elif s == 2:
                        ins = nc.scalar.activation(ctxT[:, 0, :], stage_ps[:, :], ACT.Copy)
                    else:
                        ins = nc.scalar.activation(keysT[p][:, s - 4, :], stage_ps[:, :], ACT.Identity,
                                                   bias=bk[:, s - 4:s - 3])
                    ins.then_inc(s_free, 1)

                def tile(t, p, last):
                    for what in ORDER:
                        g = int(what[1:] or 0)
                        if what[0] == "S":
                            act.wait_ge(s_peak, GROUPS * t + g + 1)
                            act.wait_ge(s_turn, 2 * (GROUPS * t + g + 1))
                            for r in range(PAIRS):
                                if mask is None:
                                    scores = score_ps[g % 2][r // 2][:, (r % 2) * KEYS:(r % 2 + 1) * KEYS]
                                else:
                                    scores = masked[:, g % 2, r, :]
                                ins = nc.scalar.activation(probs[:, g % 2, r, :], scores, ACT.Exp,
                                                           bias=negpeak[:, g % 2, r:r + 1],
                                                           accum_out=total[:, g % 2, r:r + 1])
                            ins.then_inc(s_exp, 1)
                        elif what[0] == "T":
                            act.wait_ge(s_turn, TURNED + 2 * (GROUPS * t + g) + 2)
                            nc.scalar.activation(probsT[:, 2:4, :, :].rearrange("p r k q -> p (r k q)"),
                                                 turn_ps[1][:, :], ACT.Copy).then_inc(s_turned1, 1)
                        elif what[0] == "G" and not last:
                            prep(t + 1, 1 - p, step_number(t, g), g)

                norm_scales_scalar(nc, res, act, s_var, s_std)
                act.wait_ge(s_w, 16 * N_LOADS)
                for s in range(PREP):
                    prep(0, 0, s, s)
                with act.Fori(0, TILES // 2 - 1) as i:
                    tile(2 * i, 0, False)
                    tile(2 * i + 1, 1, False)
                tile(TILES - 2, 0, False)
                tile(TILES - 1, 1, True)

            @block.gpsimd
            def _(pool):
                def spread(u, p, n):
                    pool.wait_ge(s_free, n + 1)
                    for b in range(BPT):
                        for half in range(KC):
                            nc.gpsimd.tensor_tensor(
                                qspread[p][:, b * KC + half, :, :],
                                queries[:, half, b * SEQ:(b + 1) * SEQ].unsqueeze(1).to_broadcast([P, HALF_HEADS, SEQ]),
                                headmask[:, :].unsqueeze(2).to_broadcast([P, HALF_HEADS, SEQ]),
                                ALU.mult).then_inc(s_spread, 1)

                pool.wait_ge(s_w, 16 * N_LOADS)
                spread(0, 0, 1)
                spread(1, 1, step_number(0, 1))
                with pool.Fori(1, TILES // 2) as i:
                    for p in range(2):
                        before = pool.snap((2 * i + p) * GROUPS - 2 * GROUPS + GROUPS)
                        pool.wait_ge(s_score_used, 2 + before)
                        spread(2 * i + p, p, step_number(2 * i + p - 1, 1))

            @block.vector
            def _(dve):
                chain = Chain(dve, s_chain)

                def normalised(u):
                    normalise(nc, res, xn[:, :], u).then_inc(s_xn, 1)
                    dve.wait_ge(s_xn, u + 1)
                    nc.vector.tensor_tensor(row(res.x, u), row(res.x, u), bo[:, :], ALU.add).then_inc(s_bo, 1)

                def prep(u, p, n, s):
                    if s == 0:
                        normalised(u)
                    if s not in (0, 3, 6, 7):
                        return
                    dve.wait_ge(s_full, n + 1)
                    if s == 0:
                        ins = nc.vector.tensor_copy(xnT[:, :, :].rearrange("p k q -> p (k q)"), stage_ps[:, 0:DIM])
                    elif s == 3:
                        ins = nc.vector.tensor_copy(ctxT[:, 1, :], stage_ps[:, :])
                    else:
                        j = 2 * (s - 6)
                        ins = nc.vector.tensor_copy(values[p][:, j:j + 2, :].rearrange("p j d -> p (j d)"), stage_ps[:, :])
                    ins.then_inc(s_free, 1)

                def tile(t, p, last):
                    chain = Chain(dve, s_tile, t * (GROUPS + KC))
                    for what in ORDER:
                        g = int(what[1:] or 0)
                        k = GROUPS * t + g
                        if what[0] == "S":
                            if mask is None:
                                for j in range(2):
                                    dve.wait_ge(s_score, 2 * k + j + 1)
                                    ins = nc.vector.tensor_reduce(
                                        negpeak[:, g % 2, 2 * j:2 * j + 2],
                                        score_ps[g % 2][j][:, :].rearrange("p (r k) -> p r k", r=2),
                                        AX.X, ALU.max, negate=True)
                                ins.then_inc(s_peak, 1)
                            else:
                                dve.wait_ge(s_exp, k + 1)
                                for r in range(PAIRS):
                                    if r % 2 == 0:
                                        dve.wait_ge(s_score, 2 * k + r // 2 + 1)
                                        dve.sem_inc(s_seen, 1)
                                    ins = nc.vector.tensor_tensor_reduce(
                                        masked[:, g % 2, r, :],
                                        score_ps[g % 2][r // 2][:, (r % 2) * KEYS:(r % 2 + 1) * KEYS],
                                        maskadd[:, :], 1.0, LOWEST, ALU.add, ALU.max, peak[:, g % 2, r:r + 1])
                                ins.then_inc(s_score_used, 1)
                                dve.wait_ge(s_score_used, 2 + k + 1)
                                nc.vector.tensor_scalar(negpeak[:, g % 2, :], peak[:, g % 2, :], -1.0, None,
                                                        ALU.mult).then_inc(s_peak, 1)
                        elif what[0] == "T":
                            dve.wait_ge(s_exp, 2 + k + 1)
                            chain.step(nc.vector.reciprocal(inverse[:, g % 2, :], total[:, g % 2, :]))
                            chain.settle()
                            for r in range(PAIRS):
                                ins = nc.vector.tensor_scalar(probs[:, g % 2, r, :], probs[:, g % 2, r, :],
                                                              inverse[:, g % 2, r:r + 1], None, ALU.mult)
                            ins.then_inc(s_probs, 1)
                            dve.wait_ge(s_turn, TURNED + 2 * k + 1)
                            nc.vector.tensor_copy(probsT[:, 0:2, :, :].rearrange("p r k q -> p (r k q)"),
                                                  turn_ps[0][:, :]).then_inc(s_turned0, 1)
                        elif what[0] == "G" and not last:
                            prep(t + 1, 1 - p, step_number(t, g), g)
                        elif what[0] == "O":
                            dve.wait_ge(s_out, t + 1)
                            o = out_ps[:, :].rearrange("p (b m e q) -> p b m e q", b=BPT, m=KC, e=2)
                            for m in range(KC):
                                chain.step(nc.vector.tensor_scalar(outT0[:, m, :, :], o[:, :, m, 0, :], parmask[:, 0:1],
                                                                   bv[:, m:m + 1], ALU.mult, ALU.add))
                            chain.settle()
                            for m in range(KC):
                                ins = nc.vector.scalar_tensor_tensor(outT[:, m, :, :], o[:, :, m, 1, :], parmask[:, 1:2],
                                                                     outT0[:, m, :, :], ALU.mult, ALU.add)
                            ins.then_inc(s_outT, 1)
                            dve.wait_ge(s_bo, t + 1)
                            dve.wait_ge(s_full, out_step(t, last) + 1)
                            nc.vector.tensor_tensor(row(res.x, t), row(res.x, t), stage_ps[:, 0:DIM],
                                                    ALU.add).then_inc(s_free, 1)
                            dve.wait_ge(s_free, out_step(t, last) + 1)
                            nc.vector.bn_stats(row(res.stats, t), row(res.x, t)).then_inc(s_stats, 1)

                norm_scales_vector(nc, res, chain, s_var, s_std, s_rstd)
                dve.sem_inc(s_score_used, 2)
                dve.sem_inc(s_turn, TURNED)
                if mask is not None:
                    dve.sem_inc(s_exp, 2)
                    nc.vector.memset(maskadd[:], LOWEST).then_inc(s_maskadd, 1)
                    nc.vector.memset(zeros[:], 0.0).then_inc(s_maskadd, 1)
                    dve.wait_ge(s_maskadd, 2)
                    dve.wait_ge(s_mask, 32)
                    nc.vector.copy_predicated(maskadd[:, :], keep[:, :], zeros[:, :]).then_inc(s_maskadd, 1)
                    dve.wait_ge(s_maskadd, 3)
                dve.wait_ge(s_w, 16 * N_LOADS)
                for s in range(PREP):
                    prep(0, 0, s, s)
                with dve.Fori(0, TILES // 2 - 1) as i:
                    tile(2 * i, 0, False)
                    tile(2 * i + 1, 1, False)
                tile(TILES - 2, 0, False)
                tile(TILES - 1, 1, True)
                dve.wait_ge(s_stats, TILES)


D_HEADS, D_HEAD, TAPS = 4, 64, 4
LEVELS = (2, 4, 8, 16, 32)
QKV = 3 * KC
MASK_OPS = 4 + len(LEVELS)
DELTA_ORDER = ["A0", "Y1", "B0", "T1", "A1", "Y2", "B1", "T2", "A2", "Y3", "B2", "T3", "A3", "Y4", "T4", "A4",
               "Y5", "T5", "A5", "U", "O"]


def delta_rule(nc, res, a):
    with ExitStack() as ctx:
        st = Stage(nc, ctx, "delta")
        wqkv = [st.sb(f"w{n}", [P, KC, DIM]) for n in "qkv"]
        wb, taps = st.sb("wb", [P, KC, D_HEADS]), st.sb("taps", [P, QKV, TAPS])
        head_ones = st.sb("head_ones", [P, 2])
        strict, causalT = st.sb("strict", [P, P]), st.sb("causalT", [P, P])
        join1, join1T = st.sb("join1", [P, P]), st.sb("join1T", [P, P])
        joinT = st.sb("joinT", [P, len(LEVELS), P])
        xn, xnT, pre = st.sb("xn", [P, DIM]), st.sb("xnT", [P, KC, P]), st.sb("pre", [P, QKV, BPT, SEQ])
        qkvT = [st.sb(f"qkvT{i}", [P, QKV, P]) for i in range(2)]
        squares = st.sb("squares", [P, 2 * KC, P])
        inv_sq, inv_norm = ([st.sb(f"{n}{i}", [P, 2 * D_HEADS]) for i in range(2)] for n in ("inv_sq", "inv_norm"))
        tanh, beta = st.sb("tanh", [P, D_HEADS]), [st.sb(f"beta{i}", [P, D_HEADS]) for i in range(2)]
        row_scale, value_scale = st.sb("row_scale", [P, D_HEADS]), st.sb("value_scale", [P, D_HEADS])
        query_scale = [st.sb(f"query_scale{i}", [P, D_HEADS]) for i in range(2)]
        vb = [st.sb(f"vb{i}", [P, D_HEADS, D_HEAD]) for i in range(2)]
        lower, lowerT = st.sb("lower", [P, D_HEADS, P]), st.sb("lowerT", [P, D_HEADS, P])
        part, partT = st.sb("part", [P, D_HEADS, P]), st.sb("partT", [P, D_HEADS, P])
        joined = [st.sb(f"joined{i}", [P, len(LEVELS), D_HEADS, P]) for i in range(2)]
        first, firstT = ([st.sb(f"{n}{i}", [P, D_HEADS, P]) for i in range(2)] for n in ("first", "firstT"))
        attnT = [st.sb(f"attnT{i}", [P, D_HEADS, P]) for i in range(2)]
        inv, invT, rest = (st.sb(n, [P, D_HEADS, P]) for n in ("inv", "invT", "rest"))
        u_sb, o_sq = st.sb("u", [P, DIM]), st.sb("o_sq", [P, DIM])
        qk_ps, v_ps = st.ps("qk"), st.ps("v")
        gram_ps = [st.ps(f"gram{i}") for i in range(2)]
        y_ps, t_ps, tt_ps, uo_ps = (st.ps(n) for n in ("y", "t", "tt", "uo"))
        BETA, SUMS = DIM, DIM + D_HEADS

        s = Resident()
        s.weights, s.var, s.std, s.rstd = (st.sem(n) for n in ("weights", "var", "std", "rstd"))
        s.vector_step, s.xn, s.turned, s.xnT = (st.sem(n) for n in ("vector_step", "xn", "turned", "xnT"))
        s.qk, s.v, s.conv, s.conv_step = (st.sem(n) for n in ("qk", "v", "conv", "conv_step"))
        s.silu, s.tanh, s.squares, s.sums = (st.sem(n) for n in ("silu", "tanh", "squares", "sums"))
        s.inv_sq, s.inv_norm, s.scales, s.vturned = (st.sem(n) for n in ("inv_sq", "inv_norm", "scales", "vturned"))
        s.vb, s.gram, s.attn, s.attn_masked = (st.sem(n) for n in ("vb", "gram", "attn", "attn_masked"))
        s.lower, s.lturned, s.lowerT, s.masks = (st.sem(n) for n in ("lower", "lturned", "lowerT", "masks"))
        s.y, s.rest, s.t, s.tt = (st.sem(n) for n in ("y", "rest", "t", "tt"))
        s.inv, s.invT, s.u_full, s.u_copied = (st.sem(n) for n in ("inv", "invT", "u_full", "u_copied"))
        s.o_full, s.o_read, s.out_step = (st.sem(n) for n in ("o_full", "o_read", "out_step"))
        every = lambda m, h=D_HEADS: m.unsqueeze(1).to_broadcast([P, h, P])
        N_LOADS = 11
        with nc.Block() as block:
            @block.sync
            def _(sp):
                for dst, n in zip(wqkv, "qkv"):
                    sp.dma_start(dst[:], a[f"L0_attn_W{n}"].rearrange("(k p) n -> p k n", p=P)).then_inc(s.weights, 16)
                sp.dma_start(wb[:], a["L0_attn_Wb"].rearrange("(k p) n -> p k n", p=P)).then_inc(s.weights, 16)
                sp.dma_start(taps[:], a["L0_attn_taps"]).then_inc(s.weights, 16)
                for dst, n in ((head_ones, "head_ones"), (strict, "strict"), (causalT, "causalT"), (join1, "join1"),
                               (join1T, "join1T"), (joinT, "joinT")):
                    sp.dma_start(dst[:], a[n]).then_inc(s.weights, 16)
                sp.wait_ge(s.weights, 16 * N_LOADS)

            @block.tensor
            def _(pe):
                def a_step(u, p, n):
                    if n == 0:
                        pe.wait_ge(s.xn, u + 1)
                        pe.wait_ge(s.conv, u)
                        for k in range(KC):
                            mm = nc.tensor.transpose(qk_ps[:, k * P:(k + 1) * P], xn[:, k * P:(k + 1) * P], res.ident[:])
                        mm.then_inc(s.turned, 1)
                    elif n == 1:
                        pe.wait_ge(s.xnT, u + 1)
                        for i in range(2 * KC):
                            for k in range(KC):
                                mm = nc.tensor.matmul(qk_ps[:, i * P:(i + 1) * P],
                                                      wqkv[i // KC][:, k, (i % KC) * P:(i % KC + 1) * P], xnT[:, k, :],
                                                      start=k == 0, stop=k == KC - 1)
                        mm.then_inc(s.qk, 1)
                        pe.wait_ge(s.inv_sq, u)
                        pe.wait_ge(s.tanh, u)
                        for i in range(KC):
                            for k in range(KC):
                                nc.tensor.matmul(v_ps[:, i * P:(i + 1) * P], wqkv[2][:, k, i * P:(i + 1) * P], xnT[:, k, :],
                                                 start=k == 0, stop=k == KC - 1)
                        for k in range(KC):
                            mm = nc.tensor.matmul(v_ps[:, BETA:BETA + D_HEADS], xnT[:, k, :], wb[:, k, :],
                                                  start=k == 0, stop=k == KC - 1)
                        mm.then_inc(s.v, 1)
                    elif n == 5:
                        pe.wait_ge(s.squares, u + 1)
                        for i in range(2 * KC):
                            mm = nc.tensor.matmul(v_ps[:, SUMS + 2 * i:SUMS + 2 * i + 2], squares[:, i, :], head_ones[:],
                                                  start=True, stop=True)
                        mm.then_inc(s.sums, 1)

                def b_step(u, p, n):
                    if n == 0:
                        pe.wait_ge(s.silu, u + 1)
                        pe.wait_ge(s.lowerT, u)
                        for i in range(KC):
                            mm = nc.tensor.transpose(gram_ps[0][:, i * P:(i + 1) * P], qkvT[p][:, 2 * KC + i, :], res.ident[:])
                        mm.then_inc(s.vturned, 1)
                    elif n == 1:
                        pe.wait_ge(s.vb, u + 1)
                        for of in range(2):
                            for h in range(D_HEADS):
                                rows = slice(D_HEAD * (h % 2), D_HEAD * (h % 2 + 1))
                                col = (2 * of + h // 2) * P
                                mm = nc.tensor.matmul(gram_ps[h % 2][:, col:col + P], qkvT[p][rows, KC + h // 2, :],
                                                      qkvT[p][rows, (KC if of == 0 else 0) + h // 2, :], start=True, stop=True)
                                if of == 1 and h == D_HEADS - 2:
                                    mm.then_inc(s.gram, 1)
                        mm.then_inc(s.gram, 1)
                    else:
                        pe.wait_ge(s.lower, u + 1)
                        pe.wait_ge(s.attn_masked, u + 1)
                        for h in range(D_HEADS):
                            mm = nc.tensor.transpose(gram_ps[0][:, h * P:(h + 1) * P], lower[:, h, :], res.ident[:])
                        mm.then_inc(s.lturned, 1)

                def tail(t, p, what):
                    if what[0] == "Y":
                        n = int(what[1:])
                        if n == 1:
                            pe.wait_ge(s.masks, MASK_OPS * (t + 1))
                            m = first[p]
                        else:
                            pe.wait_ge(s.inv, (len(LEVELS) - 1) * t + n - 1)
                            m = inv
                        for h in range(D_HEADS):
                            mm = nc.tensor.matmul(y_ps[:, h * P:(h + 1) * P], joined[p][:, n - 1, h, :], m[:, h, :],
                                                  start=True, stop=True)
                        mm.then_inc(s.y, 1)
                    elif what[0] == "T":
                        n = int(what[1:])
                        mT = firstT[p] if n == 1 else invT
                        pe.wait_ge(s.rest, len(LEVELS) * t + n)
                        pe.wait_ge(s.invT, len(LEVELS) * t + n - 1)
                        if n < len(LEVELS):
                            for h in range(D_HEADS):
                                mm = nc.tensor.matmul(t_ps[:, h * P:(h + 1) * P], mT[:, h, :], rest[:, h, :],
                                                      start=True, stop=True)
                            mm.then_inc(s.t, 1)
                        for h in range(D_HEADS):
                            mm = nc.tensor.matmul(tt_ps[:, h * P:(h + 1) * P], rest[:, h, :], mT[:, h, :],
                                                  start=True, stop=True)
                        mm.then_inc(s.tt, 1)
                    elif what == "U":
                        pe.wait_ge(s.invT, len(LEVELS) * (t + 1))
                        pe.wait_ge(s.o_read, t)
                        for h in range(D_HEADS):
                            mm = nc.tensor.matmul(uo_ps[:, h * D_HEAD:(h + 1) * D_HEAD], invT[:, h, :], vb[p][:, h, :],
                                                  start=True, stop=True)
                        mm.then_inc(s.u_full, 1)
                    else:
                        pe.wait_ge(s.u_copied, t + 1)
                        for h in range(D_HEADS):
                            mm = nc.tensor.matmul(uo_ps[:, DIM + h * D_HEAD:DIM + (h + 1) * D_HEAD], attnT[p][:, h, :],
                                                  u_sb[:, h * D_HEAD:(h + 1) * D_HEAD], start=True, stop=True)
                        mm.then_inc(s.o_full, 1)

                pe.wait_ge(s.weights, 16 * N_LOADS)
                delta_loop(pe, a_step, b_step, tail)

            @block.scalar
            def _(act):
                def a_step(u, p, n):
                    if n == 0:
                        act.wait_ge(s.turned, u + 1)
                        nc.scalar.activation(xnT[:, :, :].rearrange("p k q -> p (k q)"), qk_ps[:, 0:DIM],
                                             ACT.Copy).then_inc(s.xnT, 1)
                    elif n == 1:
                        act.wait_ge(s.v, u + 1)
                        act.wait_ge(s.inv_sq, u)
                        nc.scalar.activation(tanh[:, :], v_ps[:, BETA:BETA + D_HEADS], ACT.Tanh, scale=0.5).then_inc(s.tanh, 1)
                    elif n == 5:
                        if not isinstance(u, int) or u > 1:
                            act.wait_ge(s.gram, 2 * (u - 1))
                        act.wait_ge(s.conv, u + 1)
                        nc.scalar.activation(qkvT[p][:, :, :].rearrange("p i q -> p (i q)"),
                                             pre[:, :, :, :].rearrange("p i b q -> p (i b q)"), ACT.Silu).then_inc(s.silu, 1)
                        act.wait_ge(s.silu, u + 1)
                        act.wait_ge(s.sums, u)
                        nc.scalar.activation(squares[:, :, :], qkvT[p][:, 0:2 * KC, :], ACT.Square).then_inc(s.squares, 1)
                        act.wait_ge(s.inv_sq, u + 1)
                        if not isinstance(u, int) or u > 1:
                            act.wait_ge(s.scales, u - 1)
                        nc.scalar.activation(inv_norm[p][:, :], inv_sq[p][:, :], ACT.Sqrt).then_inc(s.inv_norm, 1)

                def b_step(u, p, n):
                    if n == 2:
                        act.wait_ge(s.lturned, u + 1)
                        act.wait_ge(s.masks, MASK_OPS * u)
                        nc.scalar.activation(lowerT[:, :, :].rearrange("p h q -> p (h q)"), gram_ps[0][:, :],
                                             ACT.Copy).then_inc(s.lowerT, 1)

                def tail(t, p, what):
                    if what[0] == "T" and int(what[1:]) < len(LEVELS):
                        act.wait_ge(s.t, (len(LEVELS) - 1) * t + int(what[1:]))
                        nc.scalar.activation(inv[:, :, :].rearrange("p h q -> p (h q)"), t_ps[:, :],
                                             ACT.Copy).then_inc(s.inv, 1)
                    elif what == "U":
                        act.wait_ge(s.u_full, t + 1)
                        nc.scalar.activation(u_sb[:, :], uo_ps[:, 0:DIM], ACT.Copy).then_inc(s.u_copied, 1)

                norm_scales_scalar(nc, res, act, s.var, s.std)
                delta_loop(act, a_step, b_step, tail)

            @block.gpsimd
            def _(pool):
                def a_step(u, p, n):
                    pass

                def b_step(u, p, n):
                    if n != 2:
                        return
                    pool.wait_ge(s.lowerT, u + 1)
                    if not isinstance(u, int) or u > 1:
                        pool.wait_ge(s.y, len(LEVELS) * (u - 1))
                    nc.gpsimd.tensor_tensor(partT[:], lowerT[:], every(join1T[:, :]), ALU.mult).then_inc(s.masks, 1)
                    nc.gpsimd.tensor_tensor(part[:], lower[:], every(join1[:, :]), ALU.mult).then_inc(s.masks, 1)
                    for i in range(len(LEVELS)):
                        nc.gpsimd.tensor_tensor(joined[p][:, i, :, :], lowerT[:], every(joinT[:, i, :]),
                                                ALU.mult).then_inc(s.masks, 1)
                    pool.wait_ge(s.masks, MASK_OPS * u + 2)
                    nc.gpsimd.tensor_tensor(firstT[p][:], every(res.ident[:, :]), partT[:], ALU.subtract).then_inc(s.masks, 1)
                    nc.gpsimd.tensor_tensor(first[p][:], every(res.ident[:, :]), part[:], ALU.subtract).then_inc(s.masks, 1)

                def tail(t, p, what):
                    pass

                pool.wait_ge(s.weights, 16 * N_LOADS)
                delta_loop(pool, a_step, b_step, tail)

            @block.vector
            def _(dve):
                def a_step(u, p, n):
                    if n == 0:
                        dve.wait_ge(s.turned, u)
                        normalise(nc, res, xn[:, :], u).then_inc(s.xn, 1)
                    if 1 <= n <= TAPS:
                        back = n - 1
                        if n == 1:
                            dve.wait_ge(s.silu, u)
                            dve.wait_ge(s.qk, u + 1)
                            dve.wait_ge(s.tanh, u + 1)
                        else:
                            dve.wait_ge(s.conv_step, (TAPS - 1) * u + n - 1)
                        for i in range(QKV):
                            src = (qk_ps[:, i * P:(i + 1) * P] if i < 2 * KC else v_ps[:, (i - 2 * KC) * P:(i - 2 * KC + 1) * P])
                            src = src.rearrange("p (b q) -> p b q", b=BPT)
                            tap = taps[:, i, TAPS - 1 - back:TAPS - back]
                            if n == 1:
                                ins = nc.vector.tensor_scalar(pre[:, i, :, :], src, tap, None, ALU.mult)
                            else:
                                ins = nc.vector.scalar_tensor_tensor(pre[:, i, :, back:], src[:, :, 0:SEQ - back], tap,
                                                                     pre[:, i, :, back:], ALU.mult, ALU.add)
                        ins.then_inc(s.conv if n == TAPS else s.conv_step, 1)
                    if n == 5:
                        nc.vector.tensor_scalar(beta[p][:, :], tanh[:, :], 0.5, 0.5, ALU.mult, ALU.add)
                        dve.wait_ge(s.sums, u + 1)
                        nc.vector.reciprocal(inv_sq[p][:, :], v_ps[:, SUMS:SUMS + 2 * D_HEADS]).then_inc(s.inv_sq, 1)

                def b_step(u, p, n):
                    if n == 0:
                        dve.wait_ge(s.inv_sq, u + 1)
                        nc.vector.tensor_tensor(row_scale[:, :], beta[p][:, :], inv_sq[p][:, D_HEADS:], ALU.mult)
                        dve.wait_ge(s.inv_norm, u + 1)
                        nc.vector.tensor_scalar(query_scale[p][:, :], inv_norm[p][:, 0:D_HEADS], D_HEAD ** -0.5, None, ALU.mult)
                        nc.vector.tensor_tensor(value_scale[:, :], beta[p][:, :], inv_norm[p][:, D_HEADS:],
                                                ALU.mult).then_inc(s.scales, 1)
                        dve.wait_ge(s.scales, u + 1)
                        dve.wait_ge(s.vturned, u + 1)
                        if not isinstance(u, int) or u > 1:
                            dve.wait_ge(s.u_full, u - 1)
                        nc.vector.tensor_tensor(vb[p][:, :, :], gram_ps[0][:, 0:DIM].rearrange("p (h d) -> p h d", h=D_HEADS),
                                                value_scale[:, :].unsqueeze(2).to_broadcast([P, D_HEADS, D_HEAD]),
                                                ALU.mult).then_inc(s.vb, 1)
                    elif n == 1:
                        dve.wait_ge(s.gram, 2 * (u + 1))
                        dve.wait_ge(s.masks, MASK_OPS * u)
                        for h in range(D_HEADS):
                            ins = nc.vector.scalar_tensor_tensor(lower[:, h, :], gram_ps[h % 2][:, h // 2 * P:(h // 2 + 1) * P],
                                                                 row_scale[:, h:h + 1], strict[:, :], ALU.mult, ALU.mult)
                        ins.then_inc(s.lower, 1)
                        if not isinstance(u, int) or u > 1:
                            dve.wait_ge(s.o_full, u - 1)
                        for e in range(2):
                            ins = nc.vector.tensor_tensor(
                                attnT[p][:, :, :].rearrange("p (g e) q -> p g e q", e=2)[:, :, e, :],
                                gram_ps[e][:, 2 * P:].rearrange("p (g q) -> p g q", g=2),
                                every(causalT[:, :], 2), ALU.mult)
                        ins.then_inc(s.attn_masked, 1)

                def tail(t, p, what):
                    if what[0] == "Y":
                        dve.wait_ge(s.y, len(LEVELS) * t + int(what[1:]))
                        nc.vector.tensor_tensor(rest[:, :, :], every(res.ident[:, :]),
                                                y_ps[:, :].rearrange("p (h q) -> p h q", h=D_HEADS),
                                                ALU.subtract).then_inc(s.rest, 1)
                    elif what[0] == "T":
                        dve.wait_ge(s.tt, len(LEVELS) * t + int(what[1:]))
                        nc.vector.tensor_copy(invT[:, :, :].rearrange("p h q -> p (h q)"), tt_ps[:, :]).then_inc(s.invT, 1)
                    elif what == "O":
                        dve.wait_ge(s.o_full, t + 1)
                        nc.vector.tensor_tensor(
                            row(res.mixed, t).rearrange("p (h d) -> p h d", h=D_HEADS),
                            uo_ps[:, DIM:2 * DIM].rearrange("p (h d) -> p h d", h=D_HEADS),
                            query_scale[p][:, :].unsqueeze(2).to_broadcast([P, D_HEADS, D_HEAD]),
                            ALU.mult).then_inc(s.o_read, 1)
                        dve.wait_ge(s.o_read, t + 1)
                        nc.vector.tensor_tensor(o_sq[:, :], row(res.mixed, t), row(res.mixed, t), ALU.mult).then_inc(s.out_step, 1)
                        dve.wait_ge(s.out_step, 2 * t + 1)
                        nc.vector.tensor_reduce(row(res.squares, t), o_sq[:, :].rearrange("p (h d) -> p h d", h=D_HEADS),
                                                AX.X, ALU.add).then_inc(s.out_step, 1)

                norm_scales_vector(nc, res, Chain(dve, s.vector_step), s.var, s.std, s.rstd)
                dve.wait_ge(s.weights, 16 * N_LOADS)
                delta_loop(dve, a_step, b_step, tail)
                dve.wait_ge(s.out_step, 2 * TILES)


def delta_loop(eng, a_step, b_step, tail):
    def body(t, p, has_a=True, has_b=True):
        for what in DELTA_ORDER:
            if what[0] == "A":
                if has_a:
                    a_step(t + 2, p, int(what[1:]))
            elif what[0] == "B":
                if has_b:
                    b_step(t + 1, 1 - p, int(what[1:]))
            else:
                tail(t, p, what)

    for n in range(6):
        a_step(0, 0, n)
    for n in range(6):
        a_step(1, 1, n)
    for n in range(3):
        b_step(0, 0, n)
    with eng.Fori(0, TILES // 2 - 1) as i:
        body(2 * i, 0)
        body(2 * i + 1, 1)
    body(TILES - 2, 0, has_a=False)
    body(TILES - 1, 1, has_a=False, has_b=False)


def delta_output(nc, res, a):
    with ExitStack() as ctx:
        st = Stage(nc, ctx, "dout")
        wo, rms_w = st.sb("wo", [P, KC, DIM]), st.sb("rms_w", [P, 1])
        root, scale = st.sb("root", [P, TILES, D_HEADS]), st.sb("scale", [P, TILES, D_HEADS])
        normed = [st.sb(f"normed{i}", [P, PAIR, DIM]) for i in range(2)]
        normedT = [st.sb(f"normedT{i}", [P, PAIR, KC, P]) for i in range(2)]
        turn_ps, out_ps = ([st.ps(f"{n}{i}") for i in range(2)] for n in ("turn", "out"))
        s_w, s_mean, s_root, s_scale = (st.sem(n) for n in ("weights", "mean", "root", "scale"))
        s_normed, s_turn, s_normedT, s_out, s_x, s_stats = (st.sem(n) for n in ("normed", "turn", "normedT", "out", "x", "stats"))
        with nc.Block() as block:
            @block.sync
            def _(sp):
                sp.dma_start(wo[:], a["L0_attn_Wo"].rearrange("(k p) n -> p k n", p=P)).then_inc(s_w, 16)
                sp.dma_start(rms_w[:], a["L0_attn_rms_w"]).then_inc(s_w, 16)
                sp.wait_ge(s_w, 32)

            @block.tensor
            def _(pe):
                def head(u, p):
                    pe.wait_ge(s_normed, u + 1)
                    for j in range(PAIR):
                        for k in range(KC):
                            at = (j * KC + k) * P
                            mm = nc.tensor.transpose(turn_ps[p][:, at:at + P], normed[p][:, j, k * P:(k + 1) * P], res.ident[:])
                    mm.then_inc(s_turn, 1)

                def tail(t, p):
                    pe.wait_ge(s_normedT, t + 1)
                    pe.wait_ge(s_x, t + 1)
                    for j in range(PAIR):
                        for k in range(KC):
                            mm = nc.tensor.matmul(out_ps[p][:, j * DIM:(j + 1) * DIM], normedT[p][:, j, k, :], wo[:, k, :],
                                                  start=k == 0, stop=k == KC - 1)
                    mm.then_inc(s_out, 1)

                pe.wait_ge(s_scale, KC + 1)
                two_at_a_time(pe, head, tail)

            @block.scalar
            def _(act):
                def head(u, p):
                    act.wait_ge(s_turn, u + 1)
                    nc.scalar.activation(normedT[p][:, :, :, :].rearrange("p j k q -> p (j k q)"), turn_ps[p][:, :],
                                         ACT.Copy).then_inc(s_normedT, 1)

                def tail(t, p):
                    pass

                act.wait_ge(s_mean, 1)
                nc.scalar.activation(root[:], scale[:], ACT.Sqrt).then_inc(s_root, 1)
                two_at_a_time(act, head, tail)

            @block.vector
            def _(dve):
                def head(u, p):
                    if not isinstance(u, int) or u > 1:
                        dve.wait_ge(s_out, u - 1)
                    nc.vector.tensor_tensor(
                        normed[p][:, :, :].rearrange("p j (h d) -> p (j h) d", h=D_HEADS),
                        pair_of(res.mixed, u).rearrange("p j (h d) -> p (j h) d", h=D_HEADS),
                        pair_of(scale, u).rearrange("p j h -> p (j h)").unsqueeze(2).to_broadcast([P, PAIR * D_HEADS, D_HEAD]),
                        ALU.mult).then_inc(s_normed, 1)

                def tail(t, p):
                    dve.wait_ge(s_out, t + 1)
                    nc.vector.tensor_tensor(pair_of(res.x, t), pair_of(res.x, t),
                                            out_ps[p][:, :].rearrange("p (j d) -> p j d", j=PAIR), ALU.add).then_inc(s_x, 1)
                    dve.wait_ge(s_x, 2 + t + 1)
                    for j in range(PAIR):
                        nc.vector.bn_stats(pair_rows(res.stats, t, j), pair_rows(res.x, t, j)).then_inc(s_stats, 1)

                dve.sem_inc(s_x, 2)
                nc.vector.tensor_scalar(scale[:], res.squares[:], 1.0 / D_HEAD, LN_EPS, ALU.mult, ALU.add).then_inc(s_mean, 1)
                dve.wait_ge(s_root, 1)
                nc.vector.reciprocal(scale[:], root[:]).then_inc(s_scale, 1)
                dve.wait_ge(s_w, 32)
                for k in range(KC):
                    nc.vector.tensor_scalar(wo[:, k, :], wo[:, k, :], rms_w[:, 0:1], None, ALU.mult).then_inc(s_scale, 1)
                dve.wait_ge(s_scale, KC + 1)
                two_at_a_time(dve, head, tail)
                dve.wait_ge(s_stats, TILES)


EXPERTS, FFN_HEAD = 16, 128
CHUNKS = 4
PER_CHUNK = EXPERTS // CHUNKS
TINY = 1e-12
BELOW_ALL = 1.0e30


def top_two(nc, dve_step, logits, first, second, work, rank, shape):
    peak, best, score = work
    wide = lambda m: m.unsqueeze(2).to_broadcast(shape)
    ranks = rank.unsqueeze(1).to_broadcast(shape)
    source = logits
    for chosen in (first, second):
        dve_step(nc.vector.tensor_reduce(peak, source, AX.X, ALU.max))
        dve_step(nc.vector.tensor_tensor(score, source, wide(peak), ALU.is_equal))
        dve_step(nc.vector.tensor_tensor(score, score, ranks, ALU.mult))
        dve_step(nc.vector.tensor_reduce(best, score, AX.X, ALU.max))
        dve_step(nc.vector.tensor_tensor(chosen, ranks, wide(best), ALU.is_equal))
        if chosen is first:
            dve_step(nc.vector.scalar_tensor_tensor(score, first, -BELOW_ALL, logits, ALU.mult, ALU.add))
            dve_step(nc.vector.tensor_copy(second, score))
            source = second


def switch_router(nc, res, a):
    with ExitStack() as ctx:
        st = Stage(nc, ctx, "router")
        sim, sim_sq = st.sb("sim", [P, KC, EXPERTS]), st.sb("sim_sq", [P, KC, EXPERTS])
        sim_norm, gates, rank = (st.sb(n, [P, EXPERTS]) for n in ("sim_norm", "gates", "rank"))
        row_norm = st.sb("row_norm", [P, TILES])
        xn = [st.sb(f"xn{i}", [P, PAIR, DIM]) for i in range(2)]
        xnT = [st.sb(f"xnT{i}", [P, PAIR, KC, P]) for i in range(2)]
        logits, active, one, two, score, dots = (st.sb(n, [P, TILES, EXPERTS]) for n in
                                                 ("logits", "active", "one", "two", "score", "dots"))
        peak, best, inactive = (st.sb(n, [P, TILES]) for n in ("peak", "best", "inactive"))
        turn_ps = [st.ps(f"turn{i}") for i in range(2)]
        logit_ps = [st.ps(f"logit{i}") for i in range(2)]
        sim_ps = st.ps("simsum")
        s_w, s_var, s_std, s_rstd, s_chain = (st.sem(n) for n in ("weights", "var", "std", "rstd", "vector_step"))
        s_simsq, s_simps, s_normsq, s_norm, s_sim = (st.sem(n) for n in ("simsq", "simps", "normsq", "norm", "sim"))
        s_xn, s_turn, s_xnT, s_logit, s_dots = (st.sem(n) for n in ("xn", "turn", "xnT", "logit", "dots"))
        s_step, s_shift, s_exp = (st.sem(n) for n in ("route_step", "shifted", "exp"))
        with nc.Block() as block:
            @block.sync
            def _(sp):
                sp.dma_start(sim[:], a["L0_ffn_sim_matrix"].rearrange("(k p) e -> p k e", p=P)).then_inc(s_w, 16)
                sp.dma_start(gates[:], a["L0_ffn_gates"].to_broadcast([P, EXPERTS])).then_inc(s_w, 16)
                sp.dma_start(rank[:], a["rank16"].to_broadcast([P, EXPERTS])).then_inc(s_w, 16)
                sp.wait_ge(s_w, 48)

            @block.tensor
            def _(pe):
                def head(u, p):
                    pe.wait_ge(s_xn, u + 1)
                    for j in range(PAIR):
                        for k in range(KC):
                            at = (j * KC + k) * P
                            mm = nc.tensor.transpose(turn_ps[p][:, at:at + P], xn[p][:, j, k * P:(k + 1) * P], res.ident[:])
                    mm.then_inc(s_turn, 1)

                def tail(t, p):
                    pe.wait_ge(s_xnT, t + 1)
                    pe.wait_ge(s_dots, t + 1)
                    for j in range(PAIR):
                        for k in range(KC):
                            mm = nc.tensor.matmul(logit_ps[p][:, j * EXPERTS:(j + 1) * EXPERTS], xnT[p][:, j, k, :], sim[:, k, :],
                                                  start=k == 0, stop=k == KC - 1)
                    mm.then_inc(s_logit, 1)

                pe.wait_ge(s_simsq, 1)
                for k in range(KC):
                    mm = nc.tensor.matmul(sim_ps[:, 0:EXPERTS], res.ones[:], sim_sq[:, k, :], start=k == 0, stop=k == KC - 1)
                mm.then_inc(s_simps, 1)
                pe.wait_ge(s_sim, 2)
                two_at_a_time(pe, head, tail)

            @block.scalar
            def _(act):
                def head(u, p):
                    act.wait_ge(s_turn, u + 1)
                    nc.scalar.activation(xnT[p][:, :, :, :].rearrange("p j k q -> p (j k q)"), turn_ps[p][:, :],
                                         ACT.Copy).then_inc(s_xnT, 1)

                def tail(t, p):
                    pass

                norm_scales_scalar(nc, res, act, s_var, s_std)
                act.wait_ge(s_normsq, 2)
                nc.scalar.activation(sim_norm[:], sim_norm[:], ACT.Sqrt).then_inc(s_norm, 1)
                nc.scalar.activation(row_norm[:], row_norm[:], ACT.Sqrt).then_inc(s_norm, 1)
                two_at_a_time(act, head, tail)
                act.wait_ge(s_w, 48)
                nc.scalar.activation(gates[:], gates[:], ACT.Tanh, scale=0.5).then_inc(s_norm, 1)
                act.wait_ge(s_shift, 1)
                nc.scalar.activation(score[:], score[:], ACT.Exp).then_inc(s_exp, 1)

            @block.vector
            def _(dve):
                def head(u, p):
                    if not isinstance(u, int) or u > 1:
                        dve.wait_ge(s_turn, u - 1)
                    for j in range(PAIR):
                        ins = nc.vector.tensor_scalar(xn[p][:, j, :], pair_rows(res.x, u, j),
                                                      pair_rows(res.mean_var, u, j)[:, 0:1], pair_rows(res.rstd, u, j),
                                                      ALU.subtract, ALU.mult)
                    ins.then_inc(s_xn, 1)

                def tail(t, p):
                    dve.wait_ge(s_logit, t + 1)
                    nc.vector.tensor_copy(pair_of(dots, t), logit_ps[p][:, 0:PAIR * EXPERTS].rearrange("p (j e) -> p j e", j=PAIR)
                                          ).then_inc(s_dots, 1)

                norm_scales_vector(nc, res, Chain(dve, s_chain), s_var, s_std, s_rstd)
                dve.sem_inc(s_dots, 2)
                dve.wait_ge(s_w, 48)
                nc.vector.tensor_tensor(sim_sq[:], sim[:], sim[:], ALU.mult).then_inc(s_simsq, 1)
                dve.wait_ge(s_simps, 1)
                nc.vector.tensor_scalar(sim_norm[:], sim_ps[:, 0:EXPERTS], TINY, None, ALU.add).then_inc(s_normsq, 1)
                step = Chain(dve, s_step)

                def dve_step(ins):
                    step.step(ins)
                    step.settle()

                dve_step(nc.vector.tensor_tensor(row_norm[:], res.rstd[:, :, 0], res.rstd[:, :, 0], ALU.mult))
                dve_step(nc.vector.tensor_tensor(row_norm[:], row_norm[:], res.mean_var[:, :, 1], ALU.mult))
                nc.vector.tensor_scalar(row_norm[:], row_norm[:], float(DIM), TINY, ALU.mult, ALU.add).then_inc(s_normsq, 1)
                dve.wait_ge(s_norm, 2)
                dve_step(nc.vector.reciprocal(sim_norm[:], sim_norm[:]))
                dve_step(nc.vector.reciprocal(row_norm[:], row_norm[:]))
                for k in range(KC):
                    nc.vector.tensor_tensor(sim[:, k, :], sim[:, k, :], sim_norm[:], ALU.mult).then_inc(s_sim, 1)
                two_at_a_time(dve, head, tail)
                dve.wait_ge(s_dots, 2 + PAIRS_OF_TILES)
                shape = [P, TILES, EXPERTS]
                wide = lambda m: m[:, :].unsqueeze(2).to_broadcast(shape)
                dve_step(nc.vector.tensor_tensor(dots[:], dots[:], wide(row_norm), ALU.mult))
                dve.wait_ge(s_norm, 3)
                dve_step(nc.vector.tensor_scalar(gates[:], gates[:], 0.5, 0.5, ALU.mult, ALU.add))
                dve_step(nc.vector.tensor_tensor(logits[:], dots[:], gates[:].unsqueeze(1).to_broadcast(shape), ALU.subtract))
                top_two(nc, dve_step, logits[:], one[:], two[:], (peak[:], best[:], score[:]), rank[:], shape)
                dve_step(nc.vector.tensor_scalar(active[:], logits[:], 0.0, None, ALU.is_gt))
                dve_step(nc.vector.tensor_reduce(peak[:], active[:], AX.X, ALU.max))
                dve_step(nc.vector.tensor_scalar(inactive[:], peak[:], -1.0, 1.0, ALU.mult, ALU.add))
                dve_step(nc.vector.tensor_tensor(one[:], one[:], two[:], ALU.add))
                dve_step(nc.vector.tensor_tensor(one[:], one[:], wide(inactive), ALU.mult))
                dve_step(nc.vector.tensor_tensor(active[:], active[:], one[:], ALU.add))
                dve_step(nc.vector.tensor_scalar(score[:], logits[:], 0.0, None, ALU.max))
                dve_step(nc.vector.tensor_reduce(peak[:], score[:], AX.X, ALU.max))
                nc.vector.tensor_tensor(score[:], score[:], wide(peak), ALU.subtract).then_inc(s_shift, 1)
                dve.wait_ge(s_exp, 1)
                dve_step(nc.vector.tensor_tensor(score[:], score[:], active[:], ALU.mult))
                dve_step(nc.vector.tensor_reduce(best[:], score[:], AX.X, ALU.add))
                dve_step(nc.vector.reciprocal(best[:], best[:]))
                dve_step(nc.vector.tensor_tensor(res.route[:], score[:], wide(best), ALU.mult))


SWITCH_ORDER = ["X", "R0", "R1", "Ta", "R2", "R3", "Tb", "M0", "Tc", "M1", "Td", "M2", "M3", "To"]


def switch_attention(nc, res, a):
    with ExitStack() as ctx:
        st = Stage(nc, ctx, "switch")
        wqkv = st.sb("wqkv", [P, EXPERTS, KC, 3 * FFN_HEAD])
        wo = st.sb("wo", [P, EXPERTS, DIM])
        causal = st.sb("causal", [P, P])
        xn, xnT = st.sb("xn", [P, DIM]), st.sb("xnT", [P, KC, P])
        diag = st.sb("diag", [P, EXPERTS, P])
        spread = [st.sb(f"spread{i}", [P, EXPERTS, P]) for i in range(2)]
        scaled = st.sb("scaled", [P, EXPERTS, KC, P])
        qkv, qkT, masked, probs, probsT = (st.sb("qkv", [P, 3 * FFN_HEAD]), st.sb("qkT", [P, 2 * P]), st.sb("masked", [P, P]),
                                           st.sb("probs", [P, P]), st.sb("probsT", [P, P]))
        negpeak, total, inverse = st.sb("negpeak", [P, 1]), st.sb("total", [P, 1]), st.sb("inverse", [P, 1])
        mixed = st.sb("mixed", [P, EXPERTS, P])
        x_ps, qkv_ps, a_ps, b_ps, out_ps = (st.ps(n) for n in ("x", "qkv", "a", "b", "out"))
        r_ps = [st.ps(f"r{i}") for i in range(2)]
        s_w, s_var, s_std, s_rstd, s_chain = (st.sem(n) for n in ("weights", "var", "std", "rstd", "vector_step"))
        s_xn, s_turn, s_xnT, s_diag = (st.sem(n) for n in ("xn", "turn", "xnT", "diag"))
        s_r, s_spread, s_scaled, s_qkv, s_qkv_sb = (st.sem(n) for n in ("r_full", "spread", "scaled", "qkv_full", "qkv_copied"))
        s_qk, s_qkT, s_score, s_tail, s_peak, s_exp = (st.sem(n) for n in ("qk_turned", "qkT", "score", "tail_step", "peak", "exp"))
        s_probs, s_pt, s_probsT, s_head, s_mixed = (st.sem(n) for n in ("probs", "p_turned", "probsT", "head", "mixed"))
        s_out, s_x, s_stats, s_inverse = st.sem("out"), st.sem("x"), st.sem("stats"), st.sem("inverse")

        def loop(eng, prep, tail):
            def body(t, p, last=False):
                for what in SWITCH_ORDER:
                    if what[0] == "T":
                        tail(t, p, what[1])
                    elif not last:
                        prep(t + 1, 1 - p, what)

            for what in SWITCH_ORDER:
                if what[0] != "T":
                    prep(0, 0, what)
            with eng.Fori(0, TILES // 2 - 1) as i:
                body(2 * i, 0)
                body(2 * i + 1, 1)
            body(TILES - 2, 0)
            body(TILES - 1, 1, last=True)

        with nc.Block() as block:
            @block.sync
            def _(sp):
                sp.dma_start(causal[:], a["causal"]).then_inc(s_w, 16)
                for n, name in enumerate("qkv"):
                    sp.dma_start(wqkv[:, :, :, n * FFN_HEAD:(n + 1) * FFN_HEAD],
                                 a[f"L0_ffn_{name}_proj"].rearrange("e (k p) h -> p (e k) h", p=P)).then_inc(s_w, 16)
                sp.dma_start(wo[:], a["L0_ffn_o_proj"].rearrange("e h c -> h e c")).then_inc(s_w, 16)
                sp.wait_ge(s_w, 80)

            @block.tensor
            def _(pe):
                def prep(u, p, what):
                    if what == "X":
                        pe.wait_ge(s_xn, u + 1)
                        for k in range(KC):
                            mm = nc.tensor.transpose(x_ps[:, k * P:(k + 1) * P], xn[:, k * P:(k + 1) * P], res.ident[:])
                        mm.then_inc(s_turn, 1)
                    elif what[0] == "R":
                        c = int(what[1])
                        if c == 0:
                            pe.wait_ge(s_diag, u + 1)
                        pe.wait_ge(s_spread, CHUNKS * u + c + 1)
                        nc.tensor.matmul(r_ps[c % 2][:, :], res.ones[:],
                                         diag[:, c * PER_CHUNK:(c + 1) * PER_CHUNK, :].rearrange("p e q -> p (e q)"),
                                         start=True, stop=True).then_inc(s_r, 1)
                    else:
                        c = int(what[1])
                        pe.wait_ge(s_scaled, CHUNKS * u + c + 1)
                        if c == 0:
                            pe.wait_ge(s_qkv_sb, u)
                        for e in range(c * PER_CHUNK, (c + 1) * PER_CHUNK):
                            for k in range(KC):
                                mm = nc.tensor.matmul(qkv_ps[:, 0:3 * FFN_HEAD], scaled[:, e, k, :], wqkv[:, e, k, :],
                                                      start=e == 0 and k == 0, stop=e == EXPERTS - 1 and k == KC - 1)
                        mm.then_inc(s_qkv, 1)

                def tail(t, p, what):
                    if what == "a":
                        pe.wait_ge(s_qkv_sb, t + 1)
                        for n in range(2):
                            mm = nc.tensor.transpose(a_ps[:, n * P:(n + 1) * P], qkv[:, n * P:(n + 1) * P], res.ident[:])
                        mm.then_inc(s_qk, 1)
                    elif what == "b":
                        pe.wait_ge(s_qkT, t + 1)
                        nc.tensor.matmul(a_ps[:, 2 * P:3 * P], qkT[:, 0:P], qkT[:, P:2 * P], start=True, stop=True).then_inc(s_score, 1)
                    elif what == "c":
                        pe.wait_ge(s_probs, t + 1)
                        nc.tensor.transpose(b_ps[:, 0:P], probs[:, :], res.ident[:]).then_inc(s_pt, 1)
                    elif what == "d":
                        pe.wait_ge(s_probsT, t + 1)
                        nc.tensor.matmul(b_ps[:, P:2 * P], qkv[:, 2 * P:3 * P], probsT[:, :], start=True, stop=True).then_inc(s_head, 1)
                    else:
                        pe.wait_ge(s_mixed, t + 1)
                        pe.wait_ge(s_x, t)
                        for e in range(EXPERTS):
                            mm = nc.tensor.matmul(out_ps[:, 0:DIM], mixed[:, e, :], wo[:, e, :], start=e == 0, stop=e == EXPERTS - 1)
                        mm.then_inc(s_out, 1)

                pe.wait_ge(s_w, 80)
                loop(pe, prep, tail)

            @block.scalar
            def _(act):
                def prep(u, p, what):
                    if what == "X":
                        act.wait_ge(s_turn, u + 1)
                        act.wait_ge(s_scaled, CHUNKS * u)
                        nc.scalar.activation(xnT[:, :, :].rearrange("p k q -> p (k q)"), x_ps[:, 0:DIM], ACT.Copy).then_inc(s_xnT, 1)
                    elif what[0] == "R":
                        c = int(what[1])
                        act.wait_ge(s_r, CHUNKS * u + c + 1)
                        if c == 0 and (not isinstance(u, int) or u > 1):
                            act.wait_ge(s_mixed, u - 1)
                        nc.scalar.activation(spread[p][:, c * PER_CHUNK:(c + 1) * PER_CHUNK, :].rearrange("p e q -> p (e q)"),
                                             r_ps[c % 2][:, :], ACT.Copy).then_inc(s_spread, 1)
                    elif what == "M3":
                        act.wait_ge(s_qkv, CHUNKS * (u + 1))
                        act.wait_ge(s_head, u)
                        nc.scalar.activation(qkv[:, :], qkv_ps[:, 0:3 * FFN_HEAD], ACT.Copy).then_inc(s_qkv_sb, 1)

                def tail(t, p, what):
                    if what == "a":
                        act.wait_ge(s_qk, t + 1)
                        nc.scalar.activation(qkT[:, :], a_ps[:, 0:2 * P], ACT.Copy).then_inc(s_qkT, 1)
                    elif what == "b":
                        act.wait_ge(s_peak, t + 1)
                        nc.scalar.activation(probs[:, :], masked[:, :], ACT.Exp, bias=negpeak[:, 0:1], scale=FFN_HEAD ** -0.5,
                                             accum_out=total[:, 0:1]).then_inc(s_exp, 1)
                    elif what == "c":
                        act.wait_ge(s_pt, t + 1)
                        nc.scalar.activation(probsT[:, :], b_ps[:, 0:P], ACT.Copy).then_inc(s_probsT, 1)

                norm_scales_scalar(nc, res, act, s_var, s_std)
                loop(act, prep, tail)

            @block.gpsimd
            def _(pool):
                def prep(u, p, what):
                    if what == "X":
                        pool.wait_ge(s_r, CHUNKS * u)
                        nc.gpsimd.tensor_tensor(diag[:, :, :], res.ident[:, :].unsqueeze(1).to_broadcast([P, EXPERTS, P]),
                                                row(res.route, u).unsqueeze(2).to_broadcast([P, EXPERTS, P]),
                                                ALU.mult).then_inc(s_diag, 1)

                def tail(t, p, what):
                    pass

                loop(pool, prep, tail)

            @block.vector
            def _(dve):
                def prep(u, p, what):
                    if what == "X":
                        dve.wait_ge(s_turn, u)
                        normalise(nc, res, xn[:, :], u).then_inc(s_xn, 1)
                    elif what[0] == "R":
                        c = int(what[1])
                        part = slice(c * PER_CHUNK, (c + 1) * PER_CHUNK)
                        if c == 0:
                            dve.wait_ge(s_xnT, u + 1)
                        dve.wait_ge(s_spread, 2 + CHUNKS * u + c + 1)
                        dve.wait_ge(s_qkv, CHUNKS * u)
                        shape = [P, PER_CHUNK, KC, P]
                        nc.vector.tensor_tensor(scaled[:, part, :, :], xnT[:, :, :].unsqueeze(1).to_broadcast(shape),
                                                spread[p][:, part, :].unsqueeze(2).to_broadcast(shape), ALU.mult).then_inc(s_scaled, 1)

                def tail(t, p, what):
                    if what == "b":
                        step = Chain(dve, s_tail, 2 * t)
                        dve.wait_ge(s_score, t + 1)
                        step.step(nc.vector.tensor_tensor(masked[:, :], a_ps[:, 2 * P:3 * P], causal[:, :], ALU.add))
                        step.settle()
                        step.step(nc.vector.tensor_reduce(negpeak[:, :], masked[:, :], AX.X, ALU.max, negate=True))
                        step.settle()
                        nc.vector.tensor_scalar(negpeak[:, :], negpeak[:, :], FFN_HEAD ** -0.5, None, ALU.mult).then_inc(s_peak, 1)
                    elif what == "c":
                        dve.wait_ge(s_exp, t + 1)
                        nc.vector.reciprocal(inverse[:, :], total[:, :]).then_inc(s_inverse, 1)
                        dve.wait_ge(s_inverse, t + 1)
                        nc.vector.tensor_scalar(probs[:, :], probs[:, :], inverse[:, 0:1], None, ALU.mult).then_inc(s_probs, 1)
                    elif what == "d":
                        dve.wait_ge(s_head, t + 1)
                        dve.wait_ge(s_out, t)
                        nc.vector.tensor_tensor(mixed[:, :, :], b_ps[:, P:2 * P].unsqueeze(1).to_broadcast([P, EXPERTS, P]),
                                                spread[p][:, :, :], ALU.mult).then_inc(s_mixed, 1)
                    elif what == "o":
                        dve.wait_ge(s_out, t + 1)
                        nc.vector.tensor_tensor(row(res.x, t), row(res.x, t), out_ps[:, 0:DIM], ALU.add).then_inc(s_x, 1)
                        dve.wait_ge(s_x, t + 1)
                        nc.vector.bn_stats(row(res.stats, t), row(res.x, t)).then_inc(s_stats, 1)

                norm_scales_vector(nc, res, Chain(dve, s_chain), s_var, s_std, s_rstd)
                dve.sem_inc(s_spread, 2)
                dve.wait_ge(s_w, 80)
                loop(dve, prep, tail)
                dve.wait_ge(s_stats, TILES)


def self_attention(nc, res, a):
    with ExitStack() as ctx:
        st = Stage(nc, ctx, "self")
        block_mask = st.sb("block_mask", [P, P])
        xn = [st.sb(f"xn{i}", [P, PAIR, DIM]) for i in range(2)]
        xnT = [st.sb(f"xnT{i}", [P, PAIR, KC, P]) for i in range(2)]
        masked = [st.sb(f"masked{i}", [P, PAIR, P]) for i in range(2)]
        probs = [st.sb(f"probs{i}", [P, PAIR, P]) for i in range(2)]
        negpeak, total, inverse = (st.sb(n, [P, PAIR]) for n in ("negpeak", "total", "inverse"))
        turn_ps, score_ps, out_ps = ([st.ps(f"{n}{i}") for i in range(2)] for n in ("turn", "score", "out"))
        s_mask, s_var, s_std, s_rstd, s_chain = (st.sem(n) for n in ("mask", "var", "std", "rstd", "vector_step"))
        s_xn, s_turn, s_xnT, s_score, s_tail = (st.sem(n) for n in ("xn", "turned", "xnT", "scores", "tail_step"))
        s_peak, s_exp, s_probs, s_out, s_x, s_stats = (st.sem(n) for n in ("peak", "exp", "probs", "out", "x", "stats"))
        with nc.Block() as block:
            @block.sync
            def _(sp):
                sp.dma_start(block_mask[:], a["block_mask"]).then_inc(s_mask, 16)
                sp.wait_ge(s_mask, 16)

            @block.tensor
            def _(pe):
                def head(u, p):
                    pe.wait_ge(s_xn, u + 1)
                    for j in range(PAIR):
                        for k in range(KC):
                            at = (j * KC + k) * P
                            mm = nc.tensor.transpose(turn_ps[p][:, at:at + P], xn[p][:, j, k * P:(k + 1) * P], res.ident[:])
                    mm.then_inc(s_turn, 1)
                    pe.wait_ge(s_xnT, u + 1)
                    for j in range(PAIR):
                        for k in range(KC):
                            mm = nc.tensor.matmul(score_ps[p][:, j * P:(j + 1) * P], xnT[p][:, j, k, :], xnT[p][:, j, k, :],
                                                  start=k == 0, stop=k == KC - 1)
                    mm.then_inc(s_score, 1)

                def tail(t, p):
                    pe.wait_ge(s_probs, t + 1)
                    for j in range(PAIR):
                        mm = nc.tensor.matmul(out_ps[p][:, j * DIM:(j + 1) * DIM], probs[p][:, j, :], xn[p][:, j, :],
                                              start=True, stop=True)
                    mm.then_inc(s_out, 1)

                two_at_a_time(pe, head, tail)

            @block.scalar
            def _(act):
                def head(u, p):
                    act.wait_ge(s_turn, u + 1)
                    nc.scalar.activation(xnT[p][:, :, :, :].rearrange("p j k q -> p (j k q)"), turn_ps[p][:, :],
                                         ACT.Copy).then_inc(s_xnT, 1)

                def tail(t, p):
                    act.wait_ge(s_peak, t + 1)
                    for j in range(PAIR):
                        ins = nc.scalar.activation(probs[p][:, j, :], masked[p][:, j, :], ACT.Exp,
                                                   bias=negpeak[:, j:j + 1], accum_out=total[:, j:j + 1])
                    ins.then_inc(s_exp, 1)

                norm_scales_scalar(nc, res, act, s_var, s_std)
                two_at_a_time(act, head, tail)

            @block.vector
            def _(dve):
                def head(u, p):
                    if not isinstance(u, int) or u >= 2:
                        dve.wait_ge(s_x, u - 1)
                    for j in range(PAIR):
                        ins = nc.vector.tensor_scalar(xn[p][:, j, :], pair_rows(res.x, u, j),
                                                      pair_rows(res.mean_var, u, j)[:, 0:1], pair_rows(res.rstd, u, j),
                                                      ALU.subtract, ALU.mult)
                    ins.then_inc(s_xn, 1)

                def tail(t, p):
                    chain = Chain(dve, s_tail, 2 * t)
                    dve.wait_ge(s_score, t + 1)
                    chain.step(nc.vector.tensor_tensor(
                        masked[p][:, :, :], score_ps[p][:, 0:PAIR * P].rearrange("p (j q) -> p j q", j=PAIR),
                        block_mask[:, :].unsqueeze(1).to_broadcast([P, PAIR, P]), ALU.add))
                    chain.settle()
                    nc.vector.tensor_reduce(negpeak[:, :], masked[p][:, :, :], AX.X, ALU.max, negate=True).then_inc(s_peak, 1)
                    dve.wait_ge(s_exp, t + 1)
                    chain.step(nc.vector.reciprocal(inverse[:, :], total[:, :]))
                    chain.settle()
                    nc.vector.tensor_tensor(probs[p][:, :, :], probs[p][:, :, :],
                                            inverse[:, :].unsqueeze(2).to_broadcast([P, PAIR, P]),
                                            ALU.mult).then_inc(s_probs, 1)
                    dve.wait_ge(s_out, t + 1)
                    nc.vector.tensor_tensor(pair_of(res.x, t), pair_of(res.x, t),
                                            out_ps[p][:, :].rearrange("p (j d) -> p j d", j=PAIR), ALU.add).then_inc(s_x, 1)
                    dve.wait_ge(s_x, t + 1)
                    for j in range(PAIR):
                        nc.vector.bn_stats(pair_rows(res.stats, t, j), pair_rows(res.x, t, j)).then_inc(s_stats, 1)

                norm_scales_vector(nc, res, Chain(dve, s_chain), s_var, s_std, s_rstd)
                dve.wait_ge(s_mask, 16)
                two_at_a_time(dve, head, tail)
                dve.wait_ge(s_stats, TILES)


MOE, HIDDEN, CHOSEN = 8, 1024, 2
FC = HIDDEN // P
ROW_TILES = -(-((CHOSEN * TOKENS + MOE * (P - 1)) // P) // 2) * 2
ROWS = ROW_TILES * P


def scan(nc, dve_step, a, b, n, at):
    step = 1
    while step < n:
        dve_step(nc.vector.tensor_copy(at(b, slice(0, step)), at(a, slice(0, step))))
        dve_step(nc.vector.tensor_tensor(at(b, slice(step, n)), at(a, slice(step, n)), at(a, slice(0, n - step)), ALU.add))
        a, b, step = b, a, 2 * step
    return a


def moe_router(nc, res, a, rows):
    with ExitStack() as ctx:
        st = Stage(nc, ctx, "gate")
        gate, rank = st.sb("gate", [P, KC, MOE]), st.sb("rank", [P, MOE])
        before, tile_row = st.sb("before", [P, P]), st.sb("tile_row", [P, ROW_TILES])
        zeros = st.sb("zeros", [P, DIM])
        xn = [st.sb(f"xn{i}", [P, PAIR, DIM]) for i in range(2)]
        xnT = [st.sb(f"xnT{i}", [P, PAIR, KC, P]) for i in range(2)]
        xn_all = st.sb("xn_all", [P, TILES, DIM])
        probs, one, two, score, both, count, count2, place = (
            st.sb(n, [P, TILES, MOE]) for n in ("probs", "one", "two", "score", "both", "count", "count2", "place"))
        peak, best = st.sb("peak", [P, TILES]), st.sb("best", [P, TILES])
        padded, ends, ends2, starts = (st.sb(n, [P, MOE]) for n in ("padded", "ends", "ends2", "starts"))
        padded_int = st.sb("padded_int", [P, MOE], I32)
        started, owner = st.sb("started", [P, ROW_TILES, MOE - 1]), st.sb("owner", [P, ROW_TILES])
        slot = st.sb("slot", [P, TILES])
        turn_ps = [st.ps(f"turn{i}") for i in range(2)]
        logit_ps = [st.ps(f"logit{i}") for i in range(2)]
        before_ps, all_ps = st.ps("before"), st.ps("all")
        s_w, s_var, s_std, s_rstd, s_chain = (st.sem(n) for n in ("weights", "var", "std", "rstd", "vector_step"))
        s_xn, s_turn, s_xnT, s_logit, s_dots = (st.sem(n) for n in ("xn", "turn", "xnT", "logit", "dots"))
        s_step, s_shift, s_exp, s_both, s_counts = (st.sem(n) for n in ("route_step", "shifted", "exp", "both", "counts"))
        s_zero, s_zeroed, s_slots, s_scattered = (st.sem(n) for n in ("zero", "zeroed", "slots", "scattered"))
        with nc.Block() as block:
            @block.sync
            def _(sp):
                sp.dma_start(gate[:], a["L1_ffn_gate_w"].rearrange("(k p) e -> p k e", p=P)).then_inc(s_w, 16)
                sp.dma_start(rank[:], a["rank8"].to_broadcast([P, MOE])).then_inc(s_w, 16)
                sp.dma_start(before[:], a["before"]).then_inc(s_w, 16)
                sp.dma_start(tile_row[:], a["tile_row"].to_broadcast([P, ROW_TILES])).then_inc(s_w, 16)
                sp.wait_ge(s_zero, 1)
                sp.dma_start(rows.rearrange("(t p) d -> p t d", p=P),
                             zeros[:, :].unsqueeze(1).to_broadcast([P, ROW_TILES, DIM])).then_inc(s_zeroed, 16)
                sp.wait_ge(s_w, 64)
                sp.wait_ge(s_zeroed, 16)

            @block.tensor
            def _(pe):
                def head(u, p):
                    pe.wait_ge(s_xn, u + 1)
                    for j in range(PAIR):
                        for k in range(KC):
                            at = (j * KC + k) * P
                            mm = nc.tensor.transpose(turn_ps[p][:, at:at + P], xn[p][:, j, k * P:(k + 1) * P], res.ident[:])
                    mm.then_inc(s_turn, 1)

                def tail(t, p):
                    pe.wait_ge(s_xnT, t + 1)
                    pe.wait_ge(s_dots, t + 1)
                    for j in range(PAIR):
                        for k in range(KC):
                            mm = nc.tensor.matmul(logit_ps[p][:, j * MOE:(j + 1) * MOE], xnT[p][:, j, k, :], gate[:, k, :],
                                                  start=k == 0, stop=k == KC - 1)
                    mm.then_inc(s_logit, 1)

                pe.wait_ge(s_w, 64)
                two_at_a_time(pe, head, tail)
                pe.wait_ge(s_both, 1)
                chosen = both[:, :, :].rearrange("p t e -> p (t e)")
                nc.tensor.matmul(before_ps[:, 0:P], before[:], chosen, start=True, stop=True)
                nc.tensor.matmul(all_ps[:, 0:P], res.ones[:], chosen, start=True, stop=True).then_inc(s_counts, 1)

            @block.scalar
            def _(act):
                def head(u, p):
                    act.wait_ge(s_turn, u + 1)
                    nc.scalar.activation(xnT[p][:, :, :, :].rearrange("p j k q -> p (j k q)"), turn_ps[p][:, :],
                                         ACT.Copy).then_inc(s_xnT, 1)

                def tail(t, p):
                    pass

                norm_scales_scalar(nc, res, act, s_var, s_std)
                two_at_a_time(act, head, tail)
                act.wait_ge(s_shift, 1)
                nc.scalar.activation(probs[:], probs[:], ACT.Exp).then_inc(s_exp, 1)

            @block.gpsimd
            def _(pool):
                pool.wait_ge(s_zeroed, 16)
                pool.wait_ge(s_slots, CHOSEN)
                for t in range(TILES):
                    for n in range(CHOSEN):
                        pool.indirect_dma_start(rows, bass.IndirectOffsetOnAxis(res.slots[:, n, t:t + 1], 0), xn_all[:, t, :],
                                                None).then_inc(s_scattered, 16)
                pool.wait_ge(s_scattered, 16 * CHOSEN * TILES)

            @block.vector
            def _(dve):
                def head(u, p):
                    if not isinstance(u, int) or u > 1:
                        dve.wait_ge(s_turn, u - 1)
                    for j in range(PAIR):
                        ins = nc.vector.tensor_scalar(xn[p][:, j, :], pair_rows(res.x, u, j),
                                                      pair_rows(res.mean_var, u, j)[:, 0:1], pair_rows(res.rstd, u, j),
                                                      ALU.subtract, ALU.mult)
                    ins.then_inc(s_xn, 1)
                    dve.wait_ge(s_xn, u + 1)
                    nc.vector.tensor_copy(pair_of(xn_all, u), xn[p][:, :, :])

                def tail(t, p):
                    dve.wait_ge(s_logit, t + 1)
                    nc.vector.tensor_copy(pair_of(probs, t), logit_ps[p][:, 0:PAIR * MOE].rearrange("p (j e) -> p j e", j=PAIR)
                                          ).then_inc(s_dots, 1)

                nc.vector.memset(zeros[:], 0.0).then_inc(s_zero, 1)
                norm_scales_vector(nc, res, Chain(dve, s_chain), s_var, s_std, s_rstd)
                dve.sem_inc(s_dots, 2)
                dve.wait_ge(s_w, 64)
                two_at_a_time(dve, head, tail)
                dve.wait_ge(s_dots, 2 + PAIRS_OF_TILES)
                step = Chain(dve, s_step)

                def dve_step(ins):
                    step.step(ins)
                    step.settle()

                shape = [P, TILES, MOE]
                wide = lambda m: m[:, :].unsqueeze(2).to_broadcast(shape)
                dve_step(nc.vector.tensor_reduce(peak[:], probs[:], AX.X, ALU.max))
                nc.vector.tensor_tensor(probs[:], probs[:], wide(peak), ALU.subtract).then_inc(s_shift, 1)
                dve.wait_ge(s_exp, 1)
                dve_step(nc.vector.tensor_reduce(best[:], probs[:], AX.X, ALU.add))
                dve_step(nc.vector.reciprocal(best[:], best[:]))
                dve_step(nc.vector.tensor_tensor(probs[:], probs[:], wide(best), ALU.mult))
                top_two(nc, dve_step, probs[:], one[:], two[:], (peak[:], best[:], score[:]), rank[:], shape)
                nc.vector.tensor_tensor(both[:], one[:], two[:], ALU.add).then_inc(s_both, 1)
                for n, chosen in enumerate((one, two)):
                    dve_step(nc.vector.tensor_tensor(score[:], probs[:], chosen[:], ALU.mult))
                    dve_step(nc.vector.tensor_reduce(res.weight[:, n, :], score[:], AX.X, ALU.add))
                dve_step(nc.vector.tensor_tensor(peak[:], res.weight[:, 0, :], res.weight[:, 1, :], ALU.add))
                dve_step(nc.vector.reciprocal(peak[:], peak[:]))
                for n in range(CHOSEN):
                    dve_step(nc.vector.tensor_tensor(res.weight[:, n, :], res.weight[:, n, :], peak[:], ALU.mult))
                dve.wait_ge(s_counts, 1)
                dve_step(nc.vector.tensor_copy(count[:].rearrange("p t e -> p (t e)"), all_ps[:, 0:P]))
                upto = scan(nc, dve_step, count, count2, TILES, lambda m, s: m[:, s, :])
                dve_step(nc.vector.tensor_scalar(padded_int[:], upto[:, TILES - 1, :], float(P - 1), None, ALU.add))
                shift = P.bit_length() - 1
                dve_step(nc.vector.tensor_scalar(padded_int[:], padded_int[:], shift, shift,
                                                 ALU.logical_shift_right, ALU.logical_shift_left))
                dve_step(nc.vector.tensor_copy(padded[:], padded_int[:]))
                dve_step(nc.vector.tensor_copy(ends[:], padded[:]))
                end = scan(nc, dve_step, ends, ends2, MOE, lambda m, s: m[:, s])
                dve_step(nc.vector.tensor_tensor(starts[:], end[:], padded[:], ALU.subtract))
                dve_step(nc.vector.tensor_tensor(place[:], upto[:], starts[:].unsqueeze(1).to_broadcast(shape), ALU.add))
                dve_step(nc.vector.tensor_tensor(place[:].rearrange("p t e -> p (t e)"), place[:].rearrange("p t e -> p (t e)"),
                                                 all_ps[:, 0:P], ALU.subtract))
                dve_step(nc.vector.tensor_tensor(place[:].rearrange("p t e -> p (t e)"), place[:].rearrange("p t e -> p (t e)"),
                                                 before_ps[:, 0:P], ALU.add))
                for n, chosen in enumerate((one, two)):
                    dve_step(nc.vector.tensor_tensor(score[:], place[:], chosen[:], ALU.mult))
                    dve_step(nc.vector.tensor_reduce(slot[:], score[:], AX.X, ALU.add))
                    nc.vector.tensor_copy(res.slots[:, n, :], slot[:]).then_inc(s_slots, 1)
                    dve.wait_ge(s_slots, n + 1)
                dve_step(nc.vector.tensor_tensor(started[:], starts[:, 1:].unsqueeze(1).to_broadcast([P, ROW_TILES, MOE - 1]),
                                                 tile_row[:].unsqueeze(2).to_broadcast([P, ROW_TILES, MOE - 1]), ALU.is_le))
                dve_step(nc.vector.tensor_reduce(owner[:], started[:], AX.X, ALU.add))
                dve_step(nc.vector.tensor_copy(res.owner[:], owner[:]))


MOE_ORDER = ["X1", "G0", "H1", "Y0"]


def moe_experts(nc, res, rows, outs):
    with ExitStack() as ctx:
        st = Stage(nc, ctx, "moe")
        xs = [st.sb(f"xs{i}", [P, DIM]) for i in range(2)]
        y = [st.sb(f"y{i}", [P, DIM]) for i in range(2)]
        xsT, hidden, hiddenT = st.sb("xsT", [P, KC, P]), st.sb("hidden", [P, HIDDEN]), st.sb("hiddenT", [P, FC, P])
        x_ps, y_ps = st.ps("x"), st.ps("y")
        h_ps, g_ps = ([st.ps(f"{n}{i}") for i in range(2)] for n in ("h", "g"))
        s_turn, s_xsT, s_h, s_hidden = (st.sem(n) for n in ("turn", "xsT", "h", "hidden"))
        s_g, s_hiddenT, s_y, s_y_sb = (st.sem(n) for n in ("g", "hiddenT", "y", "y_sb"))
        s_xs, s_stored = ([st.sem(f"{n}{i}") for i in range(2)] for n in ("xs", "stored"))

        def loop(eng, step):
            def body(j, p, last=False):
                for what in MOE_ORDER:
                    ahead = int(what[1])
                    if not (ahead and last):
                        step(j + ahead, (p + ahead) % 2, what[0])

            for what in MOE_ORDER:
                if what[1] == "1":
                    step(0, 0, what[0])
            with eng.Fori(0, ROW_TILES // 2 - 1) as i:
                body(2 * i, 0)
                body(2 * i + 1, 1)
            body(ROW_TILES - 2, 0)
            body(ROW_TILES - 1, 1, last=True)

        with nc.Block() as block:
            @block.sync
            def _(sp):
                source = rows.rearrange("(t p) d -> t p d", p=P)
                target = outs.rearrange("(t p) d -> t p d", p=P)

                def one_tile(m, j):
                    return m[j] if isinstance(j, int) else m[bass.ds(j, 1)].rearrange("a p d -> (a p) d")

                def load(j, p):
                    sp.dma_start(xs[p][:, :], one_tile(source, j)).then_inc(s_xs[p], 16)

                def store(j, p):
                    sp.dma_start(one_tile(target, j), y[p][:, :]).then_inc(s_stored[p], 16)

                for j in range(2):
                    load(j, j)
                with sp.Fori(0, ROW_TILES // 2 - 1) as i:
                    for p in range(2):
                        j = 2 * i + p
                        ahead, now, done = sp.snap(j + 2), sp.snap(j), sp.snap(j + 1)
                        sp.wait_ge(s_turn, done)
                        load(ahead, p)
                        sp.wait_ge(s_y_sb, done)
                        store(now, p)
                for j in (ROW_TILES - 2, ROW_TILES - 1):
                    sp.wait_ge(s_y_sb, j + 1)
                    store(j, j % 2)
                for p in range(2):
                    sp.wait_ge(s_stored[p], 16 * (ROW_TILES // 2))

            @block.tensor
            def _(pe):
                def step(j, p, what):
                    if what == "X":
                        pe.wait_ge(s_xs[p], 16 * (j // 2 + 1) if isinstance(j, int) else 8 * (j - p) + 16)
                        for k in range(KC):
                            mm = nc.tensor.transpose(x_ps[:, k * P:(k + 1) * P], xs[p][:, k * P:(k + 1) * P], res.ident[:])
                        mm.then_inc(s_turn, 1)
                    elif what == "H":
                        e = expert(j)
                        pe.wait_ge(s_xsT, j + 1)
                        for n in range(2):
                            pe.wait_ge(s_hidden, 2 * j + n)
                            for k in range(KC):
                                mm = nc.tensor.matmul(h_ps[n][:, :], xsT[:, k, :],
                                                      res.w1[:, bass.ds(e * KC + k, 1), n * 512:(n + 1) * 512].rearrange("p a f -> p (a f)"),
                                                      start=k == 0, stop=k == KC - 1)
                            mm.then_inc(s_h, 1)
                    elif what == "G":
                        for n in range(2):
                            pe.wait_ge(s_hidden, 2 * j + n + 1)
                            pe.wait_ge(s_hiddenT, 2 * j)
                            for f in range(4):
                                at = n * 4 + f
                                mm = nc.tensor.transpose(g_ps[n][:, f * P:(f + 1) * P], hidden[:, at * P:(at + 1) * P], res.ident[:])
                            mm.then_inc(s_g, 1)
                    else:
                        e = expert(j)
                        pe.wait_ge(s_hiddenT, 2 * (j + 1))
                        pe.wait_ge(s_y_sb, j)
                        for f in range(FC):
                            mm = nc.tensor.matmul(y_ps[:, 0:DIM], hiddenT[:, f, :],
                                                  res.w2[:, bass.ds(e * FC + f, 1), :].rearrange("p a d -> p (a d)"),
                                                  start=f == 0, stop=f == FC - 1)
                        mm.then_inc(s_y, 1)

                def expert(j):
                    at = res.owner[0:1, j:j + 1] if isinstance(j, int) else res.owner[0:1, bass.ds(j, 1)]
                    return pe.value_load(at, min_val=0, max_val=MOE - 1)

                pe.wait_ge(res.moe_loaded, 32)
                loop(pe, step)

            @block.scalar
            def _(act):
                def step(j, p, what):
                    if what == "X":
                        act.wait_ge(s_turn, j + 1)
                        nc.scalar.activation(xsT[:, :, :].rearrange("p k q -> p (k q)"), x_ps[:, 0:DIM], ACT.Copy).then_inc(s_xsT, 1)
                    elif what == "H":
                        for n in range(2):
                            act.wait_ge(s_h, 2 * j + n + 1)
                            act.wait_ge(s_g, 2 * j)
                            nc.scalar.activation(hidden[:, n * 512:(n + 1) * 512], h_ps[n][:, :],
                                                 ACT.Gelu_apprx_tanh).then_inc(s_hidden, 1)

                loop(act, step)

            @block.vector
            def _(dve):
                def step(j, p, what):
                    if what == "G":
                        for n in range(2):
                            dve.wait_ge(s_g, 2 * j + n + 1)
                            dve.wait_ge(s_y, j)
                            nc.vector.tensor_copy(hiddenT[:, n * 4:(n + 1) * 4, :].rearrange("p f q -> p (f q)"),
                                                  g_ps[n][:, :]).then_inc(s_hiddenT, 1)
                    elif what == "Y":
                        dve.wait_ge(s_y, j + 1)
                        dve.wait_ge(s_stored[p], 16 * (j // 2) if isinstance(j, int) else 8 * (j - p))
                        nc.vector.tensor_copy(y[p][:, :], y_ps[:, 0:DIM]).then_inc(s_y_sb, 1)

                loop(dve, step)


def moe_combine(nc, res, outs, out):
    with ExitStack() as ctx:
        st = Stage(nc, ctx, "mix")
        DEEP = 4
        got = [[st.sb(f"got{i}{n}", [P, DIM]) for n in range(CHOSEN)] for i in range(DEEP)]
        s_got = [st.sem(f"got{i}") for i in range(DEEP)]
        s_first, s_mixed, s_out = st.sem("first"), st.sem("mixed"), st.sem("out")
        with nc.Block() as block:
            @block.gpsimd
            def _(pool):
                for t in range(TILES):
                    if t >= DEEP:
                        pool.wait_ge(s_mixed, t - DEEP + 1)
                    for n in range(CHOSEN):
                        pool.indirect_dma_start(got[t % DEEP][n][:, :], None, outs,
                                                bass.IndirectOffsetOnAxis(res.slots[:, n, t:t + 1], 0)).then_inc(s_got[t % DEEP], 16)

            @block.vector
            def _(dve):
                for t in range(TILES):
                    dve.wait_ge(s_got[t % DEEP], 16 * CHOSEN * (t // DEEP + 1))
                    nc.vector.scalar_tensor_tensor(res.x[:, t, :], got[t % DEEP][0][:, :], res.weight[:, 0, t:t + 1],
                                                   res.x[:, t, :], ALU.mult, ALU.add).then_inc(s_first, 1)
                    dve.wait_ge(s_first, t + 1)
                    nc.vector.scalar_tensor_tensor(res.x[:, t, :], got[t % DEEP][1][:, :], res.weight[:, 1, t:t + 1],
                                                   res.x[:, t, :], ALU.mult, ALU.add).then_inc(s_mixed, 1)

            @block.sync
            def _(sp):
                target = out.rearrange("(t p) d -> p t d", p=P)
                for t in range(0, TILES, 4):
                    sp.wait_ge(s_mixed, t + 4)
                    sp.dma_start(target[:, t:t + 4, :], res.x[:, t:t + 4, :]).then_inc(s_out, 16)
                sp.wait_ge(s_out, 16 * (TILES // 4))


def load_experts(sp, res, a, which):
    if which == 0:
        sp.dma_start(res.w1[:], a["L1_ffn_w1"].rearrange("e (k p) f -> p (e k) f", p=P)).then_inc(res.moe_loaded, 16)
    else:
        sp.dma_start(res.w2[:], a["L1_ffn_w2"].rearrange("e (k p) d -> p (e k) d", p=P)).then_inc(res.moe_loaded, 16)


def store_residual(nc, res, out):
    with ExitStack() as ctx:
        st = Stage(nc, ctx, "store")
        s_out = st.sem("out")
        with nc.Block() as block:
            @block.sync
            def _(sp):
                sp.dma_start(out.rearrange("(t p) d -> p t d", p=P), res.x[:]).then_inc(s_out, 16)
                sp.wait_ge(s_out, 16)


def perceiver(nc, a, out, stages=("x0", "d", "s", "x1", "e", "f")):
    with ExitStack() as ctx:
        st = Stage(nc, ctx, "res")
        res = Resident()
        res.x = st.sb("x", [P, TILES, DIM])
        res.stats = st.sb("stats", [P, TILES, 6])
        res.mean_var = st.sb("mean_var", [P, TILES, 2])
        res.std, res.rstd = st.sb("std", [P, TILES]), st.sb("rstd", [P, TILES, 1])
        res.ident, res.ones = st.sb("ident", [P, P]), st.sb("ones", [P, P])
        load_residual(nc, res, a["x"], a)
        for stage in stages:
            if stage in ("x0", "x1"):
                w = {n: a[f"L{stage[1]}_xattn_{n}"] for n in ("Wq", "Wk", "Wv", "Wo", "bq", "bk", "bv", "bo")}
                w["headmask"], w["parmask"] = a["headmask"], a["parmask"]
                cross_attention(nc, res, stage, a["ctx"], w, a["mask"] if stage == "x0" else None)
            elif stage == "d":
                with ExitStack() as inner:
                    held = Stage(nc, inner, "held")
                    res.mixed, res.squares = held.sb("mixed", [P, TILES, DIM]), held.sb("squares", [P, TILES, D_HEADS])
                    delta_rule(nc, res, a)
                    delta_output(nc, res, a)
            elif stage == "s":
                with ExitStack() as inner:
                    res.route = Stage(nc, inner, "held").sb("route", [P, TILES, EXPERTS])
                    switch_router(nc, res, a)
                    switch_attention(nc, res, a)
            elif stage == "e":
                self_attention(nc, res, a)
            elif stage == "f":
                held = Stage(nc, ctx, "moe_held")
                res.w1, res.w2 = held.sb("w1", [P, MOE * KC, HIDDEN]), held.sb("w2", [P, MOE * FC, DIM])
                res.moe_loaded = held.sem("moe_loaded")
                res.slots, res.weight = held.sb("slots", [P, CHOSEN, TILES], U32), held.sb("weight", [P, CHOSEN, TILES])
                res.owner = held.sb("owner", [P, ROW_TILES], I32)
                rows = nc.dram_tensor("rows", (ROWS, DIM), F32, kind="Internal").ap()
                outs = nc.dram_tensor("outs", (ROWS, DIM), F32, kind="Internal").ap()
                with nc.Block() as block:
                    @block.sync
                    def _(sp):
                        load_experts(sp, res, a, 0)
                        load_experts(sp, res, a, 1)
                moe_router(nc, res, a, rows)
                moe_experts(nc, res, rows, outs)
                moe_combine(nc, res, outs, out)
        if "f" not in stages:
            store_residual(nc, res, out)


def constants():
    import numpy as np
    c = np.arange(P)
    head = (c[:, None] // HEAD == np.arange(HALF_HEADS)[None, :]) * HEAD ** -0.5
    par = (c[:, None] // HEAD) % 2 == np.arange(2)[None, :]
    batch = c // SEQ
    block_mask = np.where(batch[:, None] == batch[None, :], 0.0, LOWEST)
    row_, col = c[:, None], c[None, :]
    same = batch[:, None] == batch[None, :]

    def join(size):
        return (row_ // (2 * size) == col // (2 * size)) & (row_ // size % 2 == 1) & (col // size % 2 == 0)

    causal = np.where(same & (row_ >= col), 0.0, LOWEST)
    delta = {"before": row_ < col, "rank8": np.arange(MOE, 0, -1)[None, :], "tile_row": P * np.arange(ROW_TILES)[None, :],
             "causal": causal, "rank16": np.arange(EXPERTS, 0, -1)[None, :], "head_ones": c[:, None] // D_HEAD == np.arange(2)[None, :], "strict": same & (row_ > col),
             "causalT": same & (row_ <= col), "join1": join(1), "join1T": join(1).T,
             "joinT": np.stack([join(n).T for n in LEVELS], axis=1)}
    return {k: v.astype(np.float32) for k, v in delta.items()} | {"block_mask": block_mask.astype(np.float32), "ident": np.eye(P, dtype=np.float32), "headmask": head.astype(np.float32), "parmask": par.astype(np.float32)}


def laid_out(inputs):
    import numpy as np
    a = {k: np.ascontiguousarray(v) for k, v in inputs.items()}
    out = {"x": a["x"].reshape(TOKENS, DIM), "ctx": a["ctx_1024"].reshape(BATCH * KEYS, DIM),
           "mask": a["mask_1x1xSxS2_ik0"].reshape(SEQ, KEYS)}
    for layer in range(2):
        pre = f"L{layer}_xattn_"
        for n in ("Wq", "Wk", "Wv", "Wo"):
            out[pre + n] = a[pre + n].T if layer == 0 else a[pre + n]
        for n in ("bq", "bk", "bv"):
            out[pre + n] = a[pre + n].reshape(KC, P).T
        out[pre + "bo"] = a[pre + "bo"].reshape(1, DIM)
    for n in ("Wq", "Wk", "Wv", "Wb", "Wo"):
        out["L0_attn_" + n] = a["L0_attn_" + n]
    for n in ("q_proj", "k_proj", "v_proj", "o_proj", "sim_matrix"):
        out["L0_ffn_" + n] = a["L0_ffn_" + n]
    for n in ("gate_w", "w1", "w2"):
        out["L1_ffn_" + n] = a["L1_ffn_" + n]
    out["L0_ffn_gates"] = a["L0_ffn_gates"].reshape(1, EXPERTS)
    out["L0_attn_taps"] = np.concatenate([a[f"L0_attn_conv_{n}_w"].reshape(KC, P, TAPS) for n in "qkv"]).transpose(1, 0, 2)
    out["L0_attn_rms_w"] = np.tile(a["L0_attn_rms_w"], P // D_HEAD).reshape(P, 1)
    out.update(constants())
    return {k: np.ascontiguousarray(v) for k, v in out.items()}


def kernel(**inputs):
    import concourse.bacc as bacc
    from concourse.bass_utils import run_bass_kernel_spmd

    nc = bacc.Bacc("TRN2", target_bir_lowering=False, num_devices=1)
    arrays = {f"in_{k}": v for k, v in laid_out(inputs).items()}
    aps = {k[3:]: nc.dram_tensor(k, v.shape, mybir.dt.from_np(v.dtype), kind="ExternalInput").ap()
           for k, v in arrays.items()}
    out = nc.dram_tensor("out", (TOKENS, DIM), F32, kind="ExternalOutput").ap()
    perceiver(nc, aps, out)
    r = run_bass_kernel_spmd(nc, [arrays], core_ids=[0])
    return r.results[0]["out"].reshape(BATCH, SEQ, DIM)
```

```python
from contextlib import ExitStack

import concourse.bass as bass
from concourse import mybir

F32 = mybir.dt.float32
I32 = mybir.dt.int32
U32 = mybir.dt.uint32
ACT = mybir.ActivationFunctionType
ALU = mybir.AluOpType
AX = mybir.AxisListType

P = 128
BATCH, SEQ, DIM = 32, 64, 256
KEYS = 256
TOKENS = BATCH * SEQ
TILES = TOKENS // P
BPT = P // SEQ
KC = DIM // P
LN_EPS = 1e-5


class Resident:
    pass


class Stage:

    def __init__(self, nc, ctx, tag):
        self.nc, self.ctx, self.tag, self.sems = nc, ctx, tag, []
        ctx.callback(self.clear)

    def clear(self):
        if self.sems:
            self.nc.clear_and_free_semaphores(self.sems)
            self.nc.all_engine_barrier()

    def sb(self, name, shape, dt=F32):
        return self.ctx.enter_context(self.nc.sbuf_tensor(f"{self.tag}_{name}", shape, dt))

    def ps(self, name, shape=(P, 512)):
        return self.ctx.enter_context(self.nc.psum_tensor(f"{self.tag}_{name}_ps", list(shape), F32))

    def sem(self, name):
        self.sems.append(self.nc.alloc_semaphore(f"{self.tag}_{name}"))
        return self.sems[-1]


class Chain:

    def __init__(self, eng, sem, base=0):
        self.eng, self.sem, self.base, self.n = eng, sem, base, 0

    def step(self, ins):
        self.n += 1
        ins.then_inc(self.sem, 1)

    def settle(self):
        self.eng.wait_ge(self.sem, self.base + self.n)


def row(tensor, t):
    if isinstance(t, int):
        return tensor[:, t, :]
    return tensor[:, bass.ds(t, 1), :].rearrange("p a c -> p (a c)")


def norm_scales_vector(nc, res, chain, s_var, s_std, s_rstd):
    for t in range(TILES):
        chain.step(nc.vector.bn_aggr(res.mean_var[:, t, :], res.stats[:, t, :]))
    chain.settle()
    nc.vector.tensor_scalar(res.rstd[:, :, 0], res.mean_var[:, :, 1], LN_EPS, None, ALU.add).then_inc(s_var, 1)
    chain.eng.wait_ge(s_std, 1)
    nc.vector.reciprocal(res.rstd[:, :, 0], res.std[:, :]).then_inc(s_rstd, 1)
    chain.eng.wait_ge(s_rstd, 1)


def norm_scales_scalar(nc, res, act, s_var, s_std):
    act.wait_ge(s_var, 1)
    nc.scalar.activation(res.std[:, :], res.rstd[:, :, 0], ACT.Sqrt).then_inc(s_std, 1)


def normalise(nc, res, out, t):
    return nc.vector.tensor_scalar(out, row(res.x, t), row(res.mean_var, t)[:, 0:1], row(res.rstd, t),
                                   ALU.subtract, ALU.mult)


PAIR = 2
PAIRS_OF_TILES = TILES // PAIR


def two_at_a_time(eng, head, tail):
    head(0, 0)
    with eng.Fori(0, PAIRS_OF_TILES // 2 - 1) as i:
        for p in range(2):
            head(2 * i + p + 1, 1 - p)
            tail(2 * i + p, p)
    head(PAIRS_OF_TILES - 1, 1)
    tail(PAIRS_OF_TILES - 2, 0)
    tail(PAIRS_OF_TILES - 1, 1)


def pair_rows(tensor, u, j):
    return row(tensor, PAIR * u + j)


def pair_of(tensor, u):
    if isinstance(u, int):
        return tensor[:, PAIR * u:PAIR * (u + 1), :]
    return tensor[:, bass.ds(PAIR * u, PAIR), :]


def load_residual(nc, res, x, consts):
    with ExitStack() as ctx:
        st = Stage(nc, ctx, "load")
        s_x, s_const, s_stats = st.sem("x_loaded"), st.sem("const_loaded"), st.sem("stats")
        with nc.Block() as block:
            @block.sync
            def _(sp):
                sp.dma_start(res.x[:], x.rearrange("(t p) d -> p t d", p=P)).then_inc(s_x, 16)
                sp.dma_start(res.ident[:], consts["ident"]).then_inc(s_const, 16)
                sp.wait_ge(s_const, 16)

            @block.vector
            def _(dve):
                nc.vector.memset(res.ones[:], 1.0).then_inc(s_stats, 1)
                dve.wait_ge(s_x, 16)
                for t in range(TILES):
                    nc.vector.bn_stats(res.stats[:, t, :], res.x[:, t, :]).then_inc(s_stats, 1)
                dve.wait_ge(s_stats, TILES + 1)


HEADS, HEAD = 16, 16
HALF_HEADS = P // HEAD
PAIRS = HALF_HEADS // 2
GROUPS = BPT * KC
CTX_ROWS = BPT * KEYS
CTX_CHUNKS = CTX_ROWS // P
TENSOR_ORDER = ['T0', 'G0', 'S2', 'G1', 'V0', 'T1', 'G2', 'S3', 'G3', 'V1', 'T2', 'G4', 'V2', 'G5', 'T3', 'G6', 'V3', 'S0', 'O', 'S1', 'G7']
SCALAR_ORDER = ['T0', 'G1', 'E2', 'T1', 'G2', 'E3', 'T2', 'G4', 'G5', 'T3', 'E0', 'E1']
VECTOR_ORDER = ['T0', 'G0', 'N1', 'M2', 'T1', 'N2', 'M3', 'G3', 'T2', 'N3', 'T3', 'G6', 'O', 'M0', 'R', 'M1', 'N0', 'G7', 'X']
PREP = 8
EARLY = ("S0", "M0", "E0", "N0", "S1", "M1", "E1")
STAGED = [what for what in TENSOR_ORDER if what[0] in "GO"]
STEPS = len(STAGED)
TURNED = 4
LOWEST = -3.0e38


def cross_attention(nc, res, tag, ctx_rows, w, mask, prefetch=None):
    with ExitStack() as ctx:
        st = Stage(nc, ctx, tag)
        wq, wk, wv, wo = (st.sb(n, [P, KC, DIM]) for n in ("wq", "wk", "wv", "wo"))
        bq, bk, bv = (st.sb(n, [P, KC]) for n in ("bq", "bk", "bv"))
        bo = st.sb("bo", [P, DIM])
        headmask, parmask = st.sb("headmask", [P, HALF_HEADS]), st.sb("parmask", [P, 2])
        ctx_in = st.sb("ctx_in", [P, CTX_CHUNKS, DIM])
        ctxT = st.sb("ctxT", [P, KC, CTX_ROWS])
        keysT = [st.sb(f"keysT{i}", [P, KC, CTX_ROWS]) for i in range(2)]
        values = [st.sb(f"values{i}", [P, CTX_CHUNKS, DIM]) for i in range(2)]
        xn, xnT, queries = st.sb("xn", [P, DIM]), st.sb("xnT", [P, KC, P]), st.sb("queries", [P, KC, P])
        qspread = [st.sb(f"qspread{i}", [P, GROUPS, HALF_HEADS, SEQ]) for i in range(2)]
        peak, total, inverse = (st.sb(n, [P, 2, PAIRS]) for n in ("peak", "total", "inverse"))
        negpeak = st.sb("negpeak", [P, 2, PAIRS])
        probs = st.sb("probs", [P, 2, PAIRS, KEYS])
        probsT = st.sb("probsT", [P, 2, PAIRS, 2, P])
        outT, outT0 = st.sb("outT", [P, KC, BPT, SEQ]), st.sb("outT0", [P, KC, BPT, SEQ])
        if mask is not None:
            maskadd, keep, zeros = st.sb("maskadd", [P, KEYS]), st.sb("keep", [P, KEYS], I32), st.sb("zeros", [P, KEYS])
            masked = st.sb("masked", [P, 2, PAIRS, KEYS])
        score_ps = [[st.ps(f"score{i}{j}") for j in range(2)] for i in range(2)]
        turn_ps = [st.ps(f"turn{j}") for j in range(2)]
        out_ps, stage_ps = st.ps("out"), st.ps("stage")

        s_w, s_ctx = st.sem("weights"), st.sem("ctx_loaded")
        s_var, s_std, s_rstd = st.sem("var"), st.sem("std"), st.sem("rstd")
        s_chain, s_inverse, s_even, s_mask, s_maskadd = (
            st.sem(n) for n in ("vector_step", "inverse", "even_heads", "mask", "maskadd"))
        s_bo, s_stats, s_seen = st.sem("bo_added"), st.sem("stats"), st.sem("scores_seen")
        s_xn = st.sem("xn_ready")
        s_full, s_free = st.sem("stage_full"), st.sem("stage_free")
        s_spread = st.sem("queries_spread")
        s_score, s_score_used = st.sem("scores_ready"), st.sem("scores_used")
        s_peak, s_exp = st.sem("peaks_ready"), st.sem("exp_done")
        s_probs = st.sem("probs_ready")
        if mask is None:
            s_score_used = s_exp
        s_turn, s_turned0, s_turned1 = st.sem("turn_full"), st.sem("turned_by_vector"), st.sem("turned_by_scalar")
        s_out, s_outT = st.sem("out_full"), st.sem("outT_ready")

        def step_number(t, what):
            return PREP + STEPS * t + STAGED.index(what)

        def out_step(t, last):
            return step_number(t, "O") - (STAGED.index("O") if last else 0)

        def in_turn(eng, order, prep, scores, step):
            def one(t, p, what, last=False):
                if what[0] in "SME":
                    scores(t, p, int(what[1]))
                else:
                    step(t, p, last, what[0], int(what[1:] or 0))

            def turn(t, p, last=False):
                for what in order:
                    if what[0] == "G":
                        if not last:
                            prep(t + 1, 1 - p, step_number(t, what), int(what[1]))
                    elif what not in EARLY:
                        one(t, p, what, last)
                    elif not last:
                        one(t + 1, 1 - p, what)

            for s in range(PREP):
                prep(0, 0, s, s)
            for what in order:
                if what in EARLY:
                    one(0, 0, what)
            with eng.Fori(0, TILES // 2 - 1) as i:
                turn(2 * i, 0)
                turn(2 * i + 1, 1)
            turn(TILES - 2, 0)
            turn(TILES - 1, 1, last=True)

        N_LOADS = 10
        with nc.Block() as block:
            @block.sync
            def _(sp):
                for dst, src in ((wq, w["Wq"]), (wk, w["Wk"]), (wv, w["Wv"]), (wo, w["Wo"])):
                    sp.dma_start(dst[:], src.rearrange("(k p) n -> p k n", p=P)).then_inc(s_w, 16)
                for dst, src in ((bq, w["bq"]), (bk, w["bk"]), (bv, w["bv"]),
                                 (headmask, w["headmask"]), (parmask, w["parmask"])):
                    sp.dma_start(dst[:], src).then_inc(s_w, 16)
                sp.dma_start(bo[:], w["bo"].to_broadcast([P, DIM])).then_inc(s_w, 16)
                if mask is not None:
                    for half in range(2):
                        sp.dma_start(keep[half * SEQ:(half + 1) * SEQ, :], mask).then_inc(s_mask, 16)
                source = ctx_rows.rearrange("(j p) d -> p j d", p=P)
                sp.dma_start(ctx_in[:], source[:, 0:CTX_CHUNKS, :]).then_inc(s_ctx, 16)
                sp.wait_ge(s_full, 4)
                sp.dma_start(ctx_in[:], source[:, CTX_CHUNKS:2 * CTX_CHUNKS, :]).then_inc(s_ctx, 16)
                with sp.Fori(2, TILES) as t:
                    first = sp.snap(t * CTX_CHUNKS)
                    turned = sp.snap(t * STEPS + (step_number(0, "G3") + 1 - 2 * STEPS))
                    sp.wait_ge(s_full, turned)
                    sp.dma_start(ctx_in[:], source[:, bass.ds(first, CTX_CHUNKS), :]).then_inc(s_ctx, 16)
                if prefetch is not None:
                    prefetch(sp)

            @block.tensor
            def _(pe):
                def prep(u, p, n, s):
                    if s == 0:
                        pe.wait_ge(s_xn, u + 1)
                    if s == 2:
                        pe.wait_ge(s_ctx, 16 * (u + 1))
                    pe.wait_ge(s_free, n)
                    if s == 0:
                        for k in range(KC):
                            mm = nc.tensor.transpose(stage_ps[:, k * P:(k + 1) * P], xn[:, k * P:(k + 1) * P], res.ident[:])
                    elif s == 1:
                        for m in range(KC):
                            for k in range(KC):
                                mm = nc.tensor.matmul(stage_ps[:, m * P:(m + 1) * P], wq[:, k, m * P:(m + 1) * P],
                                                      xnT[:, k, :], start=k == 0, stop=k == KC - 1)
                    elif s in (2, 3):
                        for j in range(CTX_CHUNKS):
                            mm = nc.tensor.transpose(stage_ps[:, j * P:(j + 1) * P],
                                                     ctx_in[:, j, (s - 2) * P:(s - 1) * P], res.ident[:])
                    elif s in (4, 5):
                        m = s - 4
                        for k in range(KC):
                            mm = nc.tensor.matmul(stage_ps[:, :], wk[:, k, m * P:(m + 1) * P], ctxT[:, k, :],
                                                  start=k == 0, stop=k == KC - 1)
                    else:
                        for j in range(2):
                            chunk = (s - 6) * 2 + j
                            for k in range(KC):
                                mm = nc.tensor.matmul(stage_ps[:, j * DIM:(j + 1) * DIM], ctxT[:, k, chunk * P:(chunk + 1) * P],
                                                      wv[:, k, :], start=k == 0, stop=k == KC - 1)
                    mm.then_inc(s_full, 1)

                def scores(t, p, g):
                    b, half = g // KC, g % KC
                    if g == 0:
                        pe.wait_ge(s_spread, GROUPS * (t + 1))
                        pe.wait_ge(s_free, PREP if isinstance(t, int) and t == 0 else step_number(t - 1, "G5") + 1)
                    pe.wait_ge(s_score_used, GROUPS * t + g + 1)
                    for r in range(PAIRS):
                        mm = nc.tensor.matmul(
                            score_ps[g % 2][r // 2][:, (r % 2) * KEYS:(r % 2 + 1) * KEYS],
                            qspread[p][:, g, 2 * r:2 * r + 2, :].rearrange("p h q -> p (h q)"),
                            keysT[p][:, half, b * KEYS:(b + 1) * KEYS], start=True, stop=True)
                        if r % 2:
                            mm.then_inc(s_score, 1)

                def step(t, p, last, what, g):
                    b, half = g // KC, g % KC
                    if what == "T":
                        pe.wait_ge(s_probs, GROUPS * t + g + 1)
                        for j in range(2):
                            pe.wait_ge((s_turned0, s_turned1)[j], GROUPS * t + g)
                            for r in range(2 * j, 2 * j + 2):
                                for k in range(2):
                                    at = ((r % 2) * 2 + k) * P
                                    mm = nc.tensor.transpose(turn_ps[j][:, at:at + P],
                                                             probs[:, g % 2, r, k * P:(k + 1) * P], res.ident[:])
                            mm.then_inc(s_turn, 1)
                    elif what == "V":
                        pe.wait_ge(s_turned0, GROUPS * t + g + 1)
                        pe.wait_ge(s_turned1, GROUPS * t + g + 1)
                        if g == 0:
                            pe.wait_ge(s_outT, t)
                            pe.wait_ge(s_free, PREP + STEPS * t)
                        for r in range(PAIRS):
                            for k in range(2):
                                chan = half * P + 2 * HEAD * r
                                mm = nc.tensor.matmul(out_ps[2 * HEAD * r:2 * HEAD * (r + 1), g * P:(g + 1) * P],
                                                      values[p][:, b * 2 + k, chan:chan + 2 * HEAD],
                                                      probsT[:, g % 2, r, k, :], start=k == 0, stop=k == 1)
                        if g == GROUPS - 1:
                            mm.then_inc(s_out, 1)
                    elif what == "O":
                        pe.wait_ge(s_free, out_step(t, last))
                        pe.wait_ge(s_outT, t + 1)
                        for k in range(KC):
                            mm = nc.tensor.matmul(stage_ps[:, 0:DIM], outT[:, k, :, :].rearrange("p b q -> p (b q)"),
                                                  wo[:, k, :], start=k == 0, stop=k == KC - 1)
                        mm.then_inc(s_full, 1)

                pe.wait_ge(s_w, 16 * N_LOADS)
                in_turn(pe, TENSOR_ORDER, prep, scores, step)

            @block.scalar
            def _(act):
                def prep(u, p, n, s):
                    if s not in (1, 2, 4, 5):
                        return
                    act.wait_ge(s_full, n + 1)
                    if s == 1:
                        act.wait_ge(s_spread, GROUPS * u)
                        for m in range(KC):
                            ins = nc.scalar.activation(queries[:, m, :], stage_ps[:, m * P:(m + 1) * P], ACT.Identity,
                                                       bias=bq[:, m:m + 1])
                    elif s == 2:
                        ins = nc.scalar.activation(ctxT[:, 0, :], stage_ps[:, :], ACT.Copy)
                    else:
                        ins = nc.scalar.activation(keysT[p][:, s - 4, :], stage_ps[:, :], ACT.Identity,
                                                   bias=bk[:, s - 4:s - 3])
                    ins.then_inc(s_free, 1)

                def scores(t, p, g):
                    act.wait_ge(s_peak, GROUPS * t + g + 1)
                    act.wait_ge(s_turn, 2 * (GROUPS * t + g + 1))
                    for r in range(PAIRS):
                        if mask is None:
                            scores = score_ps[g % 2][r // 2][:, (r % 2) * KEYS:(r % 2 + 1) * KEYS]
                        else:
                            scores = masked[:, g % 2, r, :]
                        ins = nc.scalar.activation(probs[:, g % 2, r, :], scores, ACT.Exp,
                                                   bias=negpeak[:, g % 2, r:r + 1],
                                                   accum_out=total[:, g % 2, r:r + 1])
                    ins.then_inc(s_exp, 1)

                def step(t, p, last, what, g):
                    if what == "T":
                        act.wait_ge(s_turn, TURNED + 2 * (GROUPS * t + g) + 2)
                        nc.scalar.activation(probsT[:, g % 2, 2:4, :, :].rearrange("p r k q -> p (r k q)"),
                                             turn_ps[1][:, :], ACT.Copy).then_inc(s_turned1, 1)

                norm_scales_scalar(nc, res, act, s_var, s_std)
                act.wait_ge(s_w, 16 * N_LOADS)
                in_turn(act, SCALAR_ORDER, prep, scores, step)

            @block.gpsimd
            def _(pool):
                def spread(u, p, n):
                    pool.wait_ge(s_free, n + 1)
                    for b in range(BPT):
                        for half in range(KC):
                            nc.gpsimd.tensor_tensor(
                                qspread[p][:, b * KC + half, :, :],
                                queries[:, half, b * SEQ:(b + 1) * SEQ].unsqueeze(1).to_broadcast([P, HALF_HEADS, SEQ]),
                                headmask[:, :].unsqueeze(2).to_broadcast([P, HALF_HEADS, SEQ]),
                                ALU.mult).then_inc(s_spread, 1)

                pool.wait_ge(s_w, 16 * N_LOADS)
                spread(0, 0, 1)
                spread(1, 1, step_number(0, "G1"))
                with pool.Fori(1, TILES // 2) as i:
                    for p in range(2):
                        before = pool.snap((2 * i + p) * GROUPS - 2 * GROUPS + GROUPS)
                        pool.wait_ge(s_score_used, 2 + before)
                        spread(2 * i + p, p, step_number(2 * i + p - 1, "G1"))

            @block.vector
            def _(dve):
                chain = Chain(dve, s_chain)

                def normalised(u):
                    normalise(nc, res, xn[:, :], u).then_inc(s_xn, 1)
                    dve.wait_ge(s_xn, u + 1)
                    nc.vector.tensor_tensor(row(res.x, u), row(res.x, u), bo[:, :], ALU.add).then_inc(s_bo, 1)

                def prep(u, p, n, s):
                    if s not in (0, 3, 6, 7):
                        return
                    dve.wait_ge(s_full, n + 1)
                    if s == 0:
                        ins = nc.vector.tensor_copy(xnT[:, :, :].rearrange("p k q -> p (k q)"), stage_ps[:, 0:DIM])
                    elif s == 3:
                        ins = nc.vector.tensor_copy(ctxT[:, 1, :], stage_ps[:, :])
                    else:
                        j = 2 * (s - 6)
                        ins = nc.vector.tensor_copy(values[p][:, j:j + 2, :].rearrange("p j d -> p (j d)"), stage_ps[:, :])
                    ins.then_inc(s_free, 1)
                    if s == 0 and isinstance(u, int) and u == 0:
                        normalised(1)

                def scores(t, p, g):
                    k = GROUPS * t + g
                    if mask is None:
                        for j in range(2):
                            dve.wait_ge(s_score, 2 * k + j + 1)
                            ins = nc.vector.tensor_reduce(
                                negpeak[:, g % 2, 2 * j:2 * j + 2],
                                score_ps[g % 2][j][:, :].rearrange("p (r k) -> p r k", r=2),
                                AX.X, ALU.max, negate=True)
                        ins.then_inc(s_peak, 1)
                    else:
                        dve.wait_ge(s_exp, k + 1)
                        for r in range(PAIRS):
                            if r % 2 == 0:
                                dve.wait_ge(s_score, 2 * k + r // 2 + 1)
                                dve.sem_inc(s_seen, 1)
                            ins = nc.vector.tensor_tensor_reduce(
                                masked[:, g % 2, r, :],
                                score_ps[g % 2][r // 2][:, (r % 2) * KEYS:(r % 2 + 1) * KEYS],
                                maskadd[:, :], 1.0, LOWEST, ALU.add, ALU.max, peak[:, g % 2, r:r + 1])
                        ins.then_inc(s_score_used, 1)
                        dve.wait_ge(s_score_used, 2 + k + 1)
                        nc.vector.tensor_scalar(negpeak[:, g % 2, :], peak[:, g % 2, :], -1.0, None,
                                                ALU.mult).then_inc(s_peak, 1)

                def step(t, p, last, what, g):
                    k = GROUPS * t + g
                    if what == "N":
                        dve.wait_ge(s_exp, 2 + k + 1)
                        nc.vector.reciprocal(inverse[:, g % 2, :], total[:, g % 2, :]).then_inc(s_inverse, 1)
                        dve.wait_ge(s_inverse, k + 1)
                        for r in range(PAIRS):
                            ins = nc.vector.tensor_scalar(probs[:, g % 2, r, :], probs[:, g % 2, r, :],
                                                          inverse[:, g % 2, r:r + 1], None, ALU.mult)
                        ins.then_inc(s_probs, 1)
                    elif what == "T":
                        dve.wait_ge(s_turn, TURNED + 2 * k + 1)
                        nc.vector.tensor_copy(probsT[:, g % 2, 0:2, :, :].rearrange("p r k q -> p (r k q)"),
                                              turn_ps[0][:, :]).then_inc(s_turned0, 1)
                    elif what == "O":
                        dve.wait_ge(s_out, t + 1)
                        o = out_ps[:, :].rearrange("p (b m e q) -> p b m e q", b=BPT, m=KC, e=2)
                        for m in range(KC):
                            ins = nc.vector.tensor_scalar(outT0[:, m, :, :], o[:, :, m, 0, :], parmask[:, 0:1],
                                                          bv[:, m:m + 1], ALU.mult, ALU.add)
                        ins.then_inc(s_even, 1)
                        dve.wait_ge(s_even, t + 1)
                        for m in range(KC):
                            ins = nc.vector.scalar_tensor_tensor(outT[:, m, :, :], o[:, :, m, 1, :], parmask[:, 1:2],
                                                                 outT0[:, m, :, :], ALU.mult, ALU.add)
                        ins.then_inc(s_outT, 1)
                    elif what == "R":
                        dve.wait_ge(s_bo, t + 1)
                        dve.wait_ge(s_full, out_step(t, last) + 1)
                        nc.vector.tensor_tensor(row(res.x, t), row(res.x, t), stage_ps[:, 0:DIM],
                                                ALU.add).then_inc(s_free, 1)
                        dve.wait_ge(s_free, out_step(t, last) + 1)
                        nc.vector.bn_stats(row(res.stats, t), row(res.x, t)).then_inc(s_stats, 1)
                    elif what == "X" and not (isinstance(t, int) and t >= TILES - 2):
                        normalised(t + 2)

                norm_scales_vector(nc, res, chain, s_var, s_std, s_rstd)
                dve.sem_inc(s_score_used, 2)
                dve.sem_inc(s_turn, TURNED)
                if mask is not None:
                    dve.sem_inc(s_exp, 2)
                    nc.vector.memset(maskadd[:], LOWEST).then_inc(s_maskadd, 1)
                    nc.vector.memset(zeros[:], 0.0).then_inc(s_maskadd, 1)
                    dve.wait_ge(s_maskadd, 2)
                    dve.wait_ge(s_mask, 32)
                    nc.vector.copy_predicated(maskadd[:, :], keep[:, :], zeros[:, :]).then_inc(s_maskadd, 1)
                    dve.wait_ge(s_maskadd, 3)
                dve.wait_ge(s_w, 16 * N_LOADS)
                normalised(0)
                in_turn(dve, VECTOR_ORDER, prep, scores, step)
                dve.wait_ge(s_stats, TILES)


D_HEADS, D_HEAD, TAPS = 4, 64, 4
LEVELS = (2, 4, 8, 16, 32)
QKV = 3 * KC
MASK_OPS = 4 + len(LEVELS)
DELTA_ORDER = ["Y1a", "Y1b", "C0", "V1", "T1a", "T1b", "C1", "Y2a", "Y2b", "B1", "T2a", "T2b", "C2", "Y3a", "Y3b", "V2",
               "T3a", "T3b", "B2", "Y4a", "Y4b", "V3", "T4a", "T4b", "B3", "Y5a", "Y5b", "V4", "T5a", "T5b", "U", "A0",
               "O", "A1"]
HALF = D_HEADS // 2


def level_of(what):
    n, half = int(what[1]), "ab".index(what[2])
    return n, half, 2 * (n - 1) + half


def delta_rule(nc, res, a, prefetch):
    with ExitStack() as ctx:
        st = Stage(nc, ctx, "delta")
        wqkv = [st.sb(f"w{n}", [P, KC, DIM]) for n in "qkv"]
        wb, taps = st.sb("wb", [P, KC, D_HEADS]), st.sb("taps", [P, QKV, TAPS])
        head_ones = st.sb("head_ones", [P, 2])
        strict, causalT = st.sb("strict", [P, P]), st.sb("causalT", [P, P])
        join1, join1T = st.sb("join1", [P, P]), st.sb("join1T", [P, P])
        joinT = st.sb("joinT", [P, len(LEVELS), P])
        xn, xnT, pre = st.sb("xn", [P, DIM]), st.sb("xnT", [P, KC, P]), st.sb("pre", [P, QKV, BPT, SEQ])
        qkvT = st.sb("qkvT", [P, QKV, P])
        squares = st.sb("squares", [P, 2 * KC, P])
        inv_sq, inv_norm = (st.sb(n, [P, 2 * D_HEADS]) for n in ("inv_sq", "inv_norm"))
        logits = [st.sb(f"logits{i}", [P, D_HEADS]) for i in range(2)]
        tanh, beta = st.sb("tanh", [P, D_HEADS]), st.sb("beta", [P, D_HEADS])
        row_scale, value_scale = st.sb("row_scale", [P, D_HEADS]), st.sb("value_scale", [P, D_HEADS])
        query_scale = [st.sb(f"query_scale{i}", [P, D_HEADS]) for i in range(2)]
        vb = [st.sb(f"vb{i}", [P, D_HEADS, D_HEAD]) for i in range(2)]
        lower, lowerT = st.sb("lower", [P, D_HEADS, P]), st.sb("lowerT", [P, D_HEADS, P])
        part, partT = st.sb("part", [P, D_HEADS, P]), st.sb("partT", [P, D_HEADS, P])
        joined = [st.sb(f"joined{i}", [P, len(LEVELS), D_HEADS, P]) for i in range(2)]
        first, firstT = ([st.sb(f"{n}{i}", [P, D_HEADS, P]) for i in range(2)] for n in ("first", "firstT"))
        attnT = [st.sb(f"attnT{i}", [P, D_HEADS, P]) for i in range(2)]
        inverse = [st.sb(f"inverse{i}", [P, 2, HALF, P]) for i in range(2)]
        rest = st.sb("rest", [P, D_HEADS, P])
        u_sb, o_sq = st.sb("u", [P, DIM]), st.sb("o_sq", [P, DIM])
        qk_ps, v_ps = st.ps("qk"), st.ps("v")
        gram_ps = [st.ps(f"gram{i}") for i in range(2)]
        y_ps, t_ps = ([st.ps(f"{n}{i}") for i in range(2)] for n in ("y", "t"))
        u_ps, o_ps = y_ps
        BETA = DIM
        sums_ps = gram_ps[1]

        s = Resident()
        s.weights, s.var, s.std, s.rstd = (st.sem(n) for n in ("weights", "var", "std", "rstd"))
        s.vector_step, s.xn, s.turned, s.xnT = (st.sem(n) for n in ("vector_step", "xn", "turned", "xnT"))
        s.projected, s.logits, s.conv, s.conv_step = (st.sem(n) for n in ("projected", "logits", "conv", "conv_step"))
        s.silu, s.tanh, s.squares, s.sums = (st.sem(n) for n in ("silu", "tanh", "squares", "sums"))
        s.inv_sq, s.inv_norm, s.row_scale, s.scales = (st.sem(n) for n in ("inv_sq", "inv_norm", "row_scale", "scales"))
        s.vturned = st.sem("vturned")
        s.vb, s.gram, s.attn, s.attn_masked = (st.sem(n) for n in ("vb", "gram", "attn", "attn_masked"))
        s.lower, s.lturned, s.lowerT, s.masks = (st.sem(n) for n in ("lower", "lturned", "lowerT", "masks"))
        s.y, s.rest, s.t, s.inverse = (st.sem(n) for n in ("y", "rest", "t", "inverse"))
        s.u_full, s.u_copied = (st.sem(n) for n in ("u_full", "u_copied"))
        PER_TILE = 2 * len(LEVELS)
        s.o_full, s.o_read, s.out_step = (st.sem(n) for n in ("o_full", "o_read", "out_step"))
        every = lambda m, h=D_HEADS: m.unsqueeze(1).to_broadcast([P, h, P])
        N_LOADS = 11
        with nc.Block() as block:
            @block.sync
            def _(sp):
                for dst, n in zip(wqkv, "qkv"):
                    sp.dma_start(dst[:], a[f"L0_attn_W{n}"].rearrange("(k p) n -> p k n", p=P)).then_inc(s.weights, 16)
                sp.dma_start(wb[:], a["L0_attn_Wb"].rearrange("(k p) n -> p k n", p=P)).then_inc(s.weights, 16)
                sp.dma_start(taps[:], a["L0_attn_taps"]).then_inc(s.weights, 16)
                for dst, n in ((head_ones, "head_ones"), (strict, "strict"), (causalT, "causalT"), (join1, "join1"),
                               (join1T, "join1T"), (joinT, "joinT")):
                    sp.dma_start(dst[:], a[n]).then_inc(s.weights, 16)
                prefetch(sp)
                sp.wait_ge(s.weights, 16 * N_LOADS)

            @block.tensor
            def _(pe):
                def a_step(u, p, n):
                    if n == 0:
                        pe.wait_ge(s.xn, u + 1)
                        pe.wait_ge(s.conv, u)
                        for k in range(KC):
                            mm = nc.tensor.transpose(qk_ps[:, k * P:(k + 1) * P], xn[:, k * P:(k + 1) * P], res.ident[:])
                        mm.then_inc(s.turned, 1)
                    else:
                        pe.wait_ge(s.xnT, u + 1)
                        for i in range(QKV):
                            bank, col = (qk_ps, i * P) if i < 2 * KC else (v_ps, (i - 2 * KC) * P)
                            for k in range(KC):
                                nc.tensor.matmul(bank[:, col:col + P], wqkv[i // KC][:, k, (i % KC) * P:(i % KC + 1) * P],
                                                 xnT[:, k, :], start=k == 0, stop=k == KC - 1)
                        for k in range(KC):
                            mm = nc.tensor.matmul(v_ps[:, BETA:BETA + D_HEADS], xnT[:, k, :], wb[:, k, :],
                                                  start=k == 0, stop=k == KC - 1)
                        mm.then_inc(s.projected, 1)

                def c_step(u, p, n):
                    if n == 1:
                        pe.wait_ge(s.squares, u + 1)
                        pe.wait_ge(s.attn_masked, u)
                        for i in range(2 * KC):
                            mm = nc.tensor.matmul(sums_ps[:, 2 * i:2 * i + 2], squares[:, i, :], head_ones[:],
                                                  start=True, stop=True)
                        mm.then_inc(s.sums, 1)

                def b_step(u, p, n):
                    if n == 1:
                        pe.wait_ge(s.silu, u + 1)
                        pe.wait_ge(s.inv_sq, u + 1)
                        pe.wait_ge(s.vb, u)
                        for of in range(2):
                            for h in range(D_HEADS):
                                rows = slice(D_HEAD * (h % 2), D_HEAD * (h % 2 + 1))
                                col = (2 * of + h // 2) * P
                                mm = nc.tensor.matmul(gram_ps[h % 2][:, col:col + P], qkvT[rows, KC + h // 2, :],
                                                      qkvT[rows, (KC if of == 0 else 0) + h // 2, :], start=True, stop=True)
                                if of == 1 and h == D_HEADS - 2:
                                    mm.then_inc(s.gram, 1)
                        mm.then_inc(s.gram, 1)
                    elif n == 2:
                        pe.wait_ge(s.lower, u + 1)
                        pe.wait_ge(s.attn_masked, u + 1)
                        for h in range(D_HEADS):
                            mm = nc.tensor.transpose(gram_ps[0][:, h * P:(h + 1) * P], lower[:, h, :], res.ident[:])
                        mm.then_inc(s.lturned, 1)
                    else:
                        pe.wait_ge(s.lowerT, u + 1)
                        for i in range(KC):
                            mm = nc.tensor.transpose(gram_ps[0][:, i * P:(i + 1) * P], qkvT[:, 2 * KC + i, :], res.ident[:])
                        mm.then_inc(s.vturned, 1)

                def tail(t, p, what):
                    if what[0] == "Y":
                        n, half, k = level_of(what)
                        pe.wait_ge(s.masks, MASK_OPS * t + MASK_OPS - len(LEVELS) + n)
                        if n == 1:
                            if half == 1:
                                pe.wait_ge(s.o_read, t)
                        else:
                            pe.wait_ge(s.inverse, PER_TILE * t + k - 1)
                        for i in range(HALF):
                            h = HALF * half + i
                            m = first[p][:, h, :] if n == 1 else inverse[half][:, 0, i, :]
                            mm = nc.tensor.matmul(y_ps[half][:, i * P:(i + 1) * P], joined[p][:, n - 1, h, :], m,
                                                  start=True, stop=True)
                        mm.then_inc(s.y, 1)
                    elif what[0] == "T":
                        n, half, k = level_of(what)
                        pe.wait_ge(s.rest, PER_TILE * t + k + 1)
                        for i in range(HALF):
                            h = HALF * half + i
                            mT = firstT[p][:, h, :] if n == 1 else inverse[half][:, 1, i, :]
                            if n < len(LEVELS):
                                nc.tensor.matmul(t_ps[half][:, i * P:(i + 1) * P], mT, rest[:, h, :], start=True, stop=True)
                            mm = nc.tensor.matmul(t_ps[half][:, (HALF + i) * P:(HALF + i + 1) * P], rest[:, h, :], mT,
                                                  start=True, stop=True)
                        mm.then_inc(s.t, 1)
                    elif what == "U":
                        pe.wait_ge(s.inverse, PER_TILE * (t + 1))
                        pe.wait_ge(s.vb, t + 1)
                        for h in range(D_HEADS):
                            mm = nc.tensor.matmul(u_ps[:, h * D_HEAD:(h + 1) * D_HEAD], inverse[h // HALF][:, 1, h % HALF, :],
                                                  vb[p][:, h, :], start=True, stop=True)
                        mm.then_inc(s.u_full, 1)
                    else:
                        pe.wait_ge(s.u_copied, t + 1)
                        for h in range(D_HEADS):
                            mm = nc.tensor.matmul(o_ps[:, h * D_HEAD:(h + 1) * D_HEAD], attnT[p][:, h, :],
                                                  u_sb[:, h * D_HEAD:(h + 1) * D_HEAD], start=True, stop=True)
                        mm.then_inc(s.o_full, 1)

                pe.wait_ge(s.weights, 16 * N_LOADS)
                delta_loop(pe, a_step, None, c_step, b_step, tail)

            @block.scalar
            def _(act):
                def a_step(u, p, n):
                    if n == 0:
                        act.wait_ge(s.turned, u + 1)
                        nc.scalar.activation(xnT[:, :, :].rearrange("p k q -> p (k q)"), qk_ps[:, 0:DIM],
                                             ACT.Copy).then_inc(s.xnT, 1)
                    else:
                        act.wait_ge(s.projected, u + 1)
                        if not isinstance(u, int) or u > 1:
                            act.wait_ge(s.tanh, u - 1)
                        nc.scalar.activation(logits[p][:, :], v_ps[:, BETA:BETA + D_HEADS], ACT.Copy).then_inc(s.logits, 1)

                def c_step(u, p, n):
                    if n == 0:
                        act.wait_ge(s.conv, u + 1)
                        act.wait_ge(s.vturned, u)
                        nc.scalar.activation(qkvT[:, :, :].rearrange("p i q -> p (i q)"),
                                             pre[:, :, :, :].rearrange("p i b q -> p (i b q)"), ACT.Silu).then_inc(s.silu, 1)
                        act.wait_ge(s.silu, u + 1)
                        act.wait_ge(s.sums, u)
                        nc.scalar.activation(squares[:, :, :], qkvT[:, 0:2 * KC, :], ACT.Square).then_inc(s.squares, 1)
                        act.wait_ge(s.logits, u + 1)
                        act.wait_ge(s.inv_sq, u)
                        nc.scalar.activation(tanh[:, :], logits[p][:, :], ACT.Tanh, scale=0.5).then_inc(s.tanh, 1)
                    elif n == 2:
                        act.wait_ge(s.inv_sq, u + 1)
                        act.wait_ge(s.scales, u)
                        nc.scalar.activation(inv_norm[:, :], inv_sq[:, :], ACT.Sqrt).then_inc(s.inv_norm, 1)

                def b_step(u, p, n):
                    if n == 2:
                        act.wait_ge(s.lturned, u + 1)
                        act.wait_ge(s.masks, MASK_OPS * u)
                        nc.scalar.activation(lowerT[:, :, :].rearrange("p h q -> p (h q)"), gram_ps[0][:, :],
                                             ACT.Copy).then_inc(s.lowerT, 1)

                def tail(t, p, what):
                    if what[0] == "T":
                        n, half, k = level_of(what)
                        act.wait_ge(s.t, PER_TILE * t + k + 1)
                        first_of = 0 if n < len(LEVELS) else 1
                        nc.scalar.activation(inverse[half][:, first_of:, :, :].rearrange("p o h q -> p (o h q)"),
                                             t_ps[half][:, first_of * HALF * P:], ACT.Copy).then_inc(s.inverse, 1)
                    elif what == "U":
                        act.wait_ge(s.u_full, t + 1)
                        nc.scalar.activation(u_sb[:, :], u_ps[:, 0:DIM], ACT.Copy).then_inc(s.u_copied, 1)

                norm_scales_scalar(nc, res, act, s.var, s.std)
                delta_loop(act, a_step, None, c_step, b_step, tail)

            @block.gpsimd
            def _(pool):
                def b_step(u, p, n):
                    if n != 2:
                        return
                    pool.wait_ge(s.lowerT, u + 1)
                    if not isinstance(u, int) or u > 1:
                        pool.wait_ge(s.y, PER_TILE * (u - 1))
                    nc.gpsimd.tensor_tensor(partT[:], lowerT[:], every(join1T[:, :]), ALU.mult).then_inc(s.masks, 1)
                    nc.gpsimd.tensor_tensor(part[:], lower[:], every(join1[:, :]), ALU.mult).then_inc(s.masks, 1)
                    pool.wait_ge(s.masks, MASK_OPS * u + 2)
                    nc.gpsimd.tensor_tensor(firstT[p][:], every(res.ident[:, :]), partT[:], ALU.subtract).then_inc(s.masks, 1)
                    nc.gpsimd.tensor_tensor(first[p][:], every(res.ident[:, :]), part[:], ALU.subtract).then_inc(s.masks, 1)
                    for i in range(len(LEVELS)):
                        nc.gpsimd.tensor_tensor(joined[p][:, i, :, :], lowerT[:], every(joinT[:, i, :]),
                                                ALU.mult).then_inc(s.masks, 1)

                pool.wait_ge(s.weights, 16 * N_LOADS)
                delta_loop(pool, None, None, None, b_step, None)

            @block.vector
            def _(dve):
                def a_step(u, p, n):
                    if n == 0:
                        dve.wait_ge(s.turned, u)
                        normalise(nc, res, xn[:, :], u).then_inc(s.xn, 1)

                def v_step(u, p, n):
                    back = n - 1
                    if n == 1:
                        dve.wait_ge(s.silu, u)
                        dve.wait_ge(s.projected, u + 1)
                        dve.wait_ge(s.logits, u + 1)
                    else:
                        dve.wait_ge(s.conv_step, (TAPS - 1) * u + n - 1)
                    for i in range(QKV):
                        src = (qk_ps[:, i * P:(i + 1) * P] if i < 2 * KC else v_ps[:, (i - 2 * KC) * P:(i - 2 * KC + 1) * P])
                        src = src.rearrange("p (b q) -> p b q", b=BPT)
                        tap = taps[:, i, TAPS - 1 - back:TAPS - back]
                        if n == 1:
                            ins = nc.vector.tensor_scalar(pre[:, i, :, :], src, tap, None, ALU.mult)
                        else:
                            ins = nc.vector.scalar_tensor_tensor(pre[:, i, :, back:], src[:, :, 0:SEQ - back], tap,
                                                                 pre[:, i, :, back:], ALU.mult, ALU.add)
                    ins.then_inc(s.conv if n == TAPS else s.conv_step, 1)

                def c_step(u, p, n):
                    if n == 1:
                        dve.wait_ge(s.tanh, u + 1)
                        nc.vector.tensor_scalar(beta[:, :], tanh[:, :], 0.5, 0.5, ALU.mult, ALU.add)
                        dve.wait_ge(s.inv_norm, u)
                        dve.wait_ge(s.sums, u + 1)
                        nc.vector.reciprocal(inv_sq[:, :], sums_ps[:, 0:2 * D_HEADS]).then_inc(s.inv_sq, 1)
                        dve.wait_ge(s.inv_sq, u + 1)
                        nc.vector.tensor_tensor(row_scale[:, :], beta[:, :], inv_sq[:, D_HEADS:], ALU.mult).then_inc(s.row_scale, 1)

                def b_step(u, p, n):
                    if n == 1:
                        dve.wait_ge(s.gram, 2 * (u + 1))
                        dve.wait_ge(s.row_scale, u + 1)
                        dve.wait_ge(s.masks, MASK_OPS * u)
                        for h in range(D_HEADS):
                            ins = nc.vector.scalar_tensor_tensor(lower[:, h, :], gram_ps[h % 2][:, h // 2 * P:(h // 2 + 1) * P],
                                                                 row_scale[:, h:h + 1], strict[:, :], ALU.mult, ALU.mult)
                        ins.then_inc(s.lower, 1)
                        if not isinstance(u, int) or u > 1:
                            dve.wait_ge(s.o_full, u - 1)
                        for e in range(2):
                            ins = nc.vector.tensor_tensor(
                                attnT[p][:, :, :].rearrange("p (g e) q -> p g e q", e=2)[:, :, e, :],
                                gram_ps[e][:, 2 * P:].rearrange("p (g q) -> p g q", g=2),
                                every(causalT[:, :], 2), ALU.mult)
                        ins.then_inc(s.attn_masked, 1)
                    elif n == 3:
                        dve.wait_ge(s.inv_norm, u + 1)
                        nc.vector.tensor_scalar(query_scale[p][:, :], inv_norm[:, 0:D_HEADS], D_HEAD ** -0.5, None, ALU.mult)
                        nc.vector.tensor_tensor(value_scale[:, :], beta[:, :], inv_norm[:, D_HEADS:],
                                                ALU.mult).then_inc(s.scales, 1)
                        dve.wait_ge(s.scales, u + 1)
                        dve.wait_ge(s.vturned, u + 1)
                        if not isinstance(u, int) or u > 1:
                            dve.wait_ge(s.u_full, u - 1)
                        nc.vector.tensor_tensor(vb[p][:, :, :], gram_ps[0][:, 0:DIM].rearrange("p (h d) -> p h d", h=D_HEADS),
                                                value_scale[:, :].unsqueeze(2).to_broadcast([P, D_HEADS, D_HEAD]),
                                                ALU.mult).then_inc(s.vb, 1)

                def tail(t, p, what):
                    if what[0] == "Y":
                        n, half, k = level_of(what)
                        dve.wait_ge(s.y, PER_TILE * t + k + 1)
                        nc.vector.tensor_tensor(rest[:, HALF * half:HALF * (half + 1), :], every(res.ident[:, :], HALF),
                                                y_ps[half][:, 0:HALF * P].rearrange("p (h q) -> p h q", h=HALF),
                                                ALU.subtract).then_inc(s.rest, 1)
                    elif what == "O":
                        dve.wait_ge(s.o_full, t + 1)
                        nc.vector.tensor_tensor(
                            row(res.mixed, t).rearrange("p (h d) -> p h d", h=D_HEADS),
                            o_ps[:, 0:DIM].rearrange("p (h d) -> p h d", h=D_HEADS),
                            query_scale[p][:, :].unsqueeze(2).to_broadcast([P, D_HEADS, D_HEAD]),
                            ALU.mult).then_inc(s.o_read, 1)
                        dve.wait_ge(s.o_read, t + 1)
                        nc.vector.tensor_tensor(o_sq[:, :], row(res.mixed, t), row(res.mixed, t), ALU.mult).then_inc(s.out_step, 1)
                        dve.wait_ge(s.out_step, 2 * t + 1)
                        nc.vector.tensor_reduce(row(res.squares, t), o_sq[:, :].rearrange("p (h d) -> p h d", h=D_HEADS),
                                                AX.X, ALU.add).then_inc(s.out_step, 1)

                norm_scales_vector(nc, res, Chain(dve, s.vector_step), s.var, s.std, s.rstd)
                dve.wait_ge(s.weights, 16 * N_LOADS)
                delta_loop(dve, a_step, v_step, c_step, b_step, tail)
                dve.wait_ge(s.out_step, 2 * TILES)


def delta_loop(eng, a_step, v_step, c_step, b_step, tail):
    ahead = {"A": 3, "V": 2, "C": 1, "B": 1}
    steps = {"A": a_step, "V": v_step, "C": c_step, "B": b_step}

    def body(t, p, left=TILES):
        for what in DELTA_ORDER:
            if what[0] not in ahead:
                if tail is not None:
                    tail(t, p, what)
            elif steps[what[0]] is not None and left > ahead[what[0]]:
                steps[what[0]](t + ahead[what[0]], (p + ahead[what[0]]) % 2, int(what[1]))

    for kinds, u in (("A", 0), ("V", 0), ("A", 1), ("BC", 0), ("V", 1), ("A", 2)):
        for what in DELTA_ORDER:
            if what[0] in kinds and steps[what[0]] is not None:
                steps[what[0]](u, u % 2, int(what[1]))
    in_loop = (TILES - ahead["A"]) // 2
    with eng.Fori(0, in_loop) as i:
        body(2 * i, 0)
        body(2 * i + 1, 1)
    for t in range(2 * in_loop, TILES):
        body(t, t % 2, left=TILES - t)


def delta_output(nc, res, a):
    with ExitStack() as ctx:
        st = Stage(nc, ctx, "dout")
        wo, rms_w = st.sb("wo", [P, KC, DIM]), st.sb("rms_w", [P, 1])
        root, scale = st.sb("root", [P, TILES, D_HEADS]), st.sb("scale", [P, TILES, D_HEADS])
        normed = [st.sb(f"normed{i}", [P, PAIR, DIM]) for i in range(2)]
        normedT = [st.sb(f"normedT{i}", [P, PAIR, KC, P]) for i in range(2)]
        turn_ps, out_ps = ([st.ps(f"{n}{i}") for i in range(2)] for n in ("turn", "out"))
        s_w, s_mean, s_root, s_scale = (st.sem(n) for n in ("weights", "mean", "root", "scale"))
        s_normed, s_turn, s_normedT, s_out, s_x, s_stats = (st.sem(n) for n in ("normed", "turn", "normedT", "out", "x", "stats"))
        with nc.Block() as block:
            @block.sync
            def _(sp):
                sp.dma_start(wo[:], a["L0_attn_Wo"].rearrange("(k p) n -> p k n", p=P)).then_inc(s_w, 16)
                sp.dma_start(rms_w[:], a["L0_attn_rms_w"]).then_inc(s_w, 16)
                sp.wait_ge(s_w, 32)

            @block.tensor
            def _(pe):
                def head(u, p):
                    pe.wait_ge(s_normed, u + 1)
                    for j in range(PAIR):
                        for k in range(KC):
                            at = (j * KC + k) * P
                            mm = nc.tensor.transpose(turn_ps[p][:, at:at + P], normed[p][:, j, k * P:(k + 1) * P], res.ident[:])
                    mm.then_inc(s_turn, 1)

                def tail(t, p):
                    pe.wait_ge(s_normedT, t + 1)
                    pe.wait_ge(s_x, t + 1)
                    for j in range(PAIR):
                        for k in range(KC):
                            mm = nc.tensor.matmul(out_ps[p][:, j * DIM:(j + 1) * DIM], normedT[p][:, j, k, :], wo[:, k, :],
                                                  start=k == 0, stop=k == KC - 1)
                    mm.then_inc(s_out, 1)

                pe.wait_ge(s_scale, KC + 1)
                two_at_a_time(pe, head, tail)

            @block.scalar
            def _(act):
                def head(u, p):
                    act.wait_ge(s_turn, u + 1)
                    nc.scalar.activation(normedT[p][:, :, :, :].rearrange("p j k q -> p (j k q)"), turn_ps[p][:, :],
                                         ACT.Copy).then_inc(s_normedT, 1)

                def tail(t, p):
                    pass

                act.wait_ge(s_mean, 1)
                nc.scalar.activation(root[:], scale[:], ACT.Sqrt).then_inc(s_root, 1)
                two_at_a_time(act, head, tail)

            @block.vector
            def _(dve):
                def head(u, p):
                    if not isinstance(u, int) or u > 1:
                        dve.wait_ge(s_out, u - 1)
                    nc.vector.tensor_tensor(
                        normed[p][:, :, :].rearrange("p j (h d) -> p (j h) d", h=D_HEADS),
                        pair_of(res.mixed, u).rearrange("p j (h d) -> p (j h) d", h=D_HEADS),
                        pair_of(scale, u).rearrange("p j h -> p (j h)").unsqueeze(2).to_broadcast([P, PAIR * D_HEADS, D_HEAD]),
                        ALU.mult).then_inc(s_normed, 1)

                def tail(t, p):
                    dve.wait_ge(s_out, t + 1)
                    nc.vector.tensor_tensor(pair_of(res.x, t), pair_of(res.x, t),
                                            out_ps[p][:, :].rearrange("p (j d) -> p j d", j=PAIR), ALU.add).then_inc(s_x, 1)
                    dve.wait_ge(s_x, 2 + t + 1)
                    for j in range(PAIR):
                        nc.vector.bn_stats(pair_rows(res.stats, t, j), pair_rows(res.x, t, j)).then_inc(s_stats, 1)

                dve.sem_inc(s_x, 2)
                nc.vector.tensor_scalar(scale[:], res.squares[:], 1.0 / D_HEAD, LN_EPS, ALU.mult, ALU.add).then_inc(s_mean, 1)
                dve.wait_ge(s_root, 1)
                nc.vector.reciprocal(scale[:], root[:]).then_inc(s_scale, 1)
                dve.wait_ge(s_w, 32)
                for k in range(KC):
                    nc.vector.tensor_scalar(wo[:, k, :], wo[:, k, :], rms_w[:, 0:1], None, ALU.mult).then_inc(s_scale, 1)
                dve.wait_ge(s_scale, KC + 1)
                two_at_a_time(dve, head, tail)
                dve.wait_ge(s_stats, TILES)


EXPERTS, FFN_HEAD = 16, 128
CHUNKS = 4
PER_CHUNK = EXPERTS // CHUNKS
TINY = 1e-12
BELOW_ALL = 1.0e30


def top_two(nc, dve_step, logits, first, second, work, rank, shape):
    peak, best, score = work
    wide = lambda m: m.unsqueeze(2).to_broadcast(shape)
    ranks = rank.unsqueeze(1).to_broadcast(shape)
    source = logits
    for chosen in (first, second):
        dve_step(nc.vector.tensor_reduce(peak, source, AX.X, ALU.max))
        dve_step(nc.vector.tensor_tensor(score, source, wide(peak), ALU.is_equal))
        dve_step(nc.vector.tensor_tensor(score, score, ranks, ALU.mult))
        dve_step(nc.vector.tensor_reduce(best, score, AX.X, ALU.max))
        dve_step(nc.vector.tensor_tensor(chosen, ranks, wide(best), ALU.is_equal))
        if chosen is first:
            dve_step(nc.vector.scalar_tensor_tensor(score, first, -BELOW_ALL, logits, ALU.mult, ALU.add))
            dve_step(nc.vector.tensor_copy(second, score))
            source = second


SWITCH_LOADS = 4


def load_switch(sp, res, a):
    for n, name in enumerate("qkv"):
        sp.dma_start(res.wqkv[:, :, :, n * FFN_HEAD:(n + 1) * FFN_HEAD],
                     a[f"L0_ffn_{name}_proj"].rearrange("e (k p) h -> p (e k) h", p=P)).then_inc(res.switch_loaded, 16)
    sp.dma_start(res.wo[:], a["L0_ffn_o_proj"].rearrange("e h c -> h e c")).then_inc(res.switch_loaded, 16)


def switch_router(nc, res, a):
    with ExitStack() as ctx:
        st = Stage(nc, ctx, "router")
        sim, sim_sq = st.sb("sim", [P, KC, EXPERTS]), st.sb("sim_sq", [P, KC, EXPERTS])
        sim_norm, gates, rank = (st.sb(n, [P, EXPERTS]) for n in ("sim_norm", "gates", "rank"))
        row_norm = st.sb("row_norm", [P, TILES])
        xn = [st.sb(f"xn{i}", [P, PAIR, DIM]) for i in range(2)]
        xnT = [st.sb(f"xnT{i}", [P, PAIR, KC, P]) for i in range(2)]
        logits, active, one, two, score, dots = (st.sb(n, [P, TILES, EXPERTS]) for n in
                                                 ("logits", "active", "one", "two", "score", "dots"))
        peak, best, inactive = (st.sb(n, [P, TILES]) for n in ("peak", "best", "inactive"))
        turn_ps = [st.ps(f"turn{i}") for i in range(2)]
        logit_ps = [st.ps(f"logit{i}") for i in range(2)]
        sim_ps = st.ps("simsum")
        s_w, s_var, s_std, s_rstd, s_chain = (st.sem(n) for n in ("weights", "var", "std", "rstd", "vector_step"))
        s_simsq, s_simps, s_normsq, s_norm, s_sim = (st.sem(n) for n in ("simsq", "simps", "normsq", "norm", "sim"))
        s_xn, s_turn, s_xnT, s_logit, s_dots = (st.sem(n) for n in ("xn", "turn", "xnT", "logit", "dots"))
        s_step, s_shift, s_exp = (st.sem(n) for n in ("route_step", "shifted", "exp"))
        with nc.Block() as block:
            @block.sync
            def _(sp):
                sp.dma_start(sim[:], a["L0_ffn_sim_matrix"].rearrange("(k p) e -> p k e", p=P)).then_inc(s_w, 16)
                sp.dma_start(gates[:], a["L0_ffn_gates"].to_broadcast([P, EXPERTS])).then_inc(s_w, 16)
                sp.dma_start(rank[:], a["rank16"].to_broadcast([P, EXPERTS])).then_inc(s_w, 16)
                sp.wait_ge(s_w, 48)

            @block.tensor
            def _(pe):
                def head(u, p):
                    pe.wait_ge(s_xn, u + 1)
                    for j in range(PAIR):
                        for k in range(KC):
                            at = (j * KC + k) * P
                            mm = nc.tensor.transpose(turn_ps[p][:, at:at + P], xn[p][:, j, k * P:(k + 1) * P], res.ident[:])
                    mm.then_inc(s_turn, 1)

                def tail(t, p):
                    pe.wait_ge(s_xnT, t + 1)
                    pe.wait_ge(s_dots, t + 1)
                    for j in range(PAIR):
                        for k in range(KC):
                            mm = nc.tensor.matmul(logit_ps[p][:, j * EXPERTS:(j + 1) * EXPERTS], xnT[p][:, j, k, :], sim[:, k, :],
                                                  start=k == 0, stop=k == KC - 1)
                    mm.then_inc(s_logit, 1)

                pe.wait_ge(s_simsq, 1)
                for k in range(KC):
                    mm = nc.tensor.matmul(sim_ps[:, 0:EXPERTS], res.ones[:], sim_sq[:, k, :], start=k == 0, stop=k == KC - 1)
                mm.then_inc(s_simps, 1)
                pe.wait_ge(s_sim, 2)
                two_at_a_time(pe, head, tail)

            @block.scalar
            def _(act):
                def head(u, p):
                    act.wait_ge(s_turn, u + 1)
                    nc.scalar.activation(xnT[p][:, :, :, :].rearrange("p j k q -> p (j k q)"), turn_ps[p][:, :],
                                         ACT.Copy).then_inc(s_xnT, 1)

                def tail(t, p):
                    pass

                norm_scales_scalar(nc, res, act, s_var, s_std)
                act.wait_ge(s_normsq, 2)
                nc.scalar.activation(sim_norm[:], sim_norm[:], ACT.Sqrt).then_inc(s_norm, 1)
                nc.scalar.activation(row_norm[:], row_norm[:], ACT.Sqrt).then_inc(s_norm, 1)
                two_at_a_time(act, head, tail)
                act.wait_ge(s_w, 48)
                nc.scalar.activation(gates[:], gates[:], ACT.Tanh, scale=0.5).then_inc(s_norm, 1)
                act.wait_ge(s_shift, 1)
                nc.scalar.activation(score[:], score[:], ACT.Exp).then_inc(s_exp, 1)

            @block.vector
            def _(dve):
                def head(u, p):
                    if not isinstance(u, int) or u > 1:
                        dve.wait_ge(s_turn, u - 1)
                    for j in range(PAIR):
                        ins = nc.vector.tensor_scalar(xn[p][:, j, :], pair_rows(res.x, u, j),
                                                      pair_rows(res.mean_var, u, j)[:, 0:1], pair_rows(res.rstd, u, j),
                                                      ALU.subtract, ALU.mult)
                    ins.then_inc(s_xn, 1)

                def tail(t, p):
                    dve.wait_ge(s_logit, t + 1)
                    nc.vector.tensor_copy(pair_of(dots, t), logit_ps[p][:, 0:PAIR * EXPERTS].rearrange("p (j e) -> p j e", j=PAIR)
                                          ).then_inc(s_dots, 1)

                norm_scales_vector(nc, res, Chain(dve, s_chain), s_var, s_std, s_rstd)
                dve.sem_inc(s_dots, 2)
                dve.wait_ge(s_w, 48)
                nc.vector.tensor_tensor(sim_sq[:], sim[:], sim[:], ALU.mult).then_inc(s_simsq, 1)
                dve.wait_ge(s_simps, 1)
                nc.vector.tensor_scalar(sim_norm[:], sim_ps[:, 0:EXPERTS], TINY, None, ALU.add).then_inc(s_normsq, 1)
                step = Chain(dve, s_step)

                def dve_step(ins):
                    step.step(ins)
                    step.settle()

                dve_step(nc.vector.tensor_tensor(row_norm[:], res.rstd[:, :, 0], res.rstd[:, :, 0], ALU.mult))
                dve_step(nc.vector.tensor_tensor(row_norm[:], row_norm[:], res.mean_var[:, :, 1], ALU.mult))
                nc.vector.tensor_scalar(row_norm[:], row_norm[:], float(DIM), TINY, ALU.mult, ALU.add).then_inc(s_normsq, 1)
                dve.wait_ge(s_norm, 2)
                dve_step(nc.vector.reciprocal(sim_norm[:], sim_norm[:]))
                dve_step(nc.vector.reciprocal(row_norm[:], row_norm[:]))
                for k in range(KC):
                    nc.vector.tensor_tensor(sim[:, k, :], sim[:, k, :], sim_norm[:], ALU.mult).then_inc(s_sim, 1)
                two_at_a_time(dve, head, tail)
                dve.wait_ge(s_dots, 2 + PAIRS_OF_TILES)
                shape = [P, TILES, EXPERTS]
                wide = lambda m: m[:, :].unsqueeze(2).to_broadcast(shape)
                dve_step(nc.vector.tensor_tensor(dots[:], dots[:], wide(row_norm), ALU.mult))
                dve.wait_ge(s_norm, 3)
                dve_step(nc.vector.tensor_scalar(gates[:], gates[:], 0.5, 0.5, ALU.mult, ALU.add))
                dve_step(nc.vector.tensor_tensor(logits[:], dots[:], gates[:].unsqueeze(1).to_broadcast(shape), ALU.subtract))
                top_two(nc, dve_step, logits[:], one[:], two[:], (peak[:], best[:], score[:]), rank[:], shape)
                dve_step(nc.vector.tensor_scalar(active[:], logits[:], 0.0, None, ALU.is_gt))
                dve_step(nc.vector.tensor_reduce(peak[:], active[:], AX.X, ALU.max))
                dve_step(nc.vector.tensor_scalar(inactive[:], peak[:], -1.0, 1.0, ALU.mult, ALU.add))
                dve_step(nc.vector.tensor_tensor(one[:], one[:], two[:], ALU.add))
                dve_step(nc.vector.tensor_tensor(one[:], one[:], wide(inactive), ALU.mult))
                dve_step(nc.vector.tensor_tensor(active[:], active[:], one[:], ALU.add))
                dve_step(nc.vector.tensor_scalar(score[:], logits[:], 0.0, None, ALU.max))
                dve_step(nc.vector.tensor_reduce(peak[:], score[:], AX.X, ALU.max))
                nc.vector.tensor_tensor(score[:], score[:], wide(peak), ALU.subtract).then_inc(s_shift, 1)
                dve.wait_ge(s_exp, 1)
                dve_step(nc.vector.tensor_tensor(score[:], score[:], active[:], ALU.mult))
                dve_step(nc.vector.tensor_reduce(best[:], score[:], AX.X, ALU.add))
                dve_step(nc.vector.reciprocal(best[:], best[:]))
                dve_step(nc.vector.tensor_tensor(res.route[:], score[:], wide(best), ALU.mult))


SWITCH_ORDER = ["X", "R0", "R1", "Ta", "R2", "R3", "Tb", "M0", "Tc", "M1", "Td", "M2", "M3", "To"]


def switch_attention(nc, res, a):
    with ExitStack() as ctx:
        st = Stage(nc, ctx, "switch")
        wqkv, wo = res.wqkv, res.wo
        causal = st.sb("causal", [P, P])
        xn, xnT = st.sb("xn", [P, DIM]), st.sb("xnT", [P, KC, P])
        diag = st.sb("diag", [P, EXPERTS, P])
        spread = [st.sb(f"spread{i}", [P, EXPERTS, P]) for i in range(2)]
        scaled = st.sb("scaled", [P, EXPERTS, KC, P])
        qkv, qkT, masked, probs, probsT = (st.sb("qkv", [P, 3 * FFN_HEAD]), st.sb("qkT", [P, 2 * P]), st.sb("masked", [P, P]),
                                           st.sb("probs", [P, P]), st.sb("probsT", [P, P]))
        negpeak, total, inverse = st.sb("negpeak", [P, 1]), st.sb("total", [P, 1]), st.sb("inverse", [P, 1])
        mixed = st.sb("mixed", [P, EXPERTS, P])
        x_ps, qkv_ps, a_ps, b_ps, out_ps = (st.ps(n) for n in ("x", "qkv", "a", "b", "out"))
        r_ps = [st.ps(f"r{i}") for i in range(2)]
        s_w, s_var, s_std, s_rstd, s_chain = (st.sem(n) for n in ("weights", "var", "std", "rstd", "vector_step"))
        s_xn, s_turn, s_xnT, s_diag = (st.sem(n) for n in ("xn", "turn", "xnT", "diag"))
        s_r, s_spread, s_scaled, s_qkv, s_qkv_sb = (st.sem(n) for n in ("r_full", "spread", "scaled", "qkv_full", "qkv_copied"))
        s_qk, s_qkT, s_score, s_tail, s_peak, s_exp = (st.sem(n) for n in ("qk_turned", "qkT", "score", "tail_step", "peak", "exp"))
        s_probs, s_pt, s_probsT, s_head, s_mixed = (st.sem(n) for n in ("probs", "p_turned", "probsT", "head", "mixed"))
        s_out, s_x, s_stats, s_inverse = st.sem("out"), st.sem("x"), st.sem("stats"), st.sem("inverse")

        def loop(eng, prep, tail):
            def body(t, p, last=False):
                for what in SWITCH_ORDER:
                    if what[0] == "T":
                        tail(t, p, what[1])
                    elif not last:
                        prep(t + 1, 1 - p, what)

            for what in SWITCH_ORDER:
                if what[0] != "T":
                    prep(0, 0, what)
            with eng.Fori(0, TILES // 2 - 1) as i:
                body(2 * i, 0)
                body(2 * i + 1, 1)
            body(TILES - 2, 0)
            body(TILES - 1, 1, last=True)

        with nc.Block() as block:
            @block.sync
            def _(sp):
                sp.dma_start(causal[:], a["causal"]).then_inc(s_w, 16)
                sp.wait_ge(s_w, 16)

            @block.tensor
            def _(pe):
                def prep(u, p, what):
                    if what == "X":
                        pe.wait_ge(s_xn, u + 1)
                        for k in range(KC):
                            mm = nc.tensor.transpose(x_ps[:, k * P:(k + 1) * P], xn[:, k * P:(k + 1) * P], res.ident[:])
                        mm.then_inc(s_turn, 1)
                    elif what[0] == "R":
                        c = int(what[1])
                        if c == 0:
                            pe.wait_ge(s_diag, u + 1)
                        pe.wait_ge(s_spread, CHUNKS * u + c + 1)
                        nc.tensor.matmul(r_ps[c % 2][:, :], res.ones[:],
                                         diag[:, c * PER_CHUNK:(c + 1) * PER_CHUNK, :].rearrange("p e q -> p (e q)"),
                                         start=True, stop=True).then_inc(s_r, 1)
                    else:
                        c = int(what[1])
                        pe.wait_ge(s_scaled, CHUNKS * u + c + 1)
                        if c == 0:
                            pe.wait_ge(s_qkv_sb, u)
                        for e in range(c * PER_CHUNK, (c + 1) * PER_CHUNK):
                            for k in range(KC):
                                mm = nc.tensor.matmul(qkv_ps[:, 0:3 * FFN_HEAD], scaled[:, e, k, :], wqkv[:, e, k, :],
                                                      start=e == 0 and k == 0, stop=e == EXPERTS - 1 and k == KC - 1)
                        mm.then_inc(s_qkv, 1)

                def tail(t, p, what):
                    if what == "a":
                        pe.wait_ge(s_qkv_sb, t + 1)
                        for n in range(2):
                            mm = nc.tensor.transpose(a_ps[:, n * P:(n + 1) * P], qkv[:, n * P:(n + 1) * P], res.ident[:])
                        mm.then_inc(s_qk, 1)
                    elif what == "b":
                        pe.wait_ge(s_qkT, t + 1)
                        nc.tensor.matmul(a_ps[:, 2 * P:3 * P], qkT[:, 0:P], qkT[:, P:2 * P], start=True, stop=True).then_inc(s_score, 1)
                    elif what == "c":
                        pe.wait_ge(s_probs, t + 1)
                        nc.tensor.transpose(b_ps[:, 0:P], probs[:, :], res.ident[:]).then_inc(s_pt, 1)
                    elif what == "d":
                        pe.wait_ge(s_probsT, t + 1)
                        nc.tensor.matmul(b_ps[:, P:2 * P], qkv[:, 2 * P:3 * P], probsT[:, :], start=True, stop=True).then_inc(s_head, 1)
                    else:
                        pe.wait_ge(s_mixed, t + 1)
                        pe.wait_ge(s_x, t)
                        for e in range(EXPERTS):
                            mm = nc.tensor.matmul(out_ps[:, 0:DIM], mixed[:, e, :], wo[:, e, :], start=e == 0, stop=e == EXPERTS - 1)
                        mm.then_inc(s_out, 1)

                pe.wait_ge(res.switch_loaded, 16 * SWITCH_LOADS)
                loop(pe, prep, tail)

            @block.scalar
            def _(act):
                def prep(u, p, what):
                    if what == "X":
                        act.wait_ge(s_turn, u + 1)
                        act.wait_ge(s_scaled, CHUNKS * u)
                        nc.scalar.activation(xnT[:, :, :].rearrange("p k q -> p (k q)"), x_ps[:, 0:DIM], ACT.Copy).then_inc(s_xnT, 1)
                    elif what[0] == "R":
                        c = int(what[1])
                        act.wait_ge(s_r, CHUNKS * u + c + 1)
                        if c == 0 and (not isinstance(u, int) or u > 1):
                            act.wait_ge(s_mixed, u - 1)
                        nc.scalar.activation(spread[p][:, c * PER_CHUNK:(c + 1) * PER_CHUNK, :].rearrange("p e q -> p (e q)"),
                                             r_ps[c % 2][:, :], ACT.Copy).then_inc(s_spread, 1)
                    elif what == "M3":
                        act.wait_ge(s_qkv, CHUNKS * (u + 1))
                        act.wait_ge(s_head, u)
                        nc.scalar.activation(qkv[:, :], qkv_ps[:, 0:3 * FFN_HEAD], ACT.Copy).then_inc(s_qkv_sb, 1)

                def tail(t, p, what):
                    if what == "a":
                        act.wait_ge(s_qk, t + 1)
                        nc.scalar.activation(qkT[:, :], a_ps[:, 0:2 * P], ACT.Copy).then_inc(s_qkT, 1)
                    elif what == "b":
                        act.wait_ge(s_peak, t + 1)
                        nc.scalar.activation(probs[:, :], masked[:, :], ACT.Exp, bias=negpeak[:, 0:1], scale=FFN_HEAD ** -0.5,
                                             accum_out=total[:, 0:1]).then_inc(s_exp, 1)
                    elif what == "c":
                        act.wait_ge(s_pt, t + 1)
                        nc.scalar.activation(probsT[:, :], b_ps[:, 0:P], ACT.Copy).then_inc(s_probsT, 1)

                norm_scales_scalar(nc, res, act, s_var, s_std)
                loop(act, prep, tail)

            @block.gpsimd
            def _(pool):
                def prep(u, p, what):
                    if what == "X":
                        pool.wait_ge(s_r, CHUNKS * u)
                        nc.gpsimd.tensor_tensor(diag[:, :, :], res.ident[:, :].unsqueeze(1).to_broadcast([P, EXPERTS, P]),
                                                row(res.route, u).unsqueeze(2).to_broadcast([P, EXPERTS, P]),
                                                ALU.mult).then_inc(s_diag, 1)

                def tail(t, p, what):
                    pass

                loop(pool, prep, tail)

            @block.vector
            def _(dve):
                def prep(u, p, what):
                    if what == "X":
                        dve.wait_ge(s_turn, u)
                        normalise(nc, res, xn[:, :], u).then_inc(s_xn, 1)
                    elif what[0] == "R":
                        c = int(what[1])
                        part = slice(c * PER_CHUNK, (c + 1) * PER_CHUNK)
                        if c == 0:
                            dve.wait_ge(s_xnT, u + 1)
                        dve.wait_ge(s_spread, 2 + CHUNKS * u + c + 1)
                        dve.wait_ge(s_qkv, CHUNKS * u)
                        shape = [P, PER_CHUNK, KC, P]
                        nc.vector.tensor_tensor(scaled[:, part, :, :], xnT[:, :, :].unsqueeze(1).to_broadcast(shape),
                                                spread[p][:, part, :].unsqueeze(2).to_broadcast(shape), ALU.mult).then_inc(s_scaled, 1)

                def tail(t, p, what):
                    if what == "b":
                        step = Chain(dve, s_tail, 2 * t)
                        dve.wait_ge(s_score, t + 1)
                        step.step(nc.vector.tensor_tensor(masked[:, :], a_ps[:, 2 * P:3 * P], causal[:, :], ALU.add))
                        step.settle()
                        step.step(nc.vector.tensor_reduce(negpeak[:, :], masked[:, :], AX.X, ALU.max, negate=True))
                        step.settle()
                        nc.vector.tensor_scalar(negpeak[:, :], negpeak[:, :], FFN_HEAD ** -0.5, None, ALU.mult).then_inc(s_peak, 1)
                    elif what == "c":
                        dve.wait_ge(s_exp, t + 1)
                        nc.vector.reciprocal(inverse[:, :], total[:, :]).then_inc(s_inverse, 1)
                        dve.wait_ge(s_inverse, t + 1)
                        nc.vector.tensor_scalar(probs[:, :], probs[:, :], inverse[:, 0:1], None, ALU.mult).then_inc(s_probs, 1)
                    elif what == "d":
                        dve.wait_ge(s_head, t + 1)
                        dve.wait_ge(s_out, t)
                        nc.vector.tensor_tensor(mixed[:, :, :], b_ps[:, P:2 * P].unsqueeze(1).to_broadcast([P, EXPERTS, P]),
                                                spread[p][:, :, :], ALU.mult).then_inc(s_mixed, 1)
                    elif what == "o":
                        dve.wait_ge(s_out, t + 1)
                        nc.vector.tensor_tensor(row(res.x, t), row(res.x, t), out_ps[:, 0:DIM], ALU.add).then_inc(s_x, 1)
                        dve.wait_ge(s_x, t + 1)
                        nc.vector.bn_stats(row(res.stats, t), row(res.x, t)).then_inc(s_stats, 1)

                norm_scales_vector(nc, res, Chain(dve, s_chain), s_var, s_std, s_rstd)
                dve.sem_inc(s_spread, 2)
                dve.wait_ge(s_w, 16)
                loop(dve, prep, tail)
                dve.wait_ge(s_stats, TILES)


def self_attention(nc, res, a, prefetch):
    with ExitStack() as ctx:
        st = Stage(nc, ctx, "self")
        block_mask = st.sb("block_mask", [P, P])
        xn = [st.sb(f"xn{i}", [P, PAIR, DIM]) for i in range(2)]
        xnT = [st.sb(f"xnT{i}", [P, PAIR, KC, P]) for i in range(2)]
        masked = [st.sb(f"masked{i}", [P, PAIR, P]) for i in range(2)]
        probs = [st.sb(f"probs{i}", [P, PAIR, P]) for i in range(2)]
        negpeak, total, inverse = (st.sb(n, [P, PAIR]) for n in ("negpeak", "total", "inverse"))
        turn_ps, score_ps, out_ps = ([st.ps(f"{n}{i}") for i in range(2)] for n in ("turn", "score", "out"))
        s_mask, s_var, s_std, s_rstd, s_chain = (st.sem(n) for n in ("mask", "var", "std", "rstd", "vector_step"))
        s_xn, s_turn, s_xnT, s_score, s_tail = (st.sem(n) for n in ("xn", "turned", "xnT", "scores", "tail_step"))
        s_peak, s_exp, s_probs, s_out, s_x, s_stats = (st.sem(n) for n in ("peak", "exp", "probs", "out", "x", "stats"))
        with nc.Block() as block:
            @block.sync
            def _(sp):
                sp.dma_start(block_mask[:], a["block_mask"]).then_inc(s_mask, 16)
                prefetch(sp)
                sp.wait_ge(s_mask, 16)

            @block.tensor
            def _(pe):
                def head(u, p):
                    pe.wait_ge(s_xn, u + 1)
                    for j in range(PAIR):
                        for k in range(KC):
                            at = (j * KC + k) * P
                            mm = nc.tensor.transpose(turn_ps[p][:, at:at + P], xn[p][:, j, k * P:(k + 1) * P], res.ident[:])
                    mm.then_inc(s_turn, 1)
                    pe.wait_ge(s_xnT, u + 1)
                    for j in range(PAIR):
                        for k in range(KC):
                            mm = nc.tensor.matmul(score_ps[p][:, j * P:(j + 1) * P], xnT[p][:, j, k, :], xnT[p][:, j, k, :],
                                                  start=k == 0, stop=k == KC - 1)
                    mm.then_inc(s_score, 1)

                def tail(t, p):
                    pe.wait_ge(s_probs, t + 1)
                    for j in range(PAIR):
                        mm = nc.tensor.matmul(out_ps[p][:, j * DIM:(j + 1) * DIM], probs[p][:, j, :], xn[p][:, j, :],
                                              start=True, stop=True)
                    mm.then_inc(s_out, 1)

                two_at_a_time(pe, head, tail)

            @block.scalar
            def _(act):
                def head(u, p):
                    act.wait_ge(s_turn, u + 1)
                    nc.scalar.activation(xnT[p][:, :, :, :].rearrange("p j k q -> p (j k q)"), turn_ps[p][:, :],
                                         ACT.Copy).then_inc(s_xnT, 1)

                def tail(t, p):
                    act.wait_ge(s_peak, t + 1)
                    for j in range(PAIR):
                        ins = nc.scalar.activation(probs[p][:, j, :], masked[p][:, j, :], ACT.Exp,
                                                   bias=negpeak[:, j:j + 1], accum_out=total[:, j:j + 1])
                    ins.then_inc(s_exp, 1)

                norm_scales_scalar(nc, res, act, s_var, s_std)
                two_at_a_time(act, head, tail)

            @block.vector
            def _(dve):
                def head(u, p):
                    if not isinstance(u, int) or u >= 2:
                        dve.wait_ge(s_x, u - 1)
                    for j in range(PAIR):
                        ins = nc.vector.tensor_scalar(xn[p][:, j, :], pair_rows(res.x, u, j),
                                                      pair_rows(res.mean_var, u, j)[:, 0:1], pair_rows(res.rstd, u, j),
                                                      ALU.subtract, ALU.mult)
                    ins.then_inc(s_xn, 1)

                def tail(t, p):
                    chain = Chain(dve, s_tail, 2 * t)
                    dve.wait_ge(s_score, t + 1)
                    chain.step(nc.vector.tensor_tensor(
                        masked[p][:, :, :], score_ps[p][:, 0:PAIR * P].rearrange("p (j q) -> p j q", j=PAIR),
                        block_mask[:, :].unsqueeze(1).to_broadcast([P, PAIR, P]), ALU.add))
                    chain.settle()
                    nc.vector.tensor_reduce(negpeak[:, :], masked[p][:, :, :], AX.X, ALU.max, negate=True).then_inc(s_peak, 1)
                    dve.wait_ge(s_exp, t + 1)
                    chain.step(nc.vector.reciprocal(inverse[:, :], total[:, :]))
                    chain.settle()
                    nc.vector.tensor_tensor(probs[p][:, :, :], probs[p][:, :, :],
                                            inverse[:, :].unsqueeze(2).to_broadcast([P, PAIR, P]),
                                            ALU.mult).then_inc(s_probs, 1)
                    dve.wait_ge(s_out, t + 1)
                    nc.vector.tensor_tensor(pair_of(res.x, t), pair_of(res.x, t),
                                            out_ps[p][:, :].rearrange("p (j d) -> p j d", j=PAIR), ALU.add).then_inc(s_x, 1)
                    dve.wait_ge(s_x, t + 1)
                    for j in range(PAIR):
                        nc.vector.bn_stats(pair_rows(res.stats, t, j), pair_rows(res.x, t, j)).then_inc(s_stats, 1)

                norm_scales_vector(nc, res, Chain(dve, s_chain), s_var, s_std, s_rstd)
                dve.wait_ge(s_mask, 16)
                two_at_a_time(dve, head, tail)
                dve.wait_ge(s_stats, TILES)


MOE, HIDDEN, CHOSEN = 8, 1024, 2
FC = HIDDEN // P
ROW_TILES = -(-((CHOSEN * TOKENS + MOE * (P - 1)) // P) // 2) * 2
ROWS = ROW_TILES * P


def scan(nc, dve_step, a, b, n, at):
    step = 1
    while step < n:
        dve_step(nc.vector.tensor_copy(at(b, slice(0, step)), at(a, slice(0, step))))
        dve_step(nc.vector.tensor_tensor(at(b, slice(step, n)), at(a, slice(step, n)), at(a, slice(0, n - step)), ALU.add))
        a, b, step = b, a, 2 * step
    return a


def moe_router(nc, res, a, rows):
    with ExitStack() as ctx:
        st = Stage(nc, ctx, "gate")
        gate, rank = st.sb("gate", [P, KC, MOE]), st.sb("rank", [P, MOE])
        before, tile_row = st.sb("before", [P, P]), st.sb("tile_row", [P, ROW_TILES])
        zeros = st.sb("zeros", [P, DIM])
        xn = [st.sb(f"xn{i}", [P, PAIR, DIM]) for i in range(2)]
        xnT = [st.sb(f"xnT{i}", [P, PAIR, KC, P]) for i in range(2)]
        xn_all = st.sb("xn_all", [P, TILES, DIM])
        probs, one, two, score, both, count, count2, place = (
            st.sb(n, [P, TILES, MOE]) for n in ("probs", "one", "two", "score", "both", "count", "count2", "place"))
        peak, best = st.sb("peak", [P, TILES]), st.sb("best", [P, TILES])
        padded, ends, ends2, starts = (st.sb(n, [P, MOE]) for n in ("padded", "ends", "ends2", "starts"))
        padded_int = st.sb("padded_int", [P, MOE], I32)
        started, owner = st.sb("started", [P, ROW_TILES, MOE - 1]), st.sb("owner", [P, ROW_TILES])
        slot = st.sb("slot", [P, TILES])
        turn_ps = [st.ps(f"turn{i}") for i in range(2)]
        logit_ps = [st.ps(f"logit{i}") for i in range(2)]
        before_ps, all_ps = st.ps("before"), st.ps("all")
        s_w, s_var, s_std, s_rstd, s_chain = (st.sem(n) for n in ("weights", "var", "std", "rstd", "vector_step"))
        s_xn, s_turn, s_xnT, s_logit, s_dots = (st.sem(n) for n in ("xn", "turn", "xnT", "logit", "dots"))
        s_step, s_shift, s_exp, s_both, s_counts = (st.sem(n) for n in ("route_step", "shifted", "exp", "both", "counts"))
        s_zero, s_zeroed, s_slots, s_scattered = (st.sem(n) for n in ("zero", "zeroed", "slots", "scattered"))
        with nc.Block() as block:
            @block.sync
            def _(sp):
                sp.dma_start(gate[:], a["L1_ffn_gate_w"].rearrange("(k p) e -> p k e", p=P)).then_inc(s_w, 16)
                sp.dma_start(rank[:], a["rank8"].to_broadcast([P, MOE])).then_inc(s_w, 16)
                sp.dma_start(before[:], a["before"]).then_inc(s_w, 16)
                sp.dma_start(tile_row[:], a["tile_row"].to_broadcast([P, ROW_TILES])).then_inc(s_w, 16)
                sp.wait_ge(s_zero, 1)
                sp.dma_start(rows.rearrange("(t p) d -> p t d", p=P),
                             zeros[:, :].unsqueeze(1).to_broadcast([P, ROW_TILES, DIM])).then_inc(s_zeroed, 16)
                sp.wait_ge(s_w, 64)
                sp.wait_ge(s_zeroed, 16)

            @block.tensor
            def _(pe):
                def head(u, p):
                    pe.wait_ge(s_xn, u + 1)
                    for j in range(PAIR):
                        for k in range(KC):
                            at = (j * KC + k) * P
                            mm = nc.tensor.transpose(turn_ps[p][:, at:at + P], xn[p][:, j, k * P:(k + 1) * P], res.ident[:])
                    mm.then_inc(s_turn, 1)

                def tail(t, p):
                    pe.wait_ge(s_xnT, t + 1)
                    pe.wait_ge(s_dots, t + 1)
                    for j in range(PAIR):
                        for k in range(KC):
                            mm = nc.tensor.matmul(logit_ps[p][:, j * MOE:(j + 1) * MOE], xnT[p][:, j, k, :], gate[:, k, :],
                                                  start=k == 0, stop=k == KC - 1)
                    mm.then_inc(s_logit, 1)

                pe.wait_ge(s_w, 64)
                two_at_a_time(pe, head, tail)
                pe.wait_ge(s_both, 1)
                chosen = both[:, :, :].rearrange("p t e -> p (t e)")
                nc.tensor.matmul(before_ps[:, 0:P], before[:], chosen, start=True, stop=True)
                nc.tensor.matmul(all_ps[:, 0:P], res.ones[:], chosen, start=True, stop=True).then_inc(s_counts, 1)

            @block.scalar
            def _(act):
                def head(u, p):
                    act.wait_ge(s_turn, u + 1)
                    nc.scalar.activation(xnT[p][:, :, :, :].rearrange("p j k q -> p (j k q)"), turn_ps[p][:, :],
                                         ACT.Copy).then_inc(s_xnT, 1)

                def tail(t, p):
                    pass

                norm_scales_scalar(nc, res, act, s_var, s_std)
                two_at_a_time(act, head, tail)
                act.wait_ge(s_shift, 1)
                nc.scalar.activation(probs[:], probs[:], ACT.Exp).then_inc(s_exp, 1)

            @block.gpsimd
            def _(pool):
                pool.wait_ge(s_zeroed, 16)
                pool.wait_ge(s_slots, CHOSEN)
                for t in range(TILES):
                    for n in range(CHOSEN):
                        pool.indirect_dma_start(rows, bass.IndirectOffsetOnAxis(res.slots[:, n, t:t + 1], 0), xn_all[:, t, :],
                                                None).then_inc(s_scattered, 16)
                pool.wait_ge(s_scattered, 16 * CHOSEN * TILES)

            @block.vector
            def _(dve):
                def head(u, p):
                    if not isinstance(u, int) or u > 1:
                        dve.wait_ge(s_turn, u - 1)
                    for j in range(PAIR):
                        ins = nc.vector.tensor_scalar(xn[p][:, j, :], pair_rows(res.x, u, j),
                                                      pair_rows(res.mean_var, u, j)[:, 0:1], pair_rows(res.rstd, u, j),
                                                      ALU.subtract, ALU.mult)
                    ins.then_inc(s_xn, 1)
                    dve.wait_ge(s_xn, u + 1)
                    nc.vector.tensor_copy(pair_of(xn_all, u), xn[p][:, :, :])

                def tail(t, p):
                    dve.wait_ge(s_logit, t + 1)
                    nc.vector.tensor_copy(pair_of(probs, t), logit_ps[p][:, 0:PAIR * MOE].rearrange("p (j e) -> p j e", j=PAIR)
                                          ).then_inc(s_dots, 1)

                nc.vector.memset(zeros[:], 0.0).then_inc(s_zero, 1)
                norm_scales_vector(nc, res, Chain(dve, s_chain), s_var, s_std, s_rstd)
                dve.sem_inc(s_dots, 2)
                dve.wait_ge(s_w, 64)
                two_at_a_time(dve, head, tail)
                dve.wait_ge(s_dots, 2 + PAIRS_OF_TILES)
                step = Chain(dve, s_step)

                def dve_step(ins):
                    step.step(ins)
                    step.settle()

                shape = [P, TILES, MOE]
                wide = lambda m: m[:, :].unsqueeze(2).to_broadcast(shape)
                dve_step(nc.vector.tensor_reduce(peak[:], probs[:], AX.X, ALU.max))
                nc.vector.tensor_tensor(probs[:], probs[:], wide(peak), ALU.subtract).then_inc(s_shift, 1)
                dve.wait_ge(s_exp, 1)
                dve_step(nc.vector.tensor_reduce(best[:], probs[:], AX.X, ALU.add))
                dve_step(nc.vector.reciprocal(best[:], best[:]))
                dve_step(nc.vector.tensor_tensor(probs[:], probs[:], wide(best), ALU.mult))
                top_two(nc, dve_step, probs[:], one[:], two[:], (peak[:], best[:], score[:]), rank[:], shape)
                nc.vector.tensor_tensor(both[:], one[:], two[:], ALU.add).then_inc(s_both, 1)
                for n, chosen in enumerate((one, two)):
                    dve_step(nc.vector.tensor_tensor(score[:], probs[:], chosen[:], ALU.mult))
                    dve_step(nc.vector.tensor_reduce(res.weight[:, n, :], score[:], AX.X, ALU.add))
                dve_step(nc.vector.tensor_tensor(peak[:], res.weight[:, 0, :], res.weight[:, 1, :], ALU.add))
                dve_step(nc.vector.reciprocal(peak[:], peak[:]))
                for n in range(CHOSEN):
                    dve_step(nc.vector.tensor_tensor(res.weight[:, n, :], res.weight[:, n, :], peak[:], ALU.mult))
                dve.wait_ge(s_counts, 1)
                dve_step(nc.vector.tensor_copy(count[:].rearrange("p t e -> p (t e)"), all_ps[:, 0:P]))
                upto = scan(nc, dve_step, count, count2, TILES, lambda m, s: m[:, s, :])
                dve_step(nc.vector.tensor_scalar(padded_int[:], upto[:, TILES - 1, :], float(P - 1), None, ALU.add))
                shift = P.bit_length() - 1
                dve_step(nc.vector.tensor_scalar(padded_int[:], padded_int[:], shift, shift,
                                                 ALU.logical_shift_right, ALU.logical_shift_left))
                dve_step(nc.vector.tensor_copy(padded[:], padded_int[:]))
                dve_step(nc.vector.tensor_copy(ends[:], padded[:]))
                end = scan(nc, dve_step, ends, ends2, MOE, lambda m, s: m[:, s])
                dve_step(nc.vector.tensor_tensor(starts[:], end[:], padded[:], ALU.subtract))
                dve_step(nc.vector.tensor_tensor(place[:], upto[:], starts[:].unsqueeze(1).to_broadcast(shape), ALU.add))
                dve_step(nc.vector.tensor_tensor(place[:].rearrange("p t e -> p (t e)"), place[:].rearrange("p t e -> p (t e)"),
                                                 all_ps[:, 0:P], ALU.subtract))
                dve_step(nc.vector.tensor_tensor(place[:].rearrange("p t e -> p (t e)"), place[:].rearrange("p t e -> p (t e)"),
                                                 before_ps[:, 0:P], ALU.add))
                for n, chosen in enumerate((one, two)):
                    dve_step(nc.vector.tensor_tensor(score[:], place[:], chosen[:], ALU.mult))
                    dve_step(nc.vector.tensor_reduce(slot[:], score[:], AX.X, ALU.add))
                    nc.vector.tensor_copy(res.slots[:, n, :], slot[:]).then_inc(s_slots, 1)
                    dve.wait_ge(s_slots, n + 1)
                dve_step(nc.vector.tensor_tensor(started[:], starts[:, 1:].unsqueeze(1).to_broadcast([P, ROW_TILES, MOE - 1]),
                                                 tile_row[:].unsqueeze(2).to_broadcast([P, ROW_TILES, MOE - 1]), ALU.is_le))
                dve_step(nc.vector.tensor_reduce(owner[:], started[:], AX.X, ALU.add))
                dve_step(nc.vector.tensor_copy(res.owner[:], owner[:]))


MOE_ORDER = ["X1", "G0", "H1", "Y0"]


def moe_experts(nc, res, rows, outs):
    with ExitStack() as ctx:
        st = Stage(nc, ctx, "moe")
        xs = [st.sb(f"xs{i}", [P, DIM]) for i in range(2)]
        y = [st.sb(f"y{i}", [P, DIM]) for i in range(2)]
        xsT, hidden, hiddenT = st.sb("xsT", [P, KC, P]), st.sb("hidden", [P, HIDDEN]), st.sb("hiddenT", [P, FC, P])
        x_ps, y_ps = st.ps("x"), st.ps("y")
        h_ps, g_ps = ([st.ps(f"{n}{i}") for i in range(2)] for n in ("h", "g"))
        s_turn, s_xsT, s_h, s_hidden = (st.sem(n) for n in ("turn", "xsT", "h", "hidden"))
        s_g, s_hiddenT, s_y, s_y_sb = (st.sem(n) for n in ("g", "hiddenT", "y", "y_sb"))
        s_xs, s_stored = ([st.sem(f"{n}{i}") for i in range(2)] for n in ("xs", "stored"))

        def loop(eng, step):
            def body(j, p, last=False):
                for what in MOE_ORDER:
                    ahead = int(what[1])
                    if not (ahead and last):
                        step(j + ahead, (p + ahead) % 2, what[0])

            for what in MOE_ORDER:
                if what[1] == "1":
                    step(0, 0, what[0])
            with eng.Fori(0, ROW_TILES // 2 - 1) as i:
                body(2 * i, 0)
                body(2 * i + 1, 1)
            body(ROW_TILES - 2, 0)
            body(ROW_TILES - 1, 1, last=True)

        with nc.Block() as block:
            @block.sync
            def _(sp):
                source = rows.rearrange("(t p) d -> t p d", p=P)
                target = outs.rearrange("(t p) d -> t p d", p=P)

                def one_tile(m, j):
                    return m[j] if isinstance(j, int) else m[bass.ds(j, 1)].rearrange("a p d -> (a p) d")

                def load(j, p):
                    sp.dma_start(xs[p][:, :], one_tile(source, j)).then_inc(s_xs[p], 16)

                def store(j, p):
                    sp.dma_start(one_tile(target, j), y[p][:, :]).then_inc(s_stored[p], 16)

                for j in range(2):
                    load(j, j)
                with sp.Fori(0, ROW_TILES // 2 - 1) as i:
                    for p in range(2):
                        j = 2 * i + p
                        ahead, now, done = sp.snap(j + 2), sp.snap(j), sp.snap(j + 1)
                        sp.wait_ge(s_turn, done)
                        load(ahead, p)
                        sp.wait_ge(s_y_sb, done)
                        store(now, p)
                for j in (ROW_TILES - 2, ROW_TILES - 1):
                    sp.wait_ge(s_y_sb, j + 1)
                    store(j, j % 2)
                for p in range(2):
                    sp.wait_ge(s_stored[p], 16 * (ROW_TILES // 2))

            @block.tensor
            def _(pe):
                def step(j, p, what):
                    if what == "X":
                        pe.wait_ge(s_xs[p], 16 * (j // 2 + 1) if isinstance(j, int) else 8 * (j - p) + 16)
                        for k in range(KC):
                            mm = nc.tensor.transpose(x_ps[:, k * P:(k + 1) * P], xs[p][:, k * P:(k + 1) * P], res.ident[:])
                        mm.then_inc(s_turn, 1)
                    elif what == "H":
                        e = expert(j)
                        pe.wait_ge(s_xsT, j + 1)
                        for n in range(2):
                            pe.wait_ge(s_hidden, 2 * j + n)
                            for k in range(KC):
                                mm = nc.tensor.matmul(h_ps[n][:, :], xsT[:, k, :],
                                                      res.w1[:, bass.ds(e * KC + k, 1), n * 512:(n + 1) * 512].rearrange("p a f -> p (a f)"),
                                                      start=k == 0, stop=k == KC - 1)
                            mm.then_inc(s_h, 1)
                    elif what == "G":
                        for n in range(2):
                            pe.wait_ge(s_hidden, 2 * j + n + 1)
                            pe.wait_ge(s_hiddenT, 2 * j)
                            for f in range(4):
                                at = n * 4 + f
                                mm = nc.tensor.transpose(g_ps[n][:, f * P:(f + 1) * P], hidden[:, at * P:(at + 1) * P], res.ident[:])
                            mm.then_inc(s_g, 1)
                    else:
                        e = expert(j)
                        pe.wait_ge(s_hiddenT, 2 * (j + 1))
                        pe.wait_ge(s_y_sb, j)
                        for f in range(FC):
                            mm = nc.tensor.matmul(y_ps[:, 0:DIM], hiddenT[:, f, :],
                                                  res.w2[:, bass.ds(e * FC + f, 1), :].rearrange("p a d -> p (a d)"),
                                                  start=f == 0, stop=f == FC - 1)
                        mm.then_inc(s_y, 1)

                def expert(j):
                    at = res.owner[0:1, j:j + 1] if isinstance(j, int) else res.owner[0:1, bass.ds(j, 1)]
                    return pe.value_load(at, min_val=0, max_val=MOE - 1)

                pe.wait_ge(res.moe_loaded, 32)
                loop(pe, step)

            @block.scalar
            def _(act):
                def step(j, p, what):
                    if what == "X":
                        act.wait_ge(s_turn, j + 1)
                        nc.scalar.activation(xsT[:, :, :].rearrange("p k q -> p (k q)"), x_ps[:, 0:DIM], ACT.Copy).then_inc(s_xsT, 1)
                    elif what == "H":
                        for n in range(2):
                            act.wait_ge(s_h, 2 * j + n + 1)
                            act.wait_ge(s_g, 2 * j)
                            nc.scalar.activation(hidden[:, n * 512:(n + 1) * 512], h_ps[n][:, :],
                                                 ACT.Gelu_apprx_tanh).then_inc(s_hidden, 1)

                loop(act, step)

            @block.vector
            def _(dve):
                def step(j, p, what):
                    if what == "G":
                        for n in range(2):
                            dve.wait_ge(s_g, 2 * j + n + 1)
                            dve.wait_ge(s_y, j)
                            nc.vector.tensor_copy(hiddenT[:, n * 4:(n + 1) * 4, :].rearrange("p f q -> p (f q)"),
                                                  g_ps[n][:, :]).then_inc(s_hiddenT, 1)
                    elif what == "Y":
                        dve.wait_ge(s_y, j + 1)
                        dve.wait_ge(s_stored[p], 16 * (j // 2) if isinstance(j, int) else 8 * (j - p))
                        nc.vector.tensor_copy(y[p][:, :], y_ps[:, 0:DIM]).then_inc(s_y_sb, 1)

                loop(dve, step)


def moe_combine(nc, res, outs, out):
    with ExitStack() as ctx:
        st = Stage(nc, ctx, "mix")
        DEEP = 4
        got = [[st.sb(f"got{i}{n}", [P, DIM]) for n in range(CHOSEN)] for i in range(DEEP)]
        s_got = [st.sem(f"got{i}") for i in range(DEEP)]
        s_first, s_mixed, s_out = st.sem("first"), st.sem("mixed"), st.sem("out")
        with nc.Block() as block:
            @block.gpsimd
            def _(pool):
                for t in range(TILES):
                    if t >= DEEP:
                        pool.wait_ge(s_mixed, t - DEEP + 1)
                    for n in range(CHOSEN):
                        pool.indirect_dma_start(got[t % DEEP][n][:, :], None, outs,
                                                bass.IndirectOffsetOnAxis(res.slots[:, n, t:t + 1], 0)).then_inc(s_got[t % DEEP], 16)

            @block.vector
            def _(dve):
                for t in range(TILES):
                    dve.wait_ge(s_got[t % DEEP], 16 * CHOSEN * (t // DEEP + 1))
                    nc.vector.scalar_tensor_tensor(res.x[:, t, :], got[t % DEEP][0][:, :], res.weight[:, 0, t:t + 1],
                                                   res.x[:, t, :], ALU.mult, ALU.add).then_inc(s_first, 1)
                    dve.wait_ge(s_first, t + 1)
                    nc.vector.scalar_tensor_tensor(res.x[:, t, :], got[t % DEEP][1][:, :], res.weight[:, 1, t:t + 1],
                                                   res.x[:, t, :], ALU.mult, ALU.add).then_inc(s_mixed, 1)

            @block.sync
            def _(sp):
                target = out.rearrange("(t p) d -> p t d", p=P)
                for t in range(0, TILES, 4):
                    sp.wait_ge(s_mixed, t + 4)
                    sp.dma_start(target[:, t:t + 4, :], res.x[:, t:t + 4, :]).then_inc(s_out, 16)
                sp.wait_ge(s_out, 16 * (TILES // 4))


def load_experts(sp, res, a, which):
    if which == 0:
        sp.dma_start(res.w1[:], a["L1_ffn_w1"].rearrange("e (k p) f -> p (e k) f", p=P)).then_inc(res.moe_loaded, 16)
    else:
        sp.dma_start(res.w2[:], a["L1_ffn_w2"].rearrange("e (k p) d -> p (e k) d", p=P)).then_inc(res.moe_loaded, 16)


def store_residual(nc, res, out):
    with ExitStack() as ctx:
        st = Stage(nc, ctx, "store")
        s_out = st.sem("out")
        with nc.Block() as block:
            @block.sync
            def _(sp):
                sp.dma_start(out.rearrange("(t p) d -> p t d", p=P), res.x[:]).then_inc(s_out, 16)
                sp.wait_ge(s_out, 16)


def perceiver(nc, a, out, stages=("x0", "d", "s", "x1", "e", "f")):
    with ExitStack() as ctx:
        st = Stage(nc, ctx, "res")
        res = Resident()
        res.x = st.sb("x", [P, TILES, DIM])
        res.stats = st.sb("stats", [P, TILES, 6])
        res.mean_var = st.sb("mean_var", [P, TILES, 2])
        res.std, res.rstd = st.sb("std", [P, TILES]), st.sb("rstd", [P, TILES, 1])
        res.ident, res.ones = st.sb("ident", [P, P]), st.sb("ones", [P, P])
        load_residual(nc, res, a["x"], a)

        def cross(layer, mask, prefetch=None):
            w = {n: a[f"L{layer}_xattn_{n}"] for n in ("Wq", "Wk", "Wv", "Wo", "bq", "bk", "bv", "bo")}
            w["headmask"], w["parmask"] = a["headmask"], a["parmask"]
            cross_attention(nc, res, f"x{layer}", a["ctx"], w, mask, prefetch)

        if "x0" in stages:
            cross(0, a["mask"])
        if "d" in stages or "s" in stages:
            with ExitStack() as layer:
                held = Stage(nc, layer, "switch_held")
                res.wqkv, res.wo = held.sb("wqkv", [P, EXPERTS, KC, 3 * FFN_HEAD]), held.sb("wo", [P, EXPERTS, DIM])
                res.switch_loaded = held.sem("switch_loaded")
                if "d" in stages:
                    with ExitStack() as inner:
                        between = Stage(nc, inner, "held")
                        res.mixed, res.squares = between.sb("mixed", [P, TILES, DIM]), between.sb("squares", [P, TILES, D_HEADS])
                        delta_rule(nc, res, a, lambda sp: load_switch(sp, res, a))
                        delta_output(nc, res, a)
                if "s" in stages:
                    with ExitStack() as inner:
                        res.route = Stage(nc, inner, "held").sb("route", [P, TILES, EXPERTS])
                        switch_router(nc, res, a)
                        switch_attention(nc, res, a)
        moe = Stage(nc, ctx, "moe_held")
        res.moe_loaded = moe.sem("moe_loaded")
        res.w1 = moe.sb("w1", [P, MOE * KC, HIDDEN])
        if "x1" in stages:
            cross(1, None, lambda sp: load_experts(sp, res, a, 0))
        if "e" in stages:
            res.w2 = moe.sb("w2", [P, MOE * FC, DIM])
            self_attention(nc, res, a, lambda sp: load_experts(sp, res, a, 1))
        if "f" in stages:
            res.slots, res.weight = moe.sb("slots", [P, CHOSEN, TILES], U32), moe.sb("weight", [P, CHOSEN, TILES])
            res.owner = moe.sb("owner", [P, ROW_TILES], I32)
            rows = nc.dram_tensor("rows", (ROWS, DIM), F32, kind="Internal").ap()
            outs = nc.dram_tensor("outs", (ROWS, DIM), F32, kind="Internal").ap()
            moe_router(nc, res, a, rows)
            moe_experts(nc, res, rows, outs)
            moe_combine(nc, res, outs, out)
        else:
            store_residual(nc, res, out)


def constants():
    import numpy as np
    c = np.arange(P)
    head = (c[:, None] // HEAD == np.arange(HALF_HEADS)[None, :]) * HEAD ** -0.5
    par = (c[:, None] // HEAD) % 2 == np.arange(2)[None, :]
    batch = c // SEQ
    block_mask = np.where(batch[:, None] == batch[None, :], 0.0, LOWEST)
    row_, col = c[:, None], c[None, :]
    same = batch[:, None] == batch[None, :]

    def join(size):
        return (row_ // (2 * size) == col // (2 * size)) & (row_ // size % 2 == 1) & (col // size % 2 == 0)

    causal = np.where(same & (row_ >= col), 0.0, LOWEST)
    delta = {"before": row_ < col, "rank8": np.arange(MOE, 0, -1)[None, :], "tile_row": P * np.arange(ROW_TILES)[None, :],
             "causal": causal, "rank16": np.arange(EXPERTS, 0, -1)[None, :], "head_ones": c[:, None] // D_HEAD == np.arange(2)[None, :], "strict": same & (row_ > col),
             "causalT": same & (row_ <= col), "join1": join(1), "join1T": join(1).T,
             "joinT": np.stack([join(n).T for n in LEVELS], axis=1)}
    return {k: v.astype(np.float32) for k, v in delta.items()} | {"block_mask": block_mask.astype(np.float32), "ident": np.eye(P, dtype=np.float32), "headmask": head.astype(np.float32), "parmask": par.astype(np.float32)}


def laid_out(inputs):
    import numpy as np
    a = {k: np.ascontiguousarray(v) for k, v in inputs.items()}
    out = {"x": a["x"].reshape(TOKENS, DIM), "ctx": a["ctx_1024"].reshape(BATCH * KEYS, DIM),
           "mask": a["mask_1x1xSxS2_ik0"].reshape(SEQ, KEYS)}
    for layer in range(2):
        pre = f"L{layer}_xattn_"
        for n in ("Wq", "Wk", "Wv", "Wo"):
            out[pre + n] = a[pre + n].T if layer == 0 else a[pre + n]
        for n in ("bq", "bk", "bv"):
            out[pre + n] = a[pre + n].reshape(KC, P).T
        out[pre + "bo"] = a[pre + "bo"].reshape(1, DIM)
    for n in ("Wq", "Wk", "Wv", "Wb", "Wo"):
        out["L0_attn_" + n] = a["L0_attn_" + n]
    for n in ("q_proj", "k_proj", "v_proj", "o_proj", "sim_matrix"):
        out["L0_ffn_" + n] = a["L0_ffn_" + n]
    for n in ("gate_w", "w1", "w2"):
        out["L1_ffn_" + n] = a["L1_ffn_" + n]
    out["L0_ffn_gates"] = a["L0_ffn_gates"].reshape(1, EXPERTS)
    out["L0_attn_taps"] = np.concatenate([a[f"L0_attn_conv_{n}_w"].reshape(KC, P, TAPS) for n in "qkv"]).transpose(1, 0, 2)
    out["L0_attn_rms_w"] = np.tile(a["L0_attn_rms_w"], P // D_HEAD).reshape(P, 1)
    out.update(constants())
    return {k: np.ascontiguousarray(v) for k, v in out.items()}


def kernel(**inputs):
    import concourse.bacc as bacc
    from concourse.bass_utils import run_bass_kernel_spmd

    nc = bacc.Bacc("TRN2", target_bir_lowering=False, num_devices=1)
    arrays = {f"in_{k}": v for k, v in laid_out(inputs).items()}
    aps = {k[3:]: nc.dram_tensor(k, v.shape, mybir.dt.from_np(v.dtype), kind="ExternalInput").ap()
           for k, v in arrays.items()}
    out = nc.dram_tensor("out", (TOKENS, DIM), F32, kind="ExternalOutput").ap()
    perceiver(nc, aps, out)
    r = run_bass_kernel_spmd(nc, [arrays], core_ids=[0])
    return r.results[0]["out"].reshape(BATCH, SEQ, DIM)
```

```python
from contextlib import ExitStack

import concourse.bass as bass
from concourse import mybir

F32 = mybir.dt.float32
I32 = mybir.dt.int32
U32 = mybir.dt.uint32
ACT = mybir.ActivationFunctionType
ALU = mybir.AluOpType
AX = mybir.AxisListType

P = 128
BATCH, SEQ, DIM = 32, 64, 256
KEYS = 256
TOKENS = BATCH * SEQ
TILES = TOKENS // P
BPT = P // SEQ
KC = DIM // P
LN_EPS = 1e-5


class Resident:
    pass


class Stage:

    def __init__(self, nc, ctx, tag):
        self.nc, self.ctx, self.tag, self.sems = nc, ctx, tag, []
        ctx.callback(self.clear)

    def clear(self):
        if self.sems:
            self.nc.clear_and_free_semaphores(self.sems)
            self.nc.all_engine_barrier()

    def sb(self, name, shape, dt=F32):
        return self.ctx.enter_context(self.nc.sbuf_tensor(f"{self.tag}_{name}", shape, dt))

    def ps(self, name, shape=(P, 512)):
        return self.ctx.enter_context(self.nc.psum_tensor(f"{self.tag}_{name}_ps", list(shape), F32))

    def sem(self, name):
        self.sems.append(self.nc.alloc_semaphore(f"{self.tag}_{name}"))
        return self.sems[-1]


class Chain:

    def __init__(self, eng, sem, base=0):
        self.eng, self.sem, self.base, self.n = eng, sem, base, 0

    def step(self, ins):
        self.n += 1
        ins.then_inc(self.sem, 1)

    def settle(self):
        self.eng.wait_ge(self.sem, self.base + self.n)


def row(tensor, t):
    if isinstance(t, int):
        return tensor[:, t, :]
    return tensor[:, bass.ds(t, 1), :].rearrange("p a c -> p (a c)")


def norm_scales_vector(nc, res, chain, s_var, s_std, s_rstd):
    for t in range(TILES):
        chain.step(nc.vector.bn_aggr(res.mean_var[:, t, :], res.stats[:, t, :]))
    chain.settle()
    nc.vector.tensor_scalar(res.rstd[:, :, 0], res.mean_var[:, :, 1], LN_EPS, None, ALU.add).then_inc(s_var, 1)
    chain.eng.wait_ge(s_std, 1)
    nc.vector.reciprocal(res.rstd[:, :, 0], res.std[:, :]).then_inc(s_rstd, 1)
    chain.eng.wait_ge(s_rstd, 1)


def norm_scales_scalar(nc, res, act, s_var, s_std):
    act.wait_ge(s_var, 1)
    nc.scalar.activation(res.std[:, :], res.rstd[:, :, 0], ACT.Sqrt).then_inc(s_std, 1)


def normalise(nc, res, out, t):
    return nc.vector.tensor_scalar(out, row(res.x, t), row(res.mean_var, t)[:, 0:1], row(res.rstd, t),
                                   ALU.subtract, ALU.mult)


PAIR = 2
PAIRS_OF_TILES = TILES // PAIR


def two_at_a_time(eng, head, tail, tail_first=False):
    def both(t, p):
        if tail_first:
            tail(t, p)
        head(t + 1, 1 - p)
        if not tail_first:
            tail(t, p)

    head(0, 0)
    with eng.Fori(0, PAIRS_OF_TILES // 2 - 1) as i:
        for p in range(2):
            both(2 * i + p, p)
    both(PAIRS_OF_TILES - 2, 0)
    tail(PAIRS_OF_TILES - 1, 1)


def pair_rows(tensor, u, j):
    return row(tensor, PAIR * u + j)


def pair_of(tensor, u):
    if isinstance(u, int):
        return tensor[:, PAIR * u:PAIR * (u + 1), :]
    return tensor[:, bass.ds(PAIR * u, PAIR), :]


def load_residual(nc, res, x, consts, start_loads):
    with ExitStack() as ctx:
        st = Stage(nc, ctx, "load")
        s_x, s_const, s_stats = [st.sem(f"x_loaded{i}") for i in range(2)], st.sem("const_loaded"), st.sem("stats")
        with nc.Block() as block:
            @block.sync
            def _(sp):
                for half in range(2):
                    part = slice(half * TILES // 2, (half + 1) * TILES // 2)
                    sp.dma_start(res.x[:, part, :], x.rearrange("(t p) d -> p t d",
                                                                p=P)[:, part, :]).then_inc(s_x[half], 16)
                sp.dma_start(res.ident[:], consts["ident"]).then_inc(s_const, 16)
                start_loads(sp)
                sp.wait_ge(s_const, 16)

            @block.vector
            def _(dve):
                nc.vector.memset(res.ones[:], 1.0).then_inc(s_stats, 1)
                for t in range(TILES):
                    if t % (TILES // 2) == 0:
                        dve.wait_ge(s_x[t // (TILES // 2)], 16)
                    nc.vector.bn_stats(res.stats[:, t, :], res.x[:, t, :]).then_inc(s_stats, 1)
                dve.wait_ge(s_stats, TILES + 1)


HEADS, HEAD = 16, 16
HALF_HEADS = P // HEAD
PAIRS = HALF_HEADS // 2
GROUPS = BPT * KC
CTX_ROWS = BPT * KEYS
CTX_CHUNKS = CTX_ROWS // P
TENSOR_ORDER = ['T0', 'G0', 'S2', 'G1', 'V0', 'T1', 'S3', 'T2', 'V1', 'G2', 'V2', 'G3', 'T3', 'G4', 'V3', 'S0', 'O',
                'S1', 'G5']
SCALAR_ORDER = ['T0', 'G1', 'E2', 'T1', 'T2', 'E3', 'G2', 'G3', 'T3', 'E0', 'E1']
VECTOR_ORDER = ['T0', 'G0', 'M2', 'N1', 'T1', 'N2', 'M3', 'T2', 'N3', 'T3', 'G4', 'O', 'M0', 'R', 'M1', 'N0', 'G5', 'X']
PREP = 6
EARLY = ("S0", "M0", "E0", "N0", "S1", "M1", "E1")
STAGED = [what for what in TENSOR_ORDER if what[0] in "GO"]
STEPS = len(STAGED)
TURNED = 4
LOWEST = -3.0e38


class CrossWeights:
    LOADS = 10

    def __init__(self, st, a, layer):
        self.sources = {n: a[f"L{layer}_xattn_{n}"] for n in ("Wq", "Wk", "Wv", "Wo", "bq", "bk", "bv")}
        self.sources["bo"] = a[f"L{layer}_xattn_bo"].to_broadcast([P, DIM])
        self.sources["headmask"], self.sources["parmask"] = a["headmask"], a["parmask"]
        self.wq, self.wk, self.wv, self.wo = (st.sb(n, [P, KC, DIM]) for n in ("wq", "wk", "wv", "wo"))
        self.bq, self.bk, self.bv = (st.sb(n, [P, KC]) for n in ("bq", "bk", "bv"))
        self.bo = st.sb("bo", [P, DIM])
        self.headmask, self.parmask = st.sb("headmask", [P, HALF_HEADS]), st.sb("parmask", [P, 2])
        self.loaded = st.sem("loaded")

    def load(self, eng):
        s = self.sources
        for dst, n in ((self.wq, "Wq"), (self.wk, "Wk"), (self.wv, "Wv"), (self.wo, "Wo")):
            eng.dma_start(dst[:], s[n].rearrange("(k p) n -> p k n", p=P)).then_inc(self.loaded, 16)
        for dst, n in ((self.bq, "bq"), (self.bk, "bk"), (self.bv, "bv"), (self.bo, "bo"),
                       (self.headmask, "headmask"), (self.parmask, "parmask")):
            eng.dma_start(dst[:], s[n]).then_inc(self.loaded, 16)


def cross_attention(nc, res, tag, ctx_T, w, mask, prefetch):
    with ExitStack() as ctx:
        st = Stage(nc, ctx, tag)
        wq, wk, wv, wo, bq, bk, bv, bo = w.wq, w.wk, w.wv, w.wo, w.bq, w.bk, w.bv, w.bo
        headmask, parmask, s_w, N_LOADS = w.headmask, w.parmask, w.loaded, CrossWeights.LOADS
        ctxT = [st.sb(f"ctxT{i}", [P, KC, CTX_ROWS]) for i in range(2)]
        keysT = [st.sb(f"keysT{i}", [P, KC, CTX_ROWS]) for i in range(2)]
        values = [st.sb(f"values{i}", [P, CTX_CHUNKS, DIM]) for i in range(2)]
        xn, xnT, queries = st.sb("xn", [P, DIM]), st.sb("xnT", [P, KC, P]), st.sb("queries", [P, KC, P])
        qspread = [st.sb(f"qspread{i}", [P, GROUPS, HALF_HEADS, SEQ]) for i in range(2)]
        peak, total, inverse = (st.sb(n, [P, 2, PAIRS]) for n in ("peak", "total", "inverse"))
        negpeak = st.sb("negpeak", [P, 2, PAIRS])
        probs = st.sb("probs", [P, 2, PAIRS, KEYS])
        probsT = st.sb("probsT", [P, 2, PAIRS, 2, P])
        outT, outT0 = st.sb("outT", [P, KC, BPT, SEQ]), st.sb("outT0", [P, KC, BPT, SEQ])
        if mask is not None:
            maskadd, keep, zeros = st.sb("maskadd", [P, KEYS]), st.sb("keep", [P, KEYS], I32), st.sb("zeros", [P, KEYS])
            masked = st.sb("masked", [P, 2, PAIRS, KEYS])
        score_ps = [[st.ps(f"score{i}{j}") for j in range(2)] for i in range(2)]
        turn_ps = [st.ps(f"turn{j}") for j in range(2)]
        out_ps, stage_ps = st.ps("out"), st.ps("stage")

        s_ctx = [st.sem(f"ctx_loaded{i}") for i in range(2)]
        s_var, s_std, s_rstd = st.sem("var"), st.sem("std"), st.sem("rstd")
        s_chain, s_inverse, s_even, s_mask, s_maskadd = (
            st.sem(n) for n in ("vector_step", "inverse", "even_heads", "mask", "maskadd"))
        s_bo, s_stats, s_seen = st.sem("bo_added"), st.sem("stats"), st.sem("scores_seen")
        s_xn = st.sem("xn_ready")
        s_full, s_free = st.sem("stage_full"), st.sem("stage_free")
        s_spread = st.sem("queries_spread")
        s_score, s_score_used = st.sem("scores_ready"), st.sem("scores_used")
        s_peak, s_exp = st.sem("peaks_ready"), st.sem("exp_done")
        s_probs = st.sem("probs_ready")
        if mask is None:
            s_score_used = s_exp
        s_turn, s_turned0, s_turned1 = st.sem("turn_full"), st.sem("turned_by_vector"), st.sem("turned_by_scalar")
        s_out, s_outT = st.sem("out_full"), st.sem("outT_ready")

        def step_number(t, what):
            return PREP + STEPS * t + STAGED.index(what)

        def out_step(t, last):
            return step_number(t, "O") - (STAGED.index("O") if last else 0)

        def in_turn(eng, order, prep, scores, step):
            def one(t, p, what, last=False):
                if what[0] in "SME":
                    scores(t, p, int(what[1]))
                else:
                    step(t, p, last, what[0], int(what[1:] or 0))

            def turn(t, p, last=False):
                for what in order:
                    if what[0] == "G":
                        if not last:
                            prep(t + 1, 1 - p, step_number(t, what), int(what[1]))
                    elif what not in EARLY:
                        one(t, p, what, last)
                    elif not last:
                        one(t + 1, 1 - p, what)

            for s in range(PREP):
                prep(0, 0, s, s)
            for what in order:
                if what in EARLY:
                    one(0, 0, what)
            turn(0, 0)
            turn(1, 1)
            with eng.Fori(1, TILES // 2 - 1) as i:
                turn(2 * i, 0)
                turn(2 * i + 1, 1)
            turn(TILES - 2, 0)
            turn(TILES - 1, 1, last=True)

        with nc.Block() as block:
            @block.sync
            def _(sp):
                source = ctx_T.rearrange("(k p) n -> p k n", p=P)
                for t in range(2):
                    sp.dma_start(ctxT[t][:], source[:, :, t * CTX_ROWS:(t + 1) * CTX_ROWS]).then_inc(s_ctx[t], 16)
                if mask is not None:
                    for half in range(2):
                        sp.dma_start(keep[half * SEQ:(half + 1) * SEQ, :], mask).then_inc(s_mask, 16)
                for t in (2, 3):
                    sp.wait_ge(s_full, PREP if t == 2 else step_number(t - 3, "G5") + 1)
                    sp.dma_start(ctxT[t % 2][:], source[:, :, t * CTX_ROWS:(t + 1) * CTX_ROWS]).then_inc(s_ctx[t % 2],
                                                                                                         16)
                with sp.Fori(2, TILES // 2) as i:
                    for p in range(2):
                        column = sp.snap((2 * i + p) * CTX_ROWS)
                        used = sp.snap((2 * i + p) * STEPS + (step_number(0, "G5") + 1 - 3 * STEPS))
                        sp.wait_ge(s_full, used)
                        sp.dma_start(ctxT[p][:], source[:, :, bass.ds(column, CTX_ROWS)]).then_inc(s_ctx[p], 16)
                prefetch(sp)

            @block.tensor
            def _(pe):
                def prep(u, p, n, s):
                    if s == 0:
                        pe.wait_ge(s_xn, u + 1)
                    if s == 2:
                        pe.wait_ge(s_ctx[p], 16 * (u // 2 + 1) if isinstance(u, int) else 8 * (u - p) + 16)
                    pe.wait_ge(s_free, n)
                    if s == 0:
                        for k in range(KC):
                            mm = nc.tensor.transpose(stage_ps[:, k * P:(k + 1) * P], xn[:, k * P:(k + 1) * P],
                                                     res.ident[:])
                    elif s == 1:
                        for m in range(KC):
                            for k in range(KC):
                                mm = nc.tensor.matmul(stage_ps[:, m * P:(m + 1) * P], wq[:, k, m * P:(m + 1) * P],
                                                      xnT[:, k, :], start=k == 0, stop=k == KC - 1)
                    elif s in (2, 3):
                        m = s - 2
                        for k in range(KC):
                            mm = nc.tensor.matmul(stage_ps[:, :], wk[:, k, m * P:(m + 1) * P], ctxT[p][:, k, :],
                                                  start=k == 0, stop=k == KC - 1)
                    else:
                        for j in range(2):
                            chunk = (s - 4) * 2 + j
                            for k in range(KC):
                                mm = nc.tensor.matmul(stage_ps[:, j * DIM:(j + 1) * DIM],
                                                      ctxT[p][:, k, chunk * P:(chunk + 1) * P],
                                                      wv[:, k, :], start=k == 0, stop=k == KC - 1)
                    mm.then_inc(s_full, 1)

                def scores(t, p, g):
                    b, half = g // KC, g % KC
                    if g == 0:
                        pe.wait_ge(s_spread, GROUPS * (t + 1))
                        pe.wait_ge(s_free, PREP if isinstance(t, int) and t == 0 else step_number(t - 1, "G3") + 1)
                    pe.wait_ge(s_score_used, GROUPS * t + g + 1)
                    for r in range(PAIRS):
                        mm = nc.tensor.matmul(
                            score_ps[g % 2][r // 2][:, (r % 2) * KEYS:(r % 2 + 1) * KEYS],
                            qspread[p][:, g, 2 * r:2 * r + 2, :].rearrange("p h q -> p (h q)"),
                            keysT[p][:, half, b * KEYS:(b + 1) * KEYS], start=True, stop=True)
                        if r % 2:
                            mm.then_inc(s_score, 1)

                def step(t, p, last, what, g):
                    b, half = g // KC, g % KC
                    if what == "T":
                        pe.wait_ge(s_probs, GROUPS * t + g + 1)
                        for j in range(2):
                            pe.wait_ge((s_turned0, s_turned1)[j], GROUPS * t + g)
                            for r in range(2 * j, 2 * j + 2):
                                for k in range(2):
                                    at = ((r % 2) * 2 + k) * P
                                    mm = nc.tensor.transpose(turn_ps[j][:, at:at + P],
                                                             probs[:, g % 2, r, k * P:(k + 1) * P], res.ident[:])
                            mm.then_inc(s_turn, 1)
                    elif what == "V":
                        pe.wait_ge(s_turned0, GROUPS * t + g + 1)
                        pe.wait_ge(s_turned1, GROUPS * t + g + 1)
                        if g == 0:
                            pe.wait_ge(s_outT, t)
                            pe.wait_ge(s_free, PREP + STEPS * t)
                        for r in range(PAIRS):
                            for k in range(2):
                                chan = half * P + 2 * HEAD * r
                                mm = nc.tensor.matmul(out_ps[2 * HEAD * r:2 * HEAD * (r + 1), g * P:(g + 1) * P],
                                                      values[p][:, b * 2 + k, chan:chan + 2 * HEAD],
                                                      probsT[:, g % 2, r, k, :], start=k == 0, stop=k == 1)
                        if g == GROUPS - 1:
                            mm.then_inc(s_out, 1)
                    elif what == "O":
                        pe.wait_ge(s_free, out_step(t, last))
                        pe.wait_ge(s_outT, t + 1)
                        for k in range(KC):
                            mm = nc.tensor.matmul(stage_ps[:, 0:DIM], outT[:, k, :, :].rearrange("p b q -> p (b q)"),
                                                  wo[:, k, :], start=k == 0, stop=k == KC - 1)
                        mm.then_inc(s_full, 1)

                pe.wait_ge(s_w, 16 * N_LOADS)
                in_turn(pe, TENSOR_ORDER, prep, scores, step)

            @block.scalar
            def _(act):
                def prep(u, p, n, s):
                    if s not in (1, 2, 3):
                        return
                    act.wait_ge(s_full, n + 1)
                    if s == 1:
                        act.wait_ge(s_spread, GROUPS * u)
                        for m in range(KC):
                            ins = nc.scalar.activation(queries[:, m, :], stage_ps[:, m * P:(m + 1) * P], ACT.Identity,
                                                       bias=bq[:, m:m + 1])
                    else:
                        ins = nc.scalar.activation(keysT[p][:, s - 2, :], stage_ps[:, :], ACT.Identity,
                                                   bias=bk[:, s - 2:s - 1])
                    ins.then_inc(s_free, 1)

                def scores(t, p, g):
                    act.wait_ge(s_peak, GROUPS * t + g + 1)
                    act.wait_ge(s_turn, 2 * (GROUPS * t + g + 1))
                    for r in range(PAIRS):
                        if mask is None:
                            scores = score_ps[g % 2][r // 2][:, (r % 2) * KEYS:(r % 2 + 1) * KEYS]
                        else:
                            scores = masked[:, g % 2, r, :]
                        ins = nc.scalar.activation(probs[:, g % 2, r, :], scores, ACT.Exp,
                                                   bias=negpeak[:, g % 2, r:r + 1],
                                                   accum_out=total[:, g % 2, r:r + 1])
                    ins.then_inc(s_exp, 1)

                def step(t, p, last, what, g):
                    if what == "T":
                        act.wait_ge(s_turn, TURNED + 2 * (GROUPS * t + g) + 2)
                        nc.scalar.activation(probsT[:, g % 2, 2:4, :, :].rearrange("p r k q -> p (r k q)"),
                                             turn_ps[1][:, :], ACT.Copy).then_inc(s_turned1, 1)

                norm_scales_scalar(nc, res, act, s_var, s_std)
                act.wait_ge(s_w, 16 * N_LOADS)
                in_turn(act, SCALAR_ORDER, prep, scores, step)

            @block.gpsimd
            def _(pool):
                def spread(u, p, n):
                    pool.wait_ge(s_free, n + 1)
                    for b in range(BPT):
                        for half in range(KC):
                            nc.gpsimd.tensor_tensor(
                                qspread[p][:, b * KC + half, :, :],
                                queries[:, half, b * SEQ:(b + 1) * SEQ].unsqueeze(1).to_broadcast([P, HALF_HEADS, SEQ]),
                                headmask[:, :].unsqueeze(2).to_broadcast([P, HALF_HEADS, SEQ]),
                                ALU.mult).then_inc(s_spread, 1)

                pool.wait_ge(s_w, 16 * N_LOADS)
                spread(0, 0, 1)
                spread(1, 1, step_number(0, "G1"))
                with pool.Fori(1, TILES // 2) as i:
                    for p in range(2):
                        before = pool.snap((2 * i + p) * GROUPS - 2 * GROUPS + GROUPS)
                        pool.wait_ge(s_score_used, 2 + before)
                        spread(2 * i + p, p, step_number(2 * i + p - 1, "G1"))

            @block.vector
            def _(dve):
                chain = Chain(dve, s_chain)

                def normalised(u):
                    normalise(nc, res, xn[:, :], u).then_inc(s_xn, 1)
                    dve.wait_ge(s_xn, u + 1)
                    nc.vector.tensor_tensor(row(res.x, u), row(res.x, u), bo[:, :], ALU.add).then_inc(s_bo, 1)

                def prep(u, p, n, s):
                    if s not in (0, 4, 5):
                        return
                    dve.wait_ge(s_full, n + 1)
                    if s == 0:
                        ins = nc.vector.tensor_copy(xnT[:, :, :].rearrange("p k q -> p (k q)"), stage_ps[:, 0:DIM])
                    else:
                        j = 2 * (s - 4)
                        ins = nc.vector.tensor_copy(values[p][:, j:j + 2, :].rearrange("p j d -> p (j d)"),
                                                    stage_ps[:, :])
                    ins.then_inc(s_free, 1)
                    if s == 0 and isinstance(u, int) and u == 0:
                        normalised(1)

                def scores(t, p, g):
                    k = GROUPS * t + g
                    if mask is None:
                        for j in range(2):
                            dve.wait_ge(s_score, 2 * k + j + 1)
                            ins = nc.vector.tensor_reduce(
                                negpeak[:, g % 2, 2 * j:2 * j + 2],
                                score_ps[g % 2][j][:, :].rearrange("p (r k) -> p r k", r=2),
                                AX.X, ALU.max, negate=True)
                        ins.then_inc(s_peak, 1)
                    else:
                        dve.wait_ge(s_exp, k + 1)
                        for r in range(PAIRS):
                            if r % 2 == 0:
                                dve.wait_ge(s_score, 2 * k + r // 2 + 1)
                                dve.sem_inc(s_seen, 1)
                            ins = nc.vector.tensor_tensor_reduce(
                                masked[:, g % 2, r, :],
                                score_ps[g % 2][r // 2][:, (r % 2) * KEYS:(r % 2 + 1) * KEYS],
                                maskadd[:, :], 1.0, LOWEST, ALU.add, ALU.max, peak[:, g % 2, r:r + 1])
                        ins.then_inc(s_score_used, 1)
                        dve.wait_ge(s_score_used, 2 + k + 1)
                        nc.vector.tensor_scalar(negpeak[:, g % 2, :], peak[:, g % 2, :], -1.0, None,
                                                ALU.mult).then_inc(s_peak, 1)

                def step(t, p, last, what, g):
                    k = GROUPS * t + g
                    if what == "N":
                        dve.wait_ge(s_exp, 2 + k + 1)
                        nc.vector.reciprocal(inverse[:, g % 2, :], total[:, g % 2, :]).then_inc(s_inverse, 1)
                        dve.wait_ge(s_inverse, k + 1)
                        for r in range(PAIRS):
                            ins = nc.vector.tensor_scalar(probs[:, g % 2, r, :], probs[:, g % 2, r, :],
                                                          inverse[:, g % 2, r:r + 1], None, ALU.mult)
                        ins.then_inc(s_probs, 1)
                    elif what == "T":
                        dve.wait_ge(s_turn, TURNED + 2 * k + 1)
                        nc.vector.tensor_copy(probsT[:, g % 2, 0:2, :, :].rearrange("p r k q -> p (r k q)"),
                                              turn_ps[0][:, :]).then_inc(s_turned0, 1)
                    elif what == "O":
                        dve.wait_ge(s_out, t + 1)
                        o = out_ps[:, :].rearrange("p (b m e q) -> p b m e q", b=BPT, m=KC, e=2)
                        for m in range(KC):
                            ins = nc.vector.tensor_scalar(outT0[:, m, :, :], o[:, :, m, 0, :], parmask[:, 0:1],
                                                          bv[:, m:m + 1], ALU.mult, ALU.add)
                        ins.then_inc(s_even, 1)
                        dve.wait_ge(s_even, t + 1)
                        for m in range(KC):
                            ins = nc.vector.scalar_tensor_tensor(outT[:, m, :, :], o[:, :, m, 1, :], parmask[:, 1:2],
                                                                 outT0[:, m, :, :], ALU.mult, ALU.add)
                        ins.then_inc(s_outT, 1)
                    elif what == "R":
                        dve.wait_ge(s_bo, t + 1)
                        dve.wait_ge(s_full, out_step(t, last) + 1)
                        nc.vector.tensor_tensor(row(res.x, t), row(res.x, t), stage_ps[:, 0:DIM],
                                                ALU.add).then_inc(s_free, 1)
                        dve.wait_ge(s_free, out_step(t, last) + 1)
                        nc.vector.bn_stats(row(res.stats, t), row(res.x, t)).then_inc(s_stats, 1)
                    elif what == "X" and not (isinstance(t, int) and t >= TILES - 2):
                        normalised(t + 2)

                norm_scales_vector(nc, res, chain, s_var, s_std, s_rstd)
                dve.sem_inc(s_score_used, 2)
                dve.sem_inc(s_turn, TURNED)
                if mask is not None:
                    dve.sem_inc(s_exp, 2)
                    nc.vector.memset(maskadd[:], LOWEST).then_inc(s_maskadd, 1)
                    nc.vector.memset(zeros[:], 0.0).then_inc(s_maskadd, 1)
                    dve.wait_ge(s_maskadd, 2)
                    dve.wait_ge(s_mask, 32)
                    nc.vector.copy_predicated(maskadd[:, :], keep[:, :], zeros[:, :]).then_inc(s_maskadd, 1)
                    dve.wait_ge(s_maskadd, 3)
                dve.wait_ge(s_w, 16 * N_LOADS)
                normalised(0)
                in_turn(dve, VECTOR_ORDER, prep, scores, step)
                dve.wait_ge(s_stats, TILES)


D_HEADS, D_HEAD, TAPS = 4, 64, 4
LEVELS = (2, 4, 8, 16, 32)
QKV = 3 * KC
MASK_OPS = 4 + len(LEVELS)
DELTA_ORDER = ['Y1a', 'C0', 'Y1b', 'V1', 'T1a', 'T1b', 'C1', 'Y2a', 'Y2b', 'B1', 'T2a', 'T2b',
               'C2', 'Y3a', 'Y3b', 'T3a', 'T3b', 'V2', 'Y4a', 'B2', 'Y4b', 'V3', 'T4a', 'T4b',
               'Y5a', 'Y5b', 'T5a', 'V4', 'T5b', 'B3', 'U', 'A0', 'O', 'A1']
HALF = D_HEADS // 2


def level_of(what):
    n, half = int(what[1]), "ab".index(what[2])
    return n, half, 2 * (n - 1) + half


class DeltaWeights:
    LOADS = 11

    def __init__(self, st, a):
        self.a = a
        self.wqkv = [st.sb(f"w{n}", [P, KC, DIM]) for n in "qkv"]
        self.wb, self.taps = st.sb("wb", [P, KC, D_HEADS]), st.sb("taps", [P, QKV, TAPS])
        self.head_ones = st.sb("head_ones", [P, 2])
        self.strict, self.causalT = st.sb("strict", [P, P]), st.sb("causalT", [P, P])
        self.join1, self.join1T = st.sb("join1", [P, P]), st.sb("join1T", [P, P])
        self.joinT = st.sb("joinT", [P, len(LEVELS), P])
        self.loaded = st.sem("loaded")

    def load(self, eng):
        for dst, n in zip(self.wqkv + [self.wb], ("q", "k", "v", "b")):
            eng.dma_start(dst[:], self.a[f"L0_attn_W{n}"].rearrange("(k p) n -> p k n", p=P)).then_inc(self.loaded, 16)
        for dst, n in ((self.taps, "L0_attn_taps"), (self.head_ones, "head_ones"), (self.strict, "strict"),
                       (self.causalT, "causalT"), (self.join1, "join1"), (self.join1T, "join1T"), (self.joinT,
                                                                                                   "joinT")):
            eng.dma_start(dst[:], self.a[n]).then_inc(self.loaded, 16)


def delta_rule(nc, res, w, prefetch):
    with ExitStack() as ctx:
        st = Stage(nc, ctx, "delta")
        wqkv, wb, taps, head_ones = w.wqkv, w.wb, w.taps, w.head_ones
        strict, causalT, join1, join1T, joinT = w.strict, w.causalT, w.join1, w.join1T, w.joinT
        xn, xnT, pre = st.sb("xn", [P, DIM]), st.sb("xnT", [P, KC, P]), st.sb("pre", [P, QKV, BPT, SEQ])
        qkvT = st.sb("qkvT", [P, QKV, P])
        squares = st.sb("squares", [P, 2 * KC, P])
        inv_sq, inv_norm = (st.sb(n, [P, 2 * D_HEADS]) for n in ("inv_sq", "inv_norm"))
        logits = [st.sb(f"logits{i}", [P, D_HEADS]) for i in range(2)]
        tanh, beta = st.sb("tanh", [P, D_HEADS]), st.sb("beta", [P, D_HEADS])
        row_scale, value_scale = st.sb("row_scale", [P, D_HEADS]), st.sb("value_scale", [P, D_HEADS])
        query_scale = [st.sb(f"query_scale{i}", [P, D_HEADS]) for i in range(2)]
        vb = [st.sb(f"vb{i}", [P, D_HEADS, D_HEAD]) for i in range(2)]
        lower, lowerT = st.sb("lower", [P, D_HEADS, P]), st.sb("lowerT", [P, D_HEADS, P])
        part, partT = st.sb("part", [P, D_HEADS, P]), st.sb("partT", [P, D_HEADS, P])
        joined = [st.sb(f"joined{i}", [P, len(LEVELS), D_HEADS, P]) for i in range(2)]
        first, firstT = ([st.sb(f"{n}{i}", [P, D_HEADS, P]) for i in range(2)] for n in ("first", "firstT"))
        attnT = [st.sb(f"attnT{i}", [P, D_HEADS, P]) for i in range(2)]
        inverse = [st.sb(f"inverse{i}", [P, 2, HALF, P]) for i in range(2)]
        rest = st.sb("rest", [P, D_HEADS, P])
        u_sb, o_sq = st.sb("u", [P, DIM]), st.sb("o_sq", [P, DIM])
        qk_ps, v_ps = st.ps("qk"), st.ps("v")
        gram_ps = [st.ps(f"gram{i}") for i in range(2)]
        y_ps, t_ps = ([st.ps(f"{n}{i}") for i in range(2)] for n in ("y", "t"))
        u_ps, o_ps = y_ps
        BETA = DIM
        sums_ps = gram_ps[1]

        s = Resident()
        s.weights = w.loaded
        s.var, s.std, s.rstd = (st.sem(n) for n in ("var", "std", "rstd"))
        s.vector_step, s.xn, s.turned, s.xnT = (st.sem(n) for n in ("vector_step", "xn", "turned", "xnT"))
        s.projected, s.logits, s.conv, s.conv_step = (st.sem(n) for n in ("projected", "logits", "conv", "conv_step"))
        s.silu, s.tanh, s.squares, s.sums = (st.sem(n) for n in ("silu", "tanh", "squares", "sums"))
        s.inv_sq, s.inv_norm, s.row_scale, s.scales = (st.sem(n) for n in ("inv_sq", "inv_norm", "row_scale", "scales"))
        s.vturned = st.sem("vturned")
        s.vb, s.gram, s.attn, s.attn_masked = (st.sem(n) for n in ("vb", "gram", "attn", "attn_masked"))
        s.lower, s.lturned, s.lowerT, s.masks = (st.sem(n) for n in ("lower", "lturned", "lowerT", "masks"))
        s.y, s.rest, s.t, s.inverse = (st.sem(n) for n in ("y", "rest", "t", "inverse"))
        s.u_full, s.u_copied = (st.sem(n) for n in ("u_full", "u_copied"))
        PER_TILE = 2 * len(LEVELS)
        s.o_full, s.o_read, s.out_step = (st.sem(n) for n in ("o_full", "o_read", "out_step"))
        every = lambda m, h=D_HEADS: m.unsqueeze(1).to_broadcast([P, h, P])
        N_LOADS = DeltaWeights.LOADS
        with nc.Block() as block:
            @block.sync
            def _(sp):
                prefetch(sp)

            @block.tensor
            def _(pe):
                def a_step(u, p, n):
                    if n == 0:
                        pe.wait_ge(s.xn, u + 1)
                        pe.wait_ge(s.conv, u)
                        for k in range(KC):
                            mm = nc.tensor.transpose(qk_ps[:, k * P:(k + 1) * P], xn[:, k * P:(k + 1) * P],
                                                     res.ident[:])
                        mm.then_inc(s.turned, 1)
                    else:
                        pe.wait_ge(s.xnT, u + 1)
                        for i in range(QKV):
                            bank, col = (qk_ps, i * P) if i < 2 * KC else (v_ps, (i - 2 * KC) * P)
                            for k in range(KC):
                                nc.tensor.matmul(bank[:, col:col + P],
                                                 wqkv[i // KC][:, k, (i % KC) * P:(i % KC + 1) * P],
                                                 xnT[:, k, :], start=k == 0, stop=k == KC - 1)
                        for k in range(KC):
                            mm = nc.tensor.matmul(v_ps[:, BETA:BETA + D_HEADS], xnT[:, k, :], wb[:, k, :],
                                                  start=k == 0, stop=k == KC - 1)
                        mm.then_inc(s.projected, 1)

                def c_step(u, p, n):
                    if n == 1:
                        pe.wait_ge(s.squares, u + 1)
                        pe.wait_ge(s.attn_masked, u)
                        for i in range(2 * KC):
                            mm = nc.tensor.matmul(sums_ps[:, 2 * i:2 * i + 2], squares[:, i, :], head_ones[:],
                                                  start=True, stop=True)
                        mm.then_inc(s.sums, 1)

                def b_step(u, p, n):
                    if n == 1:
                        pe.wait_ge(s.silu, u + 1)
                        pe.wait_ge(s.inv_sq, u + 1)
                        pe.wait_ge(s.vb, u)
                        for of in range(2):
                            for h in range(D_HEADS):
                                rows = slice(D_HEAD * (h % 2), D_HEAD * (h % 2 + 1))
                                col = (2 * of + h // 2) * P
                                mm = nc.tensor.matmul(gram_ps[h % 2][:, col:col + P], qkvT[rows, KC + h // 2, :],
                                                      qkvT[rows, (KC if of == 0 else 0) + h // 2, :], start=True, stop=True)
                                if of == 1 and h == D_HEADS - 2:
                                    mm.then_inc(s.gram, 1)
                        mm.then_inc(s.gram, 1)
                    elif n == 2:
                        pe.wait_ge(s.lower, u + 1)
                        pe.wait_ge(s.attn_masked, u + 1)
                        for h in range(D_HEADS):
                            mm = nc.tensor.transpose(gram_ps[0][:, h * P:(h + 1) * P], lower[:, h, :], res.ident[:])
                        mm.then_inc(s.lturned, 1)
                    else:
                        pe.wait_ge(s.lowerT, u + 1)
                        for i in range(KC):
                            mm = nc.tensor.transpose(gram_ps[0][:, i * P:(i + 1) * P], qkvT[:, 2 * KC + i, :],
                                                     res.ident[:])
                        mm.then_inc(s.vturned, 1)

                def tail(t, p, what):
                    if what[0] == "Y":
                        n, half, k = level_of(what)
                        pe.wait_ge(s.masks, MASK_OPS * t + MASK_OPS - len(LEVELS) + n)
                        if n == 1:
                            if half == 1:
                                pe.wait_ge(s.o_read, t)
                        else:
                            pe.wait_ge(s.inverse, PER_TILE * t + k - 1)
                        for i in range(HALF):
                            h = HALF * half + i
                            m = first[p][:, h, :] if n == 1 else inverse[half][:, 0, i, :]
                            mm = nc.tensor.matmul(y_ps[half][:, i * P:(i + 1) * P], joined[p][:, n - 1, h, :], m,
                                                  start=True, stop=True)
                        mm.then_inc(s.y, 1)
                    elif what[0] == "T":
                        n, half, k = level_of(what)
                        pe.wait_ge(s.rest, PER_TILE * t + k + 1)
                        for i in range(HALF):
                            h = HALF * half + i
                            mT = firstT[p][:, h, :] if n == 1 else inverse[half][:, 1, i, :]
                            if n < len(LEVELS):
                                nc.tensor.matmul(t_ps[half][:, i * P:(i + 1) * P], mT, rest[:, h, :], start=True,
                                                 stop=True)
                            mm = nc.tensor.matmul(t_ps[half][:, (HALF + i) * P:(HALF + i + 1) * P], rest[:, h, :], mT,
                                                  start=True, stop=True)
                        mm.then_inc(s.t, 1)
                    elif what == "U":
                        pe.wait_ge(s.inverse, PER_TILE * (t + 1))
                        pe.wait_ge(s.vb, t + 1)
                        for h in range(D_HEADS):
                            mm = nc.tensor.matmul(u_ps[:, h * D_HEAD:(h + 1) * D_HEAD],
                                                  inverse[h // HALF][:, 1, h % HALF, :],
                                                  vb[p][:, h, :], start=True, stop=True)
                        mm.then_inc(s.u_full, 1)
                    else:
                        pe.wait_ge(s.u_copied, t + 1)
                        for h in range(D_HEADS):
                            mm = nc.tensor.matmul(o_ps[:, h * D_HEAD:(h + 1) * D_HEAD], attnT[p][:, h, :],
                                                  u_sb[:, h * D_HEAD:(h + 1) * D_HEAD], start=True, stop=True)
                        mm.then_inc(s.o_full, 1)

                pe.wait_ge(s.weights, 16 * N_LOADS)
                delta_loop(pe, a_step, None, c_step, b_step, tail)

            @block.scalar
            def _(act):
                def a_step(u, p, n):
                    if n == 0:
                        act.wait_ge(s.turned, u + 1)
                        nc.scalar.activation(xnT[:, :, :].rearrange("p k q -> p (k q)"), qk_ps[:, 0:DIM],
                                             ACT.Copy).then_inc(s.xnT, 1)
                    else:
                        act.wait_ge(s.projected, u + 1)
                        if not isinstance(u, int) or u > 1:
                            act.wait_ge(s.tanh, u - 1)
                        nc.scalar.activation(logits[p][:, :], v_ps[:, BETA:BETA + D_HEADS],
                                             ACT.Copy).then_inc(s.logits, 1)

                def c_step(u, p, n):
                    if n == 0:
                        act.wait_ge(s.conv, u + 1)
                        act.wait_ge(s.vturned, u)
                        nc.scalar.activation(qkvT[:, :, :].rearrange("p i q -> p (i q)"),
                                             pre[:, :, :, :].rearrange("p i b q -> p (i b q)"), ACT.Silu).then_inc(s.silu, 1)
                        act.wait_ge(s.silu, u + 1)
                        act.wait_ge(s.sums, u)
                        nc.scalar.activation(squares[:, :, :], qkvT[:, 0:2 * KC, :], ACT.Square).then_inc(s.squares, 1)
                        act.wait_ge(s.logits, u + 1)
                        act.wait_ge(s.inv_sq, u)
                        nc.scalar.activation(tanh[:, :], logits[p][:, :], ACT.Tanh, scale=0.5).then_inc(s.tanh, 1)
                    elif n == 2:
                        act.wait_ge(s.inv_sq, u + 1)
                        act.wait_ge(s.scales, u)
                        nc.scalar.activation(inv_norm[:, :], inv_sq[:, :], ACT.Sqrt).then_inc(s.inv_norm, 1)

                def b_step(u, p, n):
                    if n == 2:
                        act.wait_ge(s.lturned, u + 1)
                        act.wait_ge(s.masks, MASK_OPS * u)
                        nc.scalar.activation(lowerT[:, :, :].rearrange("p h q -> p (h q)"), gram_ps[0][:, :],
                                             ACT.Copy).then_inc(s.lowerT, 1)

                def tail(t, p, what):
                    if what[0] == "T":
                        n, half, k = level_of(what)
                        act.wait_ge(s.t, PER_TILE * t + k + 1)
                        first_of = 0 if n < len(LEVELS) else 1
                        nc.scalar.activation(inverse[half][:, first_of:, :, :].rearrange("p o h q -> p (o h q)"),
                                             t_ps[half][:, first_of * HALF * P:], ACT.Copy).then_inc(s.inverse, 1)
                    elif what == "U":
                        act.wait_ge(s.u_full, t + 1)
                        nc.scalar.activation(u_sb[:, :], u_ps[:, 0:DIM], ACT.Copy).then_inc(s.u_copied, 1)

                norm_scales_scalar(nc, res, act, s.var, s.std)
                delta_loop(act, a_step, None, c_step, b_step, tail)

            @block.gpsimd
            def _(pool):
                def b_step(u, p, n):
                    if n != 2:
                        return
                    pool.wait_ge(s.lowerT, u + 1)
                    if not isinstance(u, int) or u > 1:
                        pool.wait_ge(s.y, PER_TILE * (u - 1))
                    nc.gpsimd.tensor_tensor(partT[:], lowerT[:], every(join1T[:, :]), ALU.mult).then_inc(s.masks, 1)
                    nc.gpsimd.tensor_tensor(part[:], lower[:], every(join1[:, :]), ALU.mult).then_inc(s.masks, 1)
                    pool.wait_ge(s.masks, MASK_OPS * u + 2)
                    nc.gpsimd.tensor_tensor(firstT[p][:], every(res.ident[:, :]), partT[:],
                                            ALU.subtract).then_inc(s.masks, 1)
                    nc.gpsimd.tensor_tensor(first[p][:], every(res.ident[:, :]), part[:],
                                            ALU.subtract).then_inc(s.masks, 1)
                    for i in range(len(LEVELS)):
                        nc.gpsimd.tensor_tensor(joined[p][:, i, :, :], lowerT[:], every(joinT[:, i, :]),
                                                ALU.mult).then_inc(s.masks, 1)

                pool.wait_ge(s.weights, 16 * N_LOADS)
                delta_loop(pool, None, None, None, b_step, None)

            @block.vector
            def _(dve):
                def a_step(u, p, n):
                    if n == 0:
                        dve.wait_ge(s.turned, u)
                        normalise(nc, res, xn[:, :], u).then_inc(s.xn, 1)

                def v_step(u, p, n):
                    back = n - 1
                    if n == 1:
                        dve.wait_ge(s.silu, u)
                        dve.wait_ge(s.projected, u + 1)
                        dve.wait_ge(s.logits, u + 1)
                    else:
                        dve.wait_ge(s.conv_step, (TAPS - 1) * u + n - 1)
                    for i in range(QKV):
                        src = (qk_ps[:, i * P:(i + 1) * P] if i < 2 * KC else v_ps[:, (i - 2 * KC) * P:(i - 2 * KC + 1) * P])
                        src = src.rearrange("p (b q) -> p b q", b=BPT)
                        tap = taps[:, i, TAPS - 1 - back:TAPS - back]
                        if n == 1:
                            ins = nc.vector.tensor_scalar(pre[:, i, :, :], src, tap, None, ALU.mult)
                        else:
                            ins = nc.vector.scalar_tensor_tensor(pre[:, i, :, back:], src[:, :, 0:SEQ - back], tap,
                                                                 pre[:, i, :, back:], ALU.mult, ALU.add)
                    ins.then_inc(s.conv if n == TAPS else s.conv_step, 1)

                def c_step(u, p, n):
                    if n == 1:
                        dve.wait_ge(s.tanh, u + 1)
                        nc.vector.tensor_scalar(beta[:, :], tanh[:, :], 0.5, 0.5, ALU.mult, ALU.add)
                        dve.wait_ge(s.inv_norm, u)
                        dve.wait_ge(s.sums, u + 1)
                        nc.vector.reciprocal(inv_sq[:, :], sums_ps[:, 0:2 * D_HEADS]).then_inc(s.inv_sq, 1)
                        dve.wait_ge(s.inv_sq, u + 1)
                        nc.vector.tensor_tensor(row_scale[:, :], beta[:, :], inv_sq[:, D_HEADS:],
                                                ALU.mult).then_inc(s.row_scale, 1)

                def b_step(u, p, n):
                    if n == 1:
                        dve.wait_ge(s.gram, 2 * (u + 1))
                        dve.wait_ge(s.row_scale, u + 1)
                        dve.wait_ge(s.masks, MASK_OPS * u)
                        for h in range(D_HEADS):
                            ins = nc.vector.scalar_tensor_tensor(lower[:, h, :],
                                                                 gram_ps[h % 2][:, h // 2 * P:(h // 2 + 1) * P],
                                                                 row_scale[:, h:h + 1], strict[:, :], ALU.mult, ALU.mult)
                        ins.then_inc(s.lower, 1)
                        if not isinstance(u, int) or u > 1:
                            dve.wait_ge(s.o_full, u - 1)
                        for e in range(2):
                            ins = nc.vector.tensor_tensor(
                                attnT[p][:, :, :].rearrange("p (g e) q -> p g e q", e=2)[:, :, e, :],
                                gram_ps[e][:, 2 * P:].rearrange("p (g q) -> p g q", g=2),
                                every(causalT[:, :], 2), ALU.mult)
                        ins.then_inc(s.attn_masked, 1)
                    elif n == 3:
                        dve.wait_ge(s.inv_norm, u + 1)
                        nc.vector.tensor_scalar(query_scale[p][:, :], inv_norm[:, 0:D_HEADS], D_HEAD ** -0.5, None,
                                                ALU.mult)
                        nc.vector.tensor_tensor(value_scale[:, :], beta[:, :], inv_norm[:, D_HEADS:],
                                                ALU.mult).then_inc(s.scales, 1)
                        dve.wait_ge(s.scales, u + 1)
                        dve.wait_ge(s.vturned, u + 1)
                        if not isinstance(u, int) or u > 1:
                            dve.wait_ge(s.u_full, u - 1)
                        nc.vector.tensor_tensor(vb[p][:, :, :], gram_ps[0][:, 0:DIM].rearrange("p (h d) -> p h d",
                                                                                               h=D_HEADS),
                                                value_scale[:, :].unsqueeze(2).to_broadcast([P, D_HEADS, D_HEAD]),
                                                ALU.mult).then_inc(s.vb, 1)

                def tail(t, p, what):
                    if what[0] == "Y":
                        n, half, k = level_of(what)
                        dve.wait_ge(s.y, PER_TILE * t + k + 1)
                        nc.vector.tensor_tensor(rest[:, HALF * half:HALF * (half + 1), :], every(res.ident[:, :], HALF),
                                                y_ps[half][:, 0:HALF * P].rearrange("p (h q) -> p h q", h=HALF),
                                                ALU.subtract).then_inc(s.rest, 1)
                    elif what == "O":
                        dve.wait_ge(s.o_full, t + 1)
                        nc.vector.tensor_tensor(
                            row(res.mixed, t).rearrange("p (h d) -> p h d", h=D_HEADS),
                            o_ps[:, 0:DIM].rearrange("p (h d) -> p h d", h=D_HEADS),
                            query_scale[p][:, :].unsqueeze(2).to_broadcast([P, D_HEADS, D_HEAD]),
                            ALU.mult).then_inc(s.o_read, 1)
                        dve.wait_ge(s.o_read, t + 1)
                        nc.vector.tensor_tensor(o_sq[:, :], row(res.mixed, t), row(res.mixed, t),
                                                ALU.mult).then_inc(s.out_step, 1)
                        dve.wait_ge(s.out_step, 2 * t + 1)
                        nc.vector.tensor_reduce(row(res.squares, t), o_sq[:, :].rearrange("p (h d) -> p h d",
                                                                                          h=D_HEADS),
                                                AX.X, ALU.add).then_inc(s.out_step, 1)

                norm_scales_vector(nc, res, Chain(dve, s.vector_step), s.var, s.std, s.rstd)
                dve.wait_ge(s.weights, 16 * N_LOADS)
                delta_loop(dve, a_step, v_step, c_step, b_step, tail)
                dve.wait_ge(s.out_step, 2 * TILES)


def delta_loop(eng, a_step, v_step, c_step, b_step, tail):
    ahead = {"A": 3, "V": 2, "C": 1, "B": 1}
    steps = {"A": a_step, "V": v_step, "C": c_step, "B": b_step}

    def body(t, p, left=TILES):
        for what in DELTA_ORDER:
            if what[0] not in ahead:
                if tail is not None:
                    tail(t, p, what)
            elif steps[what[0]] is not None and left > ahead[what[0]]:
                steps[what[0]](t + ahead[what[0]], (p + ahead[what[0]]) % 2, int(what[1]))

    for kinds, u in (("A", 0), ("V", 0), ("A", 1), ("BC", 0), ("V", 1), ("A", 2)):
        for what in DELTA_ORDER:
            if what[0] in kinds and steps[what[0]] is not None:
                steps[what[0]](u, u % 2, int(what[1]))
    in_loop = (TILES - ahead["A"]) // 2
    body(0, 0)
    body(1, 1)
    with eng.Fori(1, in_loop) as i:
        body(2 * i, 0)
        body(2 * i + 1, 1)
    for t in range(2 * in_loop, TILES):
        body(t, t % 2, left=TILES - t)


def delta_output(nc, res, a):
    with ExitStack() as ctx:
        st = Stage(nc, ctx, "dout")
        wo, rms_w = st.sb("wo", [P, KC, DIM]), st.sb("rms_w", [P, 1])
        root, scale = st.sb("root", [P, TILES, D_HEADS]), st.sb("scale", [P, TILES, D_HEADS])
        normed = [st.sb(f"normed{i}", [P, PAIR, DIM]) for i in range(2)]
        normedT = [st.sb(f"normedT{i}", [P, PAIR, KC, P]) for i in range(2)]
        turn_ps, out_ps = ([st.ps(f"{n}{i}") for i in range(2)] for n in ("turn", "out"))
        s_w, s_mean, s_root, s_scale = (st.sem(n) for n in ("weights", "mean", "root", "scale"))
        s_normed, s_turn, s_normedT, s_out, s_x, s_stats = (st.sem(n) for n in ("normed", "turn", "normedT", "out",
                                                                                "x", "stats"))
        with nc.Block() as block:
            @block.sync
            def _(sp):
                sp.dma_start(wo[:], a["L0_attn_Wo"].rearrange("(k p) n -> p k n", p=P)).then_inc(s_w, 16)
                sp.dma_start(rms_w[:], a["L0_attn_rms_w"]).then_inc(s_w, 16)
                sp.wait_ge(s_w, 32)

            @block.tensor
            def _(pe):
                def head(u, p):
                    pe.wait_ge(s_normed, u + 1)
                    for j in range(PAIR):
                        for k in range(KC):
                            at = (j * KC + k) * P
                            mm = nc.tensor.transpose(turn_ps[p][:, at:at + P], normed[p][:, j, k * P:(k + 1) * P],
                                                     res.ident[:])
                    mm.then_inc(s_turn, 1)

                def tail(t, p):
                    pe.wait_ge(s_normedT, t + 1)
                    pe.wait_ge(s_x, t + 1)
                    for j in range(PAIR):
                        for k in range(KC):
                            mm = nc.tensor.matmul(out_ps[p][:, j * DIM:(j + 1) * DIM], normedT[p][:, j, k, :],
                                                  wo[:, k, :],
                                                  start=k == 0, stop=k == KC - 1)
                    mm.then_inc(s_out, 1)

                pe.wait_ge(s_scale, KC + 1)
                two_at_a_time(pe, head, tail, tail_first=True)

            @block.scalar
            def _(act):
                def head(u, p):
                    act.wait_ge(s_turn, u + 1)
                    nc.scalar.activation(normedT[p][:, :, :, :].rearrange("p j k q -> p (j k q)"), turn_ps[p][:, :],
                                         ACT.Copy).then_inc(s_normedT, 1)

                def tail(t, p):
                    pass

                act.wait_ge(s_mean, 1)
                nc.scalar.activation(root[:], scale[:], ACT.Sqrt).then_inc(s_root, 1)
                two_at_a_time(act, head, tail)

            @block.vector
            def _(dve):
                def head(u, p):
                    if not isinstance(u, int) or u > 1:
                        dve.wait_ge(s_out, u - 1)
                    nc.vector.tensor_tensor(
                        normed[p][:, :, :].rearrange("p j (h d) -> p (j h) d", h=D_HEADS),
                        pair_of(res.mixed, u).rearrange("p j (h d) -> p (j h) d", h=D_HEADS),
                        pair_of(scale, u).rearrange("p j h -> p (j h)").unsqueeze(2).to_broadcast([P, PAIR * D_HEADS,
                                                                                                   D_HEAD]),
                        ALU.mult).then_inc(s_normed, 1)

                def tail(t, p):
                    dve.wait_ge(s_out, t + 1)
                    nc.vector.tensor_tensor(pair_of(res.x, t), pair_of(res.x, t),
                                            out_ps[p][:, :].rearrange("p (j d) -> p j d",
                                                                      j=PAIR), ALU.add).then_inc(s_x, 1)
                    dve.wait_ge(s_x, 2 + t + 1)
                    for j in range(PAIR):
                        nc.vector.bn_stats(pair_rows(res.stats, t, j), pair_rows(res.x, t, j)).then_inc(s_stats, 1)

                dve.sem_inc(s_x, 2)
                nc.vector.tensor_scalar(scale[:], res.squares[:], 1.0 / D_HEAD, LN_EPS, ALU.mult,
                                        ALU.add).then_inc(s_mean, 1)
                dve.wait_ge(s_root, 1)
                nc.vector.reciprocal(scale[:], root[:]).then_inc(s_scale, 1)
                dve.wait_ge(s_w, 32)
                for k in range(KC):
                    nc.vector.tensor_scalar(wo[:, k, :], wo[:, k, :], rms_w[:, 0:1], None, ALU.mult).then_inc(s_scale,
                                                                                                              1)
                dve.wait_ge(s_scale, KC + 1)
                two_at_a_time(dve, head, tail)
                dve.wait_ge(s_stats, TILES)


EXPERTS, FFN_HEAD = 16, 128
TINY = 1e-12
BELOW_ALL = 1.0e30


def top_two(nc, dve_step, logits, first, second, work, rank, shape):
    peak, best, score = work
    wide = lambda m: m.unsqueeze(2).to_broadcast(shape)
    ranks = rank.unsqueeze(1).to_broadcast(shape)
    source = logits
    for chosen in (first, second):
        dve_step(nc.vector.tensor_reduce(peak, source, AX.X, ALU.max))
        dve_step(nc.vector.tensor_tensor(score, source, wide(peak), ALU.is_equal))
        dve_step(nc.vector.tensor_tensor(score, score, ranks, ALU.mult))
        dve_step(nc.vector.tensor_reduce(best, score, AX.X, ALU.max))
        dve_step(nc.vector.tensor_tensor(chosen, ranks, wide(best), ALU.is_equal))
        if chosen is first:
            dve_step(nc.vector.scalar_tensor_tensor(score, first, -BELOW_ALL, logits, ALU.mult, ALU.add))
            dve_step(nc.vector.tensor_copy(second, score))
            source = second


SWITCH_LOADS = 4


def load_switch(sp, res, a):
    for n, name in enumerate("qkv"):
        sp.dma_start(res.wqkv[:, :, :, n * FFN_HEAD:(n + 1) * FFN_HEAD],
                     a[f"L0_ffn_{name}_proj"].rearrange("e (k p) h -> p (e k) h", p=P)).then_inc(res.switch_loaded, 16)
    sp.dma_start(res.wo[:], a["L0_ffn_o_proj"].rearrange("e h c -> h e c")).then_inc(res.switch_loaded, 16)


def switch_router(nc, res, a):
    with ExitStack() as ctx:
        st = Stage(nc, ctx, "router")
        sim, sim_sq = st.sb("sim", [P, KC, EXPERTS]), st.sb("sim_sq", [P, KC, EXPERTS])
        sim_norm, gates, rank = (st.sb(n, [P, EXPERTS]) for n in ("sim_norm", "gates", "rank"))
        row_norm = st.sb("row_norm", [P, TILES])
        xn = [st.sb(f"xn{i}", [P, PAIR, DIM]) for i in range(2)]
        xnT = [st.sb(f"xnT{i}", [P, PAIR, KC, P]) for i in range(2)]
        logits, active, one, two, score, dots = (st.sb(n, [P, TILES, EXPERTS]) for n in
                                                 ("logits", "active", "one", "two", "score", "dots"))
        peak, best, inactive = (st.sb(n, [P, TILES]) for n in ("peak", "best", "inactive"))
        turn_ps = [st.ps(f"turn{i}") for i in range(2)]
        logit_ps = [st.ps(f"logit{i}") for i in range(2)]
        sim_ps = st.ps("simsum")
        s_w, s_var, s_std, s_rstd, s_chain = (st.sem(n) for n in ("weights", "var", "std", "rstd", "vector_step"))
        s_simsq, s_simps, s_normsq, s_norm, s_sim = (st.sem(n) for n in ("simsq", "simps", "normsq", "norm", "sim"))
        s_xn, s_turn, s_xnT, s_logit, s_dots = (st.sem(n) for n in ("xn", "turn", "xnT", "logit", "dots"))
        s_step, s_shift, s_exp = (st.sem(n) for n in ("route_step", "shifted", "exp"))
        with nc.Block() as block:
            @block.sync
            def _(sp):
                sp.dma_start(sim[:], a["L0_ffn_sim_matrix"].rearrange("(k p) e -> p k e", p=P)).then_inc(s_w, 16)
                sp.dma_start(gates[:], a["L0_ffn_gates"].to_broadcast([P, EXPERTS])).then_inc(s_w, 16)
                sp.dma_start(rank[:], a["rank16"].to_broadcast([P, EXPERTS])).then_inc(s_w, 16)
                sp.wait_ge(s_w, 48)

            @block.tensor
            def _(pe):
                def head(u, p):
                    pe.wait_ge(s_xn, u + 1)
                    for j in range(PAIR):
                        for k in range(KC):
                            at = (j * KC + k) * P
                            mm = nc.tensor.transpose(turn_ps[p][:, at:at + P], xn[p][:, j, k * P:(k + 1) * P],
                                                     res.ident[:])
                    mm.then_inc(s_turn, 1)

                def tail(t, p):
                    pe.wait_ge(s_xnT, t + 1)
                    pe.wait_ge(s_dots, t + 1)
                    for j in range(PAIR):
                        for k in range(KC):
                            mm = nc.tensor.matmul(logit_ps[p][:, j * EXPERTS:(j + 1) * EXPERTS], xnT[p][:, j, k, :],
                                                  sim[:, k, :],
                                                  start=k == 0, stop=k == KC - 1)
                    mm.then_inc(s_logit, 1)

                pe.wait_ge(s_simsq, 1)
                for k in range(KC):
                    mm = nc.tensor.matmul(sim_ps[:, 0:EXPERTS], res.ones[:], sim_sq[:, k, :], start=k == 0,
                                          stop=k == KC - 1)
                mm.then_inc(s_simps, 1)
                pe.wait_ge(s_sim, 2)
                two_at_a_time(pe, head, tail, tail_first=True)

            @block.scalar
            def _(act):
                def head(u, p):
                    act.wait_ge(s_turn, u + 1)
                    nc.scalar.activation(xnT[p][:, :, :, :].rearrange("p j k q -> p (j k q)"), turn_ps[p][:, :],
                                         ACT.Copy).then_inc(s_xnT, 1)

                def tail(t, p):
                    act.wait_ge(s_logit, t + 1)
                    nc.scalar.activation(pair_of(dots, t),
                                         logit_ps[p][:, 0:PAIR * EXPERTS].rearrange("p (j e) -> p j e", j=PAIR),
                                         ACT.Copy).then_inc(s_dots, 1)

                norm_scales_scalar(nc, res, act, s_var, s_std)
                act.wait_ge(s_normsq, 2)
                nc.scalar.activation(sim_norm[:], sim_norm[:], ACT.Sqrt).then_inc(s_norm, 1)
                nc.scalar.activation(row_norm[:], row_norm[:], ACT.Sqrt).then_inc(s_norm, 1)
                two_at_a_time(act, head, tail, tail_first=True)
                act.wait_ge(s_w, 48)
                nc.scalar.activation(gates[:], gates[:], ACT.Tanh, scale=0.5).then_inc(s_norm, 1)
                act.wait_ge(s_shift, 1)
                nc.scalar.activation(score[:], score[:], ACT.Exp).then_inc(s_exp, 1)

            @block.vector
            def _(dve):
                def head(u, p):
                    if not isinstance(u, int) or u > 1:
                        dve.wait_ge(s_turn, u - 1)
                    for j in range(PAIR):
                        ins = nc.vector.tensor_scalar(xn[p][:, j, :], pair_rows(res.x, u, j),
                                                      pair_rows(res.mean_var, u, j)[:, 0:1], pair_rows(res.rstd, u, j),
                                                      ALU.subtract, ALU.mult)
                    ins.then_inc(s_xn, 1)

                def tail(t, p):
                    pass

                norm_scales_vector(nc, res, Chain(dve, s_chain), s_var, s_std, s_rstd)
                dve.sem_inc(s_dots, 2)
                dve.wait_ge(s_w, 48)
                nc.vector.tensor_tensor(sim_sq[:], sim[:], sim[:], ALU.mult).then_inc(s_simsq, 1)
                dve.wait_ge(s_simps, 1)
                nc.vector.tensor_scalar(sim_norm[:], sim_ps[:, 0:EXPERTS], TINY, None, ALU.add).then_inc(s_normsq, 1)
                step = Chain(dve, s_step)

                def dve_step(ins):
                    step.step(ins)
                    step.settle()

                dve_step(nc.vector.tensor_tensor(row_norm[:], res.rstd[:, :, 0], res.rstd[:, :, 0], ALU.mult))
                dve_step(nc.vector.tensor_tensor(row_norm[:], row_norm[:], res.mean_var[:, :, 1], ALU.mult))
                nc.vector.tensor_scalar(row_norm[:], row_norm[:], float(DIM), TINY, ALU.mult,
                                        ALU.add).then_inc(s_normsq, 1)
                dve.wait_ge(s_norm, 2)
                dve_step(nc.vector.reciprocal(sim_norm[:], sim_norm[:]))
                dve_step(nc.vector.reciprocal(row_norm[:], row_norm[:]))
                for k in range(KC):
                    nc.vector.tensor_tensor(sim[:, k, :], sim[:, k, :], sim_norm[:], ALU.mult).then_inc(s_sim, 1)
                two_at_a_time(dve, head, tail)
                dve.wait_ge(s_dots, 2 + PAIRS_OF_TILES)
                shape = [P, TILES, EXPERTS]
                wide = lambda m: m[:, :].unsqueeze(2).to_broadcast(shape)
                dve_step(nc.vector.tensor_tensor(dots[:], dots[:], wide(row_norm), ALU.mult))
                dve.wait_ge(s_norm, 3)
                dve_step(nc.vector.tensor_scalar(gates[:], gates[:], 0.5, 0.5, ALU.mult, ALU.add))
                dve_step(nc.vector.tensor_tensor(logits[:], dots[:], gates[:].unsqueeze(1).to_broadcast(shape),
                                                 ALU.subtract))
                top_two(nc, dve_step, logits[:], one[:], two[:], (peak[:], best[:], score[:]), rank[:], shape)
                dve_step(nc.vector.tensor_scalar(active[:], logits[:], 0.0, None, ALU.is_gt))
                dve_step(nc.vector.tensor_reduce(peak[:], active[:], AX.X, ALU.max))
                dve_step(nc.vector.tensor_scalar(inactive[:], peak[:], -1.0, 1.0, ALU.mult, ALU.add))
                dve_step(nc.vector.tensor_tensor(one[:], one[:], two[:], ALU.add))
                dve_step(nc.vector.tensor_tensor(one[:], one[:], wide(inactive), ALU.mult))
                dve_step(nc.vector.tensor_tensor(active[:], active[:], one[:], ALU.add))
                dve_step(nc.vector.tensor_scalar(score[:], logits[:], 0.0, None, ALU.max))
                dve_step(nc.vector.tensor_reduce(peak[:], score[:], AX.X, ALU.max))
                nc.vector.tensor_tensor(score[:], score[:], wide(peak), ALU.subtract).then_inc(s_shift, 1)
                dve.wait_ge(s_exp, 1)
                dve_step(nc.vector.tensor_tensor(score[:], score[:], active[:], ALU.mult))
                dve_step(nc.vector.tensor_reduce(best[:], score[:], AX.X, ALU.add))
                dve_step(nc.vector.reciprocal(best[:], best[:]))
                dve_step(nc.vector.tensor_tensor(res.route[:], score[:], wide(best), ALU.mult))


SWITCH_ORDER = ["M0", "n", "M1", "a", "M2", "M3", "b", "M4", "M5", "p", "M6", "M7", "c", "M8", "d", "M9", "o0", "M10",
                "o1", "M11", "o2", "M12", "o3", "X", "M13", "o4", "M14", "o5", "M15", "o6", "o7"]
M_BANKS, O_BANKS = 4, 2
O_PER = 2


def switch_attention(nc, res, a, prefetch):
    with ExitStack() as ctx:
        st = Stage(nc, ctx, "switch")
        wqkv, wo = res.wqkv, res.wo
        causal = st.sb("causal", [P, P])
        xn, xnT = st.sb("xn", [P, DIM]), [st.sb(f"xnT{i}", [P, KC, P]) for i in range(2)]
        qkv = [st.sb(f"qkv{i}", [P, 3 * FFN_HEAD]) for i in range(2)]
        qkT, masked = st.sb("qkT", [P, 2 * P]), st.sb("masked", [P, P])
        probs, probsT, headT = (st.sb(n, [P, P]) for n in ("probs", "probsT", "headT"))
        negpeak, total, inverse = (st.sb(n, [P, 1]) for n in ("negpeak", "total", "inverse"))
        a_ps, b_ps, ROWS_AT = st.ps("a"), st.ps("b"), 2 * P
        m_ps, o_ps = [st.ps(f"m{i}") for i in range(M_BANKS)], [st.ps(f"o{i}") for i in range(O_BANKS)]
        s_mask, s_var, s_std, s_rstd, s_chain = (st.sem(n) for n in ("mask", "var", "std", "rstd", "vector_step"))
        s_xn, s_turn, s_xnT, s_m, s_added = (st.sem(n) for n in ("xn", "turn", "xnT", "projected", "added"))
        s_qk, s_qkT, s_score, s_tail, s_peak, s_exp = (st.sem(n) for n in ("qk_turned", "qkT", "score", "tail_step",
                                                                           "peak", "exp"))
        s_probs, s_pt, s_probsT, s_head, s_headT = (st.sem(n) for n in ("probs", "p_turned", "probsT", "head", "headT"))
        s_o, s_x, s_stats, s_inverse = (st.sem(n) for n in ("out", "x", "stats", "inverse"))
        PAIRS_OUT = EXPERTS // O_PER

        def loop(eng, turned, project, tail, normalised=None):
            def turn(t, p, left=TILES):
                for what in SWITCH_ORDER:
                    if what[0] == "M":
                        if left > 1:
                            project(t + 1, 1 - p, int(what[1:]))
                    elif what == "X":
                        if left > 2 and turned is not None:
                            turned(t + 2, p)
                    elif what == "n":
                        if left > 2 and normalised is not None:
                            normalised(t + 2)
                    else:
                        tail(t, p, what[0], int(what[1:] or 0))

            for u in range(2):
                if normalised is not None:
                    normalised(u)
                if turned is not None:
                    turned(u, u)
                if u == 0:
                    for e in range(EXPERTS):
                        project(0, 0, e)
            with eng.Fori(0, TILES // 2 - 1) as i:
                turn(2 * i, 0)
                turn(2 * i + 1, 1)
            turn(TILES - 2, 0, left=2)
            turn(TILES - 1, 1, left=1)

        with nc.Block() as block:
            @block.sync
            def _(sp):
                sp.dma_start(causal[:], a["causal"]).then_inc(s_mask, 16)
                prefetch(sp)
                sp.wait_ge(s_mask, 16)

            @block.tensor
            def _(pe):
                def turned(u, p):
                    pe.wait_ge(s_xn, u + 1)
                    for k in range(KC):
                        mm = nc.tensor.transpose(b_ps[:, ROWS_AT + k * P:ROWS_AT + (k + 1) * P],
                                                 xn[:, k * P:(k + 1) * P], res.ident[:])
                    mm.then_inc(s_turn, 1)

                def project(u, p, e):
                    if e == 0:
                        pe.wait_ge(s_xnT, u + 1)
                    pe.wait_ge(s_added, EXPERTS * u + e + 1)
                    for k in range(KC):
                        mm = nc.tensor.matmul(m_ps[e % M_BANKS][:, 0:3 * FFN_HEAD], xnT[p][:, k, :], wqkv[:, e, k, :],
                                              start=k == 0, stop=k == KC - 1)
                    mm.then_inc(s_m, 1)

                def tail(t, p, what, n):
                    if what == "a":
                        pe.wait_ge(s_added, M_BANKS + EXPERTS * (t + 1))
                        for part in range(2):
                            mm = nc.tensor.transpose(a_ps[:, part * P:(part + 1) * P], qkv[p][:, part * P:(part + 1) * P],
                                                     res.ident[:])
                        mm.then_inc(s_qk, 1)
                    elif what == "b":
                        pe.wait_ge(s_qkT, t + 1)
                        nc.tensor.matmul(a_ps[:, 2 * P:3 * P], qkT[:, 0:P], qkT[:, P:2 * P], start=True,
                                         stop=True).then_inc(s_score, 1)
                    elif what == "c":
                        pe.wait_ge(s_probs, t + 1)
                        nc.tensor.transpose(b_ps[:, 0:P], probs[:, :], res.ident[:]).then_inc(s_pt, 1)
                    elif what == "d":
                        pe.wait_ge(s_probsT, t + 1)
                        nc.tensor.matmul(b_ps[:, P:2 * P], qkv[p][:, 2 * P:3 * P], probsT[:, :], start=True,
                                         stop=True).then_inc(s_head, 1)
                    elif what == "o":
                        if n == 0:
                            pe.wait_ge(s_headT, t + 1)
                        pe.wait_ge(s_x, EXPERTS * t + O_PER * (n + 1))
                        nc.tensor.matmul(o_ps[n % O_BANKS][:, :], headT[:, :],
                                         wo[:, O_PER * n:O_PER * (n + 1), :].rearrange("p e c -> p (e c)"),
                                         start=True, stop=True).then_inc(s_o, 1)

                pe.wait_ge(res.switch_loaded, 16 * SWITCH_LOADS)
                loop(pe, turned, project, tail)

            @block.scalar
            def _(act):
                def turned(u, p):
                    act.wait_ge(s_turn, u + 1)
                    if not isinstance(u, int) or u > 1:
                        act.wait_ge(s_m, EXPERTS * (u - 1))
                    nc.scalar.activation(xnT[p][:, :, :].rearrange("p k q -> p (k q)"),
                                         b_ps[:, ROWS_AT:ROWS_AT + DIM], ACT.Copy).then_inc(s_xnT, 1)

                def project(u, p, e):
                    pass

                def tail(t, p, what, n):
                    if what == "a":
                        act.wait_ge(s_qk, t + 1)
                        nc.scalar.activation(qkT[:, :], a_ps[:, 0:2 * P], ACT.Copy).then_inc(s_qkT, 1)
                    elif what == "b":
                        act.wait_ge(s_peak, t + 1)
                        nc.scalar.activation(probs[:, :], masked[:, :], ACT.Exp, bias=negpeak[:, 0:1],
                                             scale=FFN_HEAD ** -0.5,
                                             accum_out=total[:, 0:1]).then_inc(s_exp, 1)
                    elif what == "c":
                        act.wait_ge(s_pt, t + 1)
                        nc.scalar.activation(probsT[:, :], b_ps[:, 0:P], ACT.Copy).then_inc(s_probsT, 1)
                    elif what == "d":
                        act.wait_ge(s_head, t + 1)
                        nc.scalar.activation(headT[:, :], b_ps[:, P:2 * P], ACT.Copy).then_inc(s_headT, 1)

                norm_scales_scalar(nc, res, act, s_var, s_std)
                loop(act, turned, project, tail)

            @block.vector
            def _(dve):
                def normalised(u):
                    dve.wait_ge(s_turn, u)
                    normalise(nc, res, xn[:, :], u).then_inc(s_xn, 1)

                def project(u, p, e):
                    dve.wait_ge(s_m, EXPERTS * u + e + 1)
                    product, weight = m_ps[e % M_BANKS][:, 0:3 * FFN_HEAD], row(res.route, u)[:, e:e + 1]
                    if e == 0:
                        ins = nc.vector.tensor_scalar(qkv[p][:, :], product, weight, None, ALU.mult)
                    else:
                        dve.wait_ge(s_added, M_BANKS + EXPERTS * u + e)
                        ins = nc.vector.scalar_tensor_tensor(qkv[p][:, :], product, weight, qkv[p][:, :], ALU.mult,
                                                             ALU.add)
                    ins.then_inc(s_added, 1)

                def tail(t, p, what, n):
                    if what == "b":
                        step = Chain(dve, s_tail, 2 * t)
                        dve.wait_ge(s_score, t + 1)
                        step.step(nc.vector.tensor_tensor(masked[:, :], a_ps[:, 2 * P:3 * P], causal[:, :], ALU.add))
                        step.settle()
                        step.step(nc.vector.tensor_reduce(negpeak[:, :], masked[:, :], AX.X, ALU.max, negate=True))
                        step.settle()
                        nc.vector.tensor_scalar(negpeak[:, :], negpeak[:, :], FFN_HEAD ** -0.5, None,
                                                ALU.mult).then_inc(s_peak, 1)
                    elif what == "p":
                        dve.wait_ge(s_exp, t + 1)
                        nc.vector.reciprocal(inverse[:, :], total[:, :]).then_inc(s_inverse, 1)
                        dve.wait_ge(s_inverse, t + 1)
                        nc.vector.tensor_scalar(probs[:, :], probs[:, :], inverse[:, 0:1], None,
                                                ALU.mult).then_inc(s_probs, 1)
                    elif what == "o":
                        dve.wait_ge(s_o, PAIRS_OUT * t + n + 1)
                        for i in range(O_PER):
                            e = O_PER * n + i
                            if i or n:
                                dve.wait_ge(s_x, O_PER * O_BANKS + EXPERTS * t + e)
                            nc.vector.scalar_tensor_tensor(row(res.x, t), o_ps[n % O_BANKS][:, i * DIM:(i + 1) * DIM],
                                                           row(res.route, t)[:, e:e + 1], row(res.x, t),
                                                           ALU.mult, ALU.add).then_inc(s_x, 1)
                        if n == PAIRS_OUT - 1:
                            dve.wait_ge(s_x, O_PER * O_BANKS + EXPERTS * (t + 1))
                            nc.vector.bn_stats(row(res.stats, t), row(res.x, t)).then_inc(s_stats, 1)

                norm_scales_vector(nc, res, Chain(dve, s_chain), s_var, s_std, s_rstd)
                dve.sem_inc(s_added, M_BANKS)
                dve.sem_inc(s_x, O_PER * O_BANKS)
                dve.wait_ge(s_mask, 16)
                loop(dve, None, project, tail, normalised)
                dve.wait_ge(s_stats, TILES)


def self_attention(nc, res, a, prefetch):
    with ExitStack() as ctx:
        st = Stage(nc, ctx, "self")
        block_mask = st.sb("block_mask", [P, P])
        xn = [st.sb(f"xn{i}", [P, PAIR, DIM]) for i in range(2)]
        rows = st.sb("rows", [P, TILES, DIM])
        xnT = [st.sb(f"xnT{i}", [P, PAIR, KC, P]) for i in range(2)]
        masked = [st.sb(f"masked{i}", [P, PAIR, P]) for i in range(2)]
        probs = [st.sb(f"probs{i}", [P, PAIR, P]) for i in range(2)]
        negpeak, total = ([st.sb(f"{n}{i}", [P, PAIR]) for i in range(2)] for n in ("negpeak", "total"))
        inverse = st.sb("inverse", [P, PAIR])
        turn_ps, score_ps, out_ps = ([st.ps(f"{n}{i}") for i in range(2)] for n in ("turn", "score", "out"))
        s_mask, s_var, s_std, s_rstd, s_chain = (st.sem(n) for n in ("mask", "var", "std", "rstd", "vector_step"))
        s_xn, s_turn, s_xnT, s_score, s_masked, s_inverse, s_rows = (
            st.sem(n) for n in ("xn", "turned", "xnT", "scores", "masked", "inverse", "rows"))
        s_peak, s_exp, s_probs, s_out, s_x, s_stats = (st.sem(n) for n in ("peak", "exp", "probs", "out", "x", "stats"))

        def loop(eng, order, steps):
            def turn(t, p, left=PAIRS_OF_TILES):
                for what in order:
                    ahead = {"T": 2, "S": 1}.get(what, 0)
                    if left > ahead:
                        steps[what](t + ahead, (p + ahead) % 2)

            for u, kinds in ((0, "TS"), (1, "T")):
                for what in kinds:
                    if what in steps:
                        steps[what](u, u)
            with eng.Fori(0, PAIRS_OF_TILES // 2 - 1) as i:
                turn(2 * i, 0)
                turn(2 * i + 1, 1)
            turn(PAIRS_OF_TILES - 2, 0, left=2)
            turn(PAIRS_OF_TILES - 1, 1, left=1)

        with nc.Block() as block:
            @block.sync
            def _(sp):
                sp.dma_start(block_mask[:], a["block_mask"]).then_inc(s_mask, 16)
                prefetch(sp)
                sp.wait_ge(s_mask, 16)

            @block.tensor
            def _(pe):
                def turned(u, p):
                    pe.wait_ge(s_xn, u + 1)
                    for j in range(PAIR):
                        for k in range(KC):
                            at = (j * KC + k) * P
                            mm = nc.tensor.transpose(turn_ps[p][:, at:at + P], xn[p][:, j, k * P:(k + 1) * P],
                                                     res.ident[:])
                    mm.then_inc(s_turn, 1)

                def scored(u, p):
                    pe.wait_ge(s_xnT, u + 1)
                    for j in range(PAIR):
                        for k in range(KC):
                            mm = nc.tensor.matmul(score_ps[p][:, j * P:(j + 1) * P], xnT[p][:, j, k, :],
                                                  xnT[p][:, j, k, :],
                                                  start=k == 0, stop=k == KC - 1)
                    mm.then_inc(s_score, 1)

                def added(t, p):
                    pe.wait_ge(s_probs, t + 1)
                    pe.wait_ge(s_rows, t + 1)
                    for j in range(PAIR):
                        mm = nc.tensor.matmul(out_ps[p][:, j * DIM:(j + 1) * DIM], probs[p][:, j, :],
                                              pair_rows(rows, t, j),
                                              start=True, stop=True)
                    mm.then_inc(s_out, 1)

                loop(pe, "SOT", {"T": turned, "S": scored, "O": added})

            @block.scalar
            def _(act):
                def turned(u, p):
                    act.wait_ge(s_turn, u + 1)
                    nc.scalar.activation(xnT[p][:, :, :, :].rearrange("p j k q -> p (j k q)"), turn_ps[p][:, :],
                                         ACT.Copy).then_inc(s_xnT, 1)
                    nc.scalar.activation(pair_of(rows, u), xn[p][:, :, :], ACT.Copy).then_inc(s_rows, 1)

                def scored(u, p):
                    act.wait_ge(s_peak, u + 1)
                    if not isinstance(u, int) or u > 1:
                        act.wait_ge(s_out, u - 1)
                    for j in range(PAIR):
                        ins = nc.scalar.activation(probs[p][:, j, :], masked[p][:, j, :], ACT.Exp,
                                                   bias=negpeak[p][:, j:j + 1], accum_out=total[p][:, j:j + 1])
                    ins.then_inc(s_exp, 1)

                norm_scales_scalar(nc, res, act, s_var, s_std)
                loop(act, "ST", {"T": turned, "S": scored})

            @block.vector
            def _(dve):
                def normalised(u, p):
                    if not isinstance(u, int) or u > 1:
                        dve.wait_ge(s_turn, u - 1)
                        dve.wait_ge(s_rows, u - 1)
                    for j in range(PAIR):
                        ins = nc.vector.tensor_scalar(xn[p][:, j, :], pair_rows(res.x, u, j),
                                                      pair_rows(res.mean_var, u, j)[:, 0:1], pair_rows(res.rstd, u, j),
                                                      ALU.subtract, ALU.mult)
                    ins.then_inc(s_xn, 1)

                def scored(u, p):
                    dve.wait_ge(s_score, u + 1)
                    nc.vector.tensor_tensor(
                        masked[p][:, :, :], score_ps[p][:, 0:PAIR * P].rearrange("p (j q) -> p j q", j=PAIR),
                        block_mask[:, :].unsqueeze(1).to_broadcast([P, PAIR, P]), ALU.add).then_inc(s_masked, 1)
                    dve.wait_ge(s_masked, u + 1)
                    nc.vector.tensor_reduce(negpeak[p][:, :], masked[p][:, :, :], AX.X, ALU.max,
                                            negate=True).then_inc(s_peak, 1)

                def divided(t, p):
                    dve.wait_ge(s_exp, t + 1)
                    nc.vector.reciprocal(inverse[:, :], total[p][:, :]).then_inc(s_inverse, 1)
                    dve.wait_ge(s_inverse, t + 1)
                    nc.vector.tensor_tensor(probs[p][:, :, :], probs[p][:, :, :],
                                            inverse[:, :].unsqueeze(2).to_broadcast([P, PAIR, P]),
                                            ALU.mult).then_inc(s_probs, 1)

                def added(t, p):
                    dve.wait_ge(s_out, t + 1)
                    nc.vector.tensor_tensor(pair_of(res.x, t), pair_of(res.x, t),
                                            out_ps[p][:, :].rearrange("p (j d) -> p j d",
                                                                      j=PAIR), ALU.add).then_inc(s_x, 1)
                    dve.wait_ge(s_x, t + 1)
                    for j in range(PAIR):
                        nc.vector.bn_stats(pair_rows(res.stats, t, j), pair_rows(res.x, t, j)).then_inc(s_stats, 1)

                norm_scales_vector(nc, res, Chain(dve, s_chain), s_var, s_std, s_rstd)
                dve.wait_ge(s_mask, 16)
                loop(dve, "NTSO", {"T": normalised, "S": scored, "N": divided, "O": added})
                dve.wait_ge(s_stats, TILES)


MOE, HIDDEN, CHOSEN = 8, 1024, 2
FC = HIDDEN // P
ROW_TILES = -(-((CHOSEN * TOKENS + MOE * (P - 1)) // P) // 2) * 2
ROWS = ROW_TILES * P


def scan(nc, dve_step, a, b, n, at):
    step = 1
    while step < n:
        dve_step(nc.vector.tensor_copy(at(b, slice(0, step)), at(a, slice(0, step))))
        dve_step(nc.vector.tensor_tensor(at(b, slice(step, n)), at(a, slice(step, n)), at(a, slice(0, n - step)),
                                         ALU.add))
        a, b, step = b, a, 2 * step
    return a


def moe_router(nc, res, a, rows):
    with ExitStack() as ctx:
        st = Stage(nc, ctx, "gate")
        gate, rank = st.sb("gate", [P, KC, MOE]), st.sb("rank", [P, MOE])
        before, tile_row = st.sb("before", [P, P]), st.sb("tile_row", [P, ROW_TILES])
        zeros = st.sb("zeros", [P, DIM])
        xn = [st.sb(f"xn{i}", [P, PAIR, DIM]) for i in range(2)]
        xnT = [st.sb(f"xnT{i}", [P, PAIR, KC, P]) for i in range(2)]
        xn_all = st.sb("xn_all", [P, TILES, DIM])
        probs, one, two, score, both, count, count2, place = (
            st.sb(n, [P, TILES, MOE]) for n in ("probs", "one", "two", "score", "both", "count", "count2", "place"))
        peak, best = st.sb("peak", [P, TILES]), st.sb("best", [P, TILES])
        padded, ends, ends2, starts = (st.sb(n, [P, MOE]) for n in ("padded", "ends", "ends2", "starts"))
        padded_int = st.sb("padded_int", [P, MOE], I32)
        started, owner = st.sb("started", [P, ROW_TILES, MOE - 1]), st.sb("owner", [P, ROW_TILES])
        slot = st.sb("slot", [P, TILES])
        turn_ps = [st.ps(f"turn{i}") for i in range(2)]
        logit_ps = [st.ps(f"logit{i}") for i in range(2)]
        before_ps, all_ps = st.ps("before"), st.ps("all")
        s_w, s_var, s_std, s_rstd, s_chain = (st.sem(n) for n in ("weights", "var", "std", "rstd", "vector_step"))
        s_xn, s_turn, s_xnT, s_logit, s_dots = (st.sem(n) for n in ("xn", "turn", "xnT", "logit", "dots"))
        s_step, s_shift, s_exp, s_both, s_counts = (st.sem(n) for n in ("route_step", "shifted", "exp", "both",
                                                                        "counts"))
        s_zero, s_zeroed, s_slots, s_scattered = (st.sem(n) for n in ("zero", "zeroed", "slots", "scattered"))
        with nc.Block() as block:
            @block.sync
            def _(sp):
                sp.dma_start(gate[:], a["L1_ffn_gate_w"].rearrange("(k p) e -> p k e", p=P)).then_inc(s_w, 16)
                sp.dma_start(rank[:], a["rank8"].to_broadcast([P, MOE])).then_inc(s_w, 16)
                sp.dma_start(before[:], a["before"]).then_inc(s_w, 16)
                sp.dma_start(tile_row[:], a["tile_row"].to_broadcast([P, ROW_TILES])).then_inc(s_w, 16)
                sp.wait_ge(s_zero, 1)
                sp.dma_start(rows.rearrange("(t p) d -> p t d", p=P),
                             zeros[:, :].unsqueeze(1).to_broadcast([P, ROW_TILES, DIM])).then_inc(s_zeroed, 16)
                sp.wait_ge(s_w, 64)
                sp.wait_ge(s_zeroed, 16)

            @block.tensor
            def _(pe):
                def head(u, p):
                    pe.wait_ge(s_xn, u + 1)
                    for j in range(PAIR):
                        for k in range(KC):
                            at = (j * KC + k) * P
                            mm = nc.tensor.transpose(turn_ps[p][:, at:at + P], xn[p][:, j, k * P:(k + 1) * P],
                                                     res.ident[:])
                    mm.then_inc(s_turn, 1)

                def tail(t, p):
                    pe.wait_ge(s_xnT, t + 1)
                    pe.wait_ge(s_dots, t + 1)
                    for j in range(PAIR):
                        for k in range(KC):
                            mm = nc.tensor.matmul(logit_ps[p][:, j * MOE:(j + 1) * MOE], xnT[p][:, j, k, :],
                                                  gate[:, k, :],
                                                  start=k == 0, stop=k == KC - 1)
                    mm.then_inc(s_logit, 1)

                pe.wait_ge(s_w, 64)
                two_at_a_time(pe, head, tail, tail_first=True)
                pe.wait_ge(s_both, 1)
                chosen = both[:, :, :].rearrange("p t e -> p (t e)")
                nc.tensor.matmul(before_ps[:, 0:P], before[:], chosen, start=True, stop=True)
                nc.tensor.matmul(all_ps[:, 0:P], res.ones[:], chosen, start=True, stop=True).then_inc(s_counts, 1)

            @block.scalar
            def _(act):
                def head(u, p):
                    act.wait_ge(s_turn, u + 1)
                    nc.scalar.activation(xnT[p][:, :, :, :].rearrange("p j k q -> p (j k q)"), turn_ps[p][:, :],
                                         ACT.Copy).then_inc(s_xnT, 1)

                def tail(t, p):
                    act.wait_ge(s_logit, t + 1)
                    nc.scalar.activation(pair_of(probs, t), logit_ps[p][:, 0:PAIR * MOE].rearrange("p (j e) -> p j e",
                                                                                                   j=PAIR),
                                         ACT.Copy).then_inc(s_dots, 1)

                norm_scales_scalar(nc, res, act, s_var, s_std)
                two_at_a_time(act, head, tail, tail_first=True)
                act.wait_ge(s_shift, 1)
                nc.scalar.activation(probs[:], probs[:], ACT.Exp).then_inc(s_exp, 1)

            @block.gpsimd
            def _(pool):
                pool.wait_ge(s_zeroed, 16)
                for n in range(CHOSEN):
                    pool.wait_ge(s_slots, n + 1)
                    for t in range(TILES):
                        pool.indirect_dma_start(rows, bass.IndirectOffsetOnAxis(res.slots[:, n, t:t + 1], 0),
                                                xn_all[:, t, :],
                                                None).then_inc(s_scattered, 16)
                pool.wait_ge(s_scattered, 16 * CHOSEN * TILES)

            @block.vector
            def _(dve):
                def head(u, p):
                    if not isinstance(u, int) or u > 1:
                        dve.wait_ge(s_turn, u - 1)
                    for j in range(PAIR):
                        ins = nc.vector.tensor_scalar(xn[p][:, j, :], pair_rows(res.x, u, j),
                                                      pair_rows(res.mean_var, u, j)[:, 0:1], pair_rows(res.rstd, u, j),
                                                      ALU.subtract, ALU.mult)
                    ins.then_inc(s_xn, 1)
                    dve.wait_ge(s_xn, u + 1)
                    nc.vector.tensor_copy(pair_of(xn_all, u), xn[p][:, :, :])

                def tail(t, p):
                    pass

                nc.vector.memset(zeros[:], 0.0).then_inc(s_zero, 1)
                norm_scales_vector(nc, res, Chain(dve, s_chain), s_var, s_std, s_rstd)
                dve.sem_inc(s_dots, 2)
                dve.wait_ge(s_w, 64)
                two_at_a_time(dve, head, tail)
                dve.wait_ge(s_dots, 2 + PAIRS_OF_TILES)
                step = Chain(dve, s_step)

                def dve_step(ins):
                    step.step(ins)
                    step.settle()

                shape = [P, TILES, MOE]
                wide = lambda m: m[:, :].unsqueeze(2).to_broadcast(shape)
                dve_step(nc.vector.tensor_reduce(peak[:], probs[:], AX.X, ALU.max))
                nc.vector.tensor_tensor(probs[:], probs[:], wide(peak), ALU.subtract).then_inc(s_shift, 1)
                dve.wait_ge(s_exp, 1)
                dve_step(nc.vector.tensor_reduce(best[:], probs[:], AX.X, ALU.add))
                dve_step(nc.vector.reciprocal(best[:], best[:]))
                dve_step(nc.vector.tensor_tensor(probs[:], probs[:], wide(best), ALU.mult))
                top_two(nc, dve_step, probs[:], one[:], two[:], (peak[:], best[:], score[:]), rank[:], shape)
                nc.vector.tensor_tensor(both[:], one[:], two[:], ALU.add).then_inc(s_both, 1)
                dve.wait_ge(s_counts, 1)
                dve_step(nc.vector.tensor_copy(count[:].rearrange("p t e -> p (t e)"), all_ps[:, 0:P]))
                upto = scan(nc, dve_step, count, count2, TILES, lambda m, s: m[:, s, :])
                dve_step(nc.vector.tensor_scalar(padded_int[:], upto[:, TILES - 1, :], float(P - 1), None, ALU.add))
                shift = P.bit_length() - 1
                dve_step(nc.vector.tensor_scalar(padded_int[:], padded_int[:], shift, shift,
                                                 ALU.logical_shift_right, ALU.logical_shift_left))
                dve_step(nc.vector.tensor_copy(padded[:], padded_int[:]))
                dve_step(nc.vector.tensor_copy(ends[:], padded[:]))
                end = scan(nc, dve_step, ends, ends2, MOE, lambda m, s: m[:, s])
                dve_step(nc.vector.tensor_tensor(starts[:], end[:], padded[:], ALU.subtract))
                dve_step(nc.vector.tensor_tensor(place[:], upto[:], starts[:].unsqueeze(1).to_broadcast(shape),
                                                 ALU.add))
                dve_step(nc.vector.tensor_tensor(place[:].rearrange("p t e -> p (t e)"),
                                                 place[:].rearrange("p t e -> p (t e)"),
                                                 all_ps[:, 0:P], ALU.subtract))
                dve_step(nc.vector.tensor_tensor(place[:].rearrange("p t e -> p (t e)"),
                                                 place[:].rearrange("p t e -> p (t e)"),
                                                 before_ps[:, 0:P], ALU.add))
                for n, chosen in enumerate((one, two)):
                    dve_step(nc.vector.tensor_tensor(score[:], place[:], chosen[:], ALU.mult))
                    dve_step(nc.vector.tensor_reduce(slot[:], score[:], AX.X, ALU.add))
                    nc.vector.tensor_copy(res.slots[:, n, :], slot[:]).then_inc(s_slots, 1)
                    dve.wait_ge(s_slots, n + 1)
                for n, chosen in enumerate((one, two)):
                    dve_step(nc.vector.tensor_tensor(score[:], probs[:], chosen[:], ALU.mult))
                    dve_step(nc.vector.tensor_reduce(res.weight[:, n, :], score[:], AX.X, ALU.add))
                dve_step(nc.vector.tensor_tensor(peak[:], res.weight[:, 0, :], res.weight[:, 1, :], ALU.add))
                dve_step(nc.vector.reciprocal(peak[:], peak[:]))
                for n in range(CHOSEN):
                    dve_step(nc.vector.tensor_tensor(res.weight[:, n, :], res.weight[:, n, :], peak[:], ALU.mult))
                dve_step(nc.vector.tensor_tensor(started[:], starts[:, 1:].unsqueeze(1).to_broadcast([P, ROW_TILES,
                                                                                                      MOE - 1]),
                                                 tile_row[:].unsqueeze(2).to_broadcast([P, ROW_TILES,
                                                                                        MOE - 1]), ALU.is_le))
                dve_step(nc.vector.tensor_reduce(owner[:], started[:], AX.X, ALU.add))
                dve_step(nc.vector.tensor_copy(res.owner[:], owner[:]))


MOE_ORDER = ["X1", "G0", "H1", "Y0"]


def moe_experts(nc, res, rows, outs):
    with ExitStack() as ctx:
        st = Stage(nc, ctx, "moe")
        xs = [st.sb(f"xs{i}", [P, DIM]) for i in range(2)]
        y = [st.sb(f"y{i}", [P, DIM]) for i in range(2)]
        xsT, hidden, hiddenT = st.sb("xsT", [P, KC, P]), st.sb("hidden", [P, HIDDEN]), st.sb("hiddenT", [P, FC, P])
        x_ps, y_ps = st.ps("x"), st.ps("y")
        h_ps, g_ps = ([st.ps(f"{n}{i}") for i in range(2)] for n in ("h", "g"))
        s_turn, s_xsT, s_h, s_hidden = (st.sem(n) for n in ("turn", "xsT", "h", "hidden"))
        s_g, s_hiddenT, s_y, s_y_sb = (st.sem(n) for n in ("g", "hiddenT", "y", "y_sb"))
        s_xs, s_stored = ([st.sem(f"{n}{i}") for i in range(2)] for n in ("xs", "stored"))

        def loop(eng, step):
            def body(j, p, last=False):
                for what in MOE_ORDER:
                    ahead = int(what[1])
                    if not (ahead and last):
                        step(j + ahead, (p + ahead) % 2, what[0])

            for what in MOE_ORDER:
                if what[1] == "1":
                    step(0, 0, what[0])
            body(0, 0)
            body(1, 1)
            with eng.Fori(1, ROW_TILES // 2 - 1) as i:
                body(2 * i, 0)
                body(2 * i + 1, 1)
            body(ROW_TILES - 2, 0)
            body(ROW_TILES - 1, 1, last=True)

        with nc.Block() as block:
            @block.sync
            def _(sp):
                source = rows.rearrange("(t p) d -> t p d", p=P)
                target = outs.rearrange("(t p) d -> t p d", p=P)

                def one_tile(m, j):
                    return m[j] if isinstance(j, int) else m[bass.ds(j, 1)].rearrange("a p d -> (a p) d")

                def load(j, p):
                    sp.dma_start(xs[p][:, :], one_tile(source, j)).then_inc(s_xs[p], 16)

                def store(j, p):
                    sp.dma_start(one_tile(target, j), y[p][:, :]).then_inc(s_stored[p], 16)

                for j in range(2):
                    load(j, j)
                with sp.Fori(0, ROW_TILES // 2 - 1) as i:
                    for p in range(2):
                        j = 2 * i + p
                        ahead, now, done = sp.snap(j + 2), sp.snap(j), sp.snap(j + 1)
                        sp.wait_ge(s_turn, done)
                        load(ahead, p)
                        sp.wait_ge(s_y_sb, done)
                        store(now, p)
                for j in (ROW_TILES - 2, ROW_TILES - 1):
                    sp.wait_ge(s_y_sb, j + 1)
                    store(j, j % 2)
                for p in range(2):
                    sp.wait_ge(s_stored[p], 16 * (ROW_TILES // 2))

            @block.tensor
            def _(pe):
                def step(j, p, what):
                    if what == "X":
                        pe.wait_ge(s_xs[p], 16 * (j // 2 + 1) if isinstance(j, int) else 8 * (j - p) + 16)
                        for k in range(KC):
                            mm = nc.tensor.transpose(x_ps[:, k * P:(k + 1) * P], xs[p][:, k * P:(k + 1) * P],
                                                     res.ident[:])
                        mm.then_inc(s_turn, 1)
                    elif what == "H":
                        e = expert(j)
                        pe.wait_ge(s_xsT, j + 1)
                        for n in range(2):
                            pe.wait_ge(s_hidden, 2 * j + n)
                            for k in range(KC):
                                mm = nc.tensor.matmul(h_ps[n][:, :], xsT[:, k, :],
                                                      res.w1[:, bass.ds(e * KC + k, 1), n * 512:(n + 1) * 512].rearrange("p a f -> p (a f)"),
                                                      start=k == 0, stop=k == KC - 1)
                            mm.then_inc(s_h, 1)
                    elif what == "G":
                        for n in range(2):
                            pe.wait_ge(s_hidden, 2 * j + n + 1)
                            pe.wait_ge(s_hiddenT, 2 * j)
                            for f in range(4):
                                at = n * 4 + f
                                mm = nc.tensor.transpose(g_ps[n][:, f * P:(f + 1) * P],
                                                         hidden[:, at * P:(at + 1) * P], res.ident[:])
                            mm.then_inc(s_g, 1)
                    else:
                        e = expert(j)
                        pe.wait_ge(s_hiddenT, 2 * (j + 1))
                        pe.wait_ge(s_y_sb, j)
                        for f in range(FC):
                            mm = nc.tensor.matmul(y_ps[:, 0:DIM], hiddenT[:, f, :],
                                                  res.w2[:, bass.ds(e * FC + f, 1), :].rearrange("p a d -> p (a d)"),
                                                  start=f == 0, stop=f == FC - 1)
                        mm.then_inc(s_y, 1)

                def expert(j):
                    at = res.owner[0:1, j:j + 1] if isinstance(j, int) else res.owner[0:1, bass.ds(j, 1)]
                    return pe.value_load(at, min_val=0, max_val=MOE - 1)

                pe.wait_ge(res.moe_loaded, 32)
                loop(pe, step)

            @block.scalar
            def _(act):
                def step(j, p, what):
                    if what == "X":
                        act.wait_ge(s_turn, j + 1)
                        nc.scalar.activation(xsT[:, :, :].rearrange("p k q -> p (k q)"), x_ps[:, 0:DIM],
                                             ACT.Copy).then_inc(s_xsT, 1)
                    elif what == "H":
                        for n in range(2):
                            act.wait_ge(s_h, 2 * j + n + 1)
                            act.wait_ge(s_g, 2 * j)
                            nc.scalar.activation(hidden[:, n * 512:(n + 1) * 512], h_ps[n][:, :],
                                                 ACT.Gelu_apprx_tanh).then_inc(s_hidden, 1)

                loop(act, step)

            @block.vector
            def _(dve):
                def step(j, p, what):
                    if what == "G":
                        for n in range(2):
                            dve.wait_ge(s_g, 2 * j + n + 1)
                            dve.wait_ge(s_y, j)
                            nc.vector.tensor_copy(hiddenT[:, n * 4:(n + 1) * 4, :].rearrange("p f q -> p (f q)"),
                                                  g_ps[n][:, :]).then_inc(s_hiddenT, 1)
                    elif what == "Y":
                        dve.wait_ge(s_y, j + 1)
                        dve.wait_ge(s_stored[p], 16 * (j // 2) if isinstance(j, int) else 8 * (j - p))
                        nc.vector.tensor_copy(y[p][:, :], y_ps[:, 0:DIM]).then_inc(s_y_sb, 1)

                loop(dve, step)


def moe_combine(nc, res, outs, out):
    with ExitStack() as ctx:
        st = Stage(nc, ctx, "mix")
        DEEP = 4
        got = [[st.sb(f"got{i}{n}", [P, DIM]) for n in range(CHOSEN)] for i in range(DEEP)]
        s_got = [st.sem(f"got{i}") for i in range(DEEP)]
        s_first, s_mixed, s_out = st.sem("first"), st.sem("mixed"), st.sem("out")
        with nc.Block() as block:
            @block.gpsimd
            def _(pool):
                for t in range(TILES):
                    if t >= DEEP:
                        pool.wait_ge(s_mixed, t - DEEP + 1)
                    for n in range(CHOSEN):
                        pool.indirect_dma_start(got[t % DEEP][n][:, :], None, outs,
                                                bass.IndirectOffsetOnAxis(res.slots[:, n, t:t + 1],
                                                                          0)).then_inc(s_got[t % DEEP], 16)

            @block.vector
            def _(dve):
                for t in range(TILES):
                    dve.wait_ge(s_got[t % DEEP], 16 * CHOSEN * (t // DEEP + 1))
                    nc.vector.scalar_tensor_tensor(res.x[:, t, :], got[t % DEEP][0][:, :], res.weight[:, 0, t:t + 1],
                                                   res.x[:, t, :], ALU.mult, ALU.add).then_inc(s_first, 1)
                    dve.wait_ge(s_first, t + 1)
                    nc.vector.scalar_tensor_tensor(res.x[:, t, :], got[t % DEEP][1][:, :], res.weight[:, 1, t:t + 1],
                                                   res.x[:, t, :], ALU.mult, ALU.add).then_inc(s_mixed, 1)

            @block.sync
            def _(sp):
                target = out.rearrange("(t p) d -> p t d", p=P)
                for t in range(0, TILES, 4):
                    sp.wait_ge(s_mixed, t + 4)
                    sp.dma_start(target[:, t:t + 4, :], res.x[:, t:t + 4, :]).then_inc(s_out, 16)
                sp.wait_ge(s_out, 16 * (TILES // 4))


def load_experts(sp, res, a, which):
    if which == 0:
        sp.dma_start(res.w1[:], a["L1_ffn_w1"].rearrange("e (k p) f -> p (e k) f", p=P)).then_inc(res.moe_loaded, 16)
    else:
        sp.dma_start(res.w2[:], a["L1_ffn_w2"].rearrange("e (k p) d -> p (e k) d", p=P)).then_inc(res.moe_loaded, 16)


def store_residual(nc, res, out):
    with ExitStack() as ctx:
        st = Stage(nc, ctx, "store")
        s_out = st.sem("out")
        with nc.Block() as block:
            @block.sync
            def _(sp):
                sp.dma_start(out.rearrange("(t p) d -> p t d", p=P), res.x[:]).then_inc(s_out, 16)
                sp.wait_ge(s_out, 16)


def load_alone(nc, load):
    with nc.Block() as block:
        @block.sync
        def _(sp):
            load(sp)


def perceiver(nc, a, out, stages=("x0", "d", "s", "x1", "e", "f")):
    with ExitStack() as ctx:
        st = Stage(nc, ctx, "res")
        res = Resident()
        res.x = st.sb("x", [P, TILES, DIM])
        res.stats = st.sb("stats", [P, TILES, 6])
        res.mean_var = st.sb("mean_var", [P, TILES, 2])
        res.std, res.rstd = st.sb("std", [P, TILES]), st.sb("rstd", [P, TILES, 1])
        res.ident, res.ones = st.sb("ident", [P, P]), st.sb("ones", [P, P])
        def nothing(sp):
            pass

        cross = [CrossWeights(Stage(nc, ctx, f"x{layer}_weights"), a, layer) for layer in range(2)]
        load_residual(nc, res, a["x"], a, cross[0].load)
        if "x0" in stages or "d" in stages or "s" in stages:
            with ExitStack() as layer:
                delta = DeltaWeights(Stage(nc, layer, "delta_weights"), a)
                if "x0" in stages:
                    cross_attention(nc, res, "x0", a["ctx_T"], cross[0], a["mask"],
                                    delta.load if "d" in stages else nothing)
                held = Stage(nc, layer, "switch_held")
                res.wqkv, res.wo = held.sb("wqkv", [P, EXPERTS, KC, 3 * FFN_HEAD]), held.sb("wo", [P, EXPERTS, DIM])
                res.switch_loaded = held.sem("switch_loaded")
                if "d" in stages:
                    with ExitStack() as inner:
                        between = Stage(nc, inner, "held")
                        res.mixed, res.squares = between.sb("mixed", [P, TILES, DIM]), between.sb("squares",
                                                                                                  [P, TILES, D_HEADS])
                        if "x0" not in stages:
                            load_alone(nc, delta.load)
                        delta_rule(nc, res, delta, lambda sp: load_switch(sp, res, a) if "s" in stages else None)
                        delta_output(nc, res, a)
                if "s" in stages:
                    with ExitStack() as inner:
                        res.route = Stage(nc, inner, "held").sb("route", [P, TILES, EXPERTS])
                        switch_router(nc, res, a)
                        switch_attention(nc, res, a, cross[1].load if "x1" in stages else nothing)
        moe = Stage(nc, ctx, "moe_held")
        res.moe_loaded = moe.sem("moe_loaded")
        res.w1 = moe.sb("w1", [P, MOE * KC, HIDDEN])
        if "x1" in stages:
            if "s" not in stages:
                load_alone(nc, cross[1].load)
            cross_attention(nc, res, "x1", a["ctx_T"], cross[1], None, lambda sp: load_experts(sp, res, a, 0))
        if "e" in stages:
            res.w2 = moe.sb("w2", [P, MOE * FC, DIM])
            self_attention(nc, res, a, lambda sp: load_experts(sp, res, a, 1))
        if "f" in stages:
            res.slots, res.weight = moe.sb("slots", [P, CHOSEN, TILES], U32), moe.sb("weight", [P, CHOSEN, TILES])
            res.owner = moe.sb("owner", [P, ROW_TILES], I32)
            rows = nc.dram_tensor("rows", (ROWS, DIM), F32, kind="Internal").ap()
            outs = nc.dram_tensor("outs", (ROWS, DIM), F32, kind="Internal").ap()
            moe_router(nc, res, a, rows)
            moe_experts(nc, res, rows, outs)
            moe_combine(nc, res, outs, out)
        else:
            store_residual(nc, res, out)


def constants():
    import numpy as np
    c = np.arange(P)
    head = (c[:, None] // HEAD == np.arange(HALF_HEADS)[None, :]) * HEAD ** -0.5
    par = (c[:, None] // HEAD) % 2 == np.arange(2)[None, :]
    batch = c // SEQ
    block_mask = np.where(batch[:, None] == batch[None, :], 0.0, LOWEST)
    row_, col = c[:, None], c[None, :]
    same = batch[:, None] == batch[None, :]

    def join(size):
        return (row_ // (2 * size) == col // (2 * size)) & (row_ // size % 2 == 1) & (col // size % 2 == 0)

    causal = np.where(same & (row_ >= col), 0.0, LOWEST)
    tables = {"ident": np.eye(P), "headmask": head, "parmask": par, "block_mask": block_mask,
              "strict": same & (row_ > col), "before": row_ < col, "rank8": np.arange(MOE, 0, -1)[None, :],
              "tile_row": P * np.arange(ROW_TILES)[None, :],
              "causal": causal, "rank16": np.arange(EXPERTS, 0, -1)[None, :],
              "head_ones": c[:, None] // D_HEAD == np.arange(2)[None, :],
              "causalT": same & (row_ <= col), "join1": join(1), "join1T": join(1).T,
              "joinT": np.stack([join(n).T for n in LEVELS], axis=1)}
    return {k: v.astype(np.float32) for k, v in tables.items()}


def laid_out(inputs):
    import numpy as np
    a = {k: np.ascontiguousarray(v) for k, v in inputs.items()}
    out = {"x": a["x"].reshape(TOKENS, DIM), "ctx_T": a["ctx_1024"].reshape(BATCH * KEYS, DIM).T,
           "mask": a["mask_1x1xSxS2_ik0"].reshape(SEQ, KEYS)}
    for layer in range(2):
        pre = f"L{layer}_xattn_"
        for n in ("Wq", "Wk", "Wv", "Wo"):
            out[pre + n] = a[pre + n].T if layer == 0 else a[pre + n]
        for n in ("bq", "bk", "bv"):
            out[pre + n] = a[pre + n].reshape(KC, P).T
        out[pre + "bo"] = a[pre + "bo"].reshape(1, DIM)
    for n in ("Wq", "Wk", "Wv", "Wb", "Wo"):
        out["L0_attn_" + n] = a["L0_attn_" + n]
    for n in ("q_proj", "k_proj", "v_proj", "o_proj", "sim_matrix"):
        out["L0_ffn_" + n] = a["L0_ffn_" + n]
    for n in ("gate_w", "w1", "w2"):
        out["L1_ffn_" + n] = a["L1_ffn_" + n]
    out["L0_ffn_gates"] = a["L0_ffn_gates"].reshape(1, EXPERTS)
    taps = [a[f"L0_attn_conv_{n}_w"].reshape(KC, P, TAPS) for n in "qkv"]
    out["L0_attn_taps"] = np.concatenate(taps).transpose(1, 0, 2)
    out["L0_attn_rms_w"] = np.tile(a["L0_attn_rms_w"], P // D_HEAD).reshape(P, 1)
    out.update(constants())
    return {k: np.ascontiguousarray(v) for k, v in out.items()}


def kernel(**inputs):
    import concourse.bacc as bacc
    from concourse.bass_utils import run_bass_kernel_spmd

    nc = bacc.Bacc("TRN2", target_bir_lowering=False, num_devices=1)
    arrays = {f"in_{k}": v for k, v in laid_out(inputs).items()}
    aps = {k[3:]: nc.dram_tensor(k, v.shape, mybir.dt.from_np(v.dtype), kind="ExternalInput").ap()
           for k, v in arrays.items()}
    out = nc.dram_tensor("out", (TOKENS, DIM), F32, kind="ExternalOutput").ap()
    perceiver(nc, aps, out)
    r = run_bass_kernel_spmd(nc, [arrays], core_ids=[0])
    return r.results[0]["out"].reshape(BATCH, SEQ, DIM)
```
